# Optimizing a Trainium2 kernel written in Bass

```python
import numpy as np
import jax
import jax.numpy as jnp

def _softmax(x, axis=-1):
    return jax.nn.softmax(x, axis=axis)

def _gelu(x):
    return jax.nn.gelu(x, approximate=True)

def _silu(x):
    return jax.nn.silu(x)

def _sigmoid(x):
    return jax.nn.sigmoid(x)

def _layernorm(x, axis=-1, eps=1e-05):
    m = jnp.mean(x, axis=axis, keepdims=True)
    v = jnp.var(x, axis=axis, keepdims=True)
    return (x - m) / jnp.sqrt(v + eps)

def _scatter_add(tgt, idx, src, axis=0):
    return tgt.at[idx].add(src)

def _segment_sum(src, seg, n):
    return jax.ops.segment_sum(src, seg, n)
kernel_name = 'mk_early_fusion_embed_d1_tok_img1024_r4_407cf3'

def setup_inputs(seed: int=0):
    np.random.seed(seed)
    _w = jnp.asarray

    def _rec_inputs():
        import jax
        import jax.numpy as jnp
        _rk = jax.random.key(seed)
        x = 7.22013e-05 + 1.00017 * jax.random.normal(jax.random.fold_in(_rk, 1), (8, 1, 256, 256), jnp.float32)
        x_txt = jax.random.randint(jax.random.fold_in(_rk, 51), (8, 128), 0, 31921, jnp.int32)
        return (x, x_txt)
    x, x_txt = _rec_inputs()

    def _L0_tok_setup():
        import jax, jax.numpy as jnp
        import numpy as np
        EPS = 0.5
        TAU = 0.5
        MAXITER = 10
        NABLA_W = np.array([[[[0.0, 0.0, 0.0], [0.0, -1.0, 0.0], [0.0, 1.0, 0.0]]], [[[0.0, 0.0, 0.0], [0.0, -1.0, 1.0], [0.0, 0.0, 0.0]]]], dtype=np.float32)
        DIV_W = np.array([[[[0.0, -1.0, 0.0], [0.0, 1.0, 0.0], [0.0, 0.0, 0.0]], [[0.0, 0.0, 0.0], [-1.0, 1.0, 0.0], [0.0, 0.0, 0.0]]]], dtype=np.float32)

        def _conv(x, w):
            return jax.lax.conv_general_dilated(x, w, window_strides=(1, 1), padding='SAME', dimension_numbers=('NCHW', 'OIHW', 'NCHW'))
        key = jax.random.key(seed)
        k1, k2 = jax.random.split(key)
        B, H, W = (8, 256, 256)
        o = jax.random.normal(k1, (B, 1, H, W), dtype=jnp.float32)
        vector_field = jax.random.normal(k2, (H, W, 2), dtype=jnp.float32)
        nabla_w = jnp.asarray(NABLA_W)
        div_w = jnp.asarray(DIV_W)
        return {'o': o, 'vector_field': vector_field, 'nabla_w': nabla_w, 'div_w': div_w}
    _L0_tok_all = _L0_tok_setup()
    _L0_tok_in = {k: v for k, v in _L0_tok_all.items() if k in ('vector_field', 'nabla_w', 'div_w')}
    del _L0_tok_all

    def _L0_txt_setup():
        import jax, jax.numpy as jnp
        import numpy as np
        VOCAB, D, H, M, L, NMAX = (8000, 256, 16, 1024, 4, 256)
        KD = D // H
        EPS = 1e-05

        def positional_encoding(n, d):
            pos = jnp.arange(n, dtype=jnp.float32)[:, None]
            div = jnp.exp(jnp.arange(0, d, 2, dtype=jnp.float32) * (-jnp.log(10000.0) / d))
            ang = pos * div
            enc = jnp.zeros((n, d), dtype=jnp.float32)
            enc = enc.at[:, 0::2].set(jnp.sin(ang))
            enc = enc.at[:, 1::2].set(jnp.cos(ang))
            return enc

        def _layernorm(z, g, b):
            mu = jnp.mean(z, axis=-1, keepdims=True)
            var = jnp.mean((z - mu) ** 2, axis=-1, keepdims=True)
            return (z - mu) * jax.lax.rsqrt(var + EPS) * g + b

        def _block(h, p):
            wq, wk, wv, wc, w1, bb1, w2, bb2, gg1, e1, gg2, e2 = p
            B, n, d = h.shape

            def heads(w):
                return (h @ w).reshape(B, n, H, KD).transpose(0, 2, 1, 3)
            Q, K, V = (heads(wq), heads(wk), heads(wv))
            scores = jnp.einsum('bhqk,bhlk->bhql', Q, K) / np.sqrt(KD).astype(np.float32)
            attn = jax.nn.softmax(scores, axis=-1)
            out = jnp.einsum('bhql,bhlv->bhqv', attn, V)
            out = out.transpose(0, 2, 1, 3).reshape(B, n, d) @ wc
            h = _layernorm(h + out, gg1, e1)
            ff = jax.nn.relu(h @ w1 + bb1) @ w2 + bb2
            return _layernorm(h + ff, gg2, e2)
        key = jax.random.key(seed)
        ks = jax.random.split(key, 12)
        s = 0.02
        return {'x': jax.random.randint(ks[0], (2, 256), 0, VOCAB), 'emb': jax.random.normal(ks[1], (VOCAB, D), jnp.float32) * s, 'Wq': jax.random.normal(ks[2], (L, D, D), jnp.float32) * s, 'Wk': jax.random.normal(ks[3], (L, D, D), jnp.float32) * s, 'Wv': jax.random.normal(ks[4], (L, D, D), jnp.float32) * s, 'Wc': jax.random.normal(ks[5], (L, D, D), jnp.float32) * s, 'W1': jax.random.normal(ks[6], (L, D, M), jnp.float32) * s, 'b1': jnp.zeros((L, M), jnp.float32), 'W2': jax.random.normal(ks[7], (L, M, D), jnp.float32) * s, 'b2': jnp.zeros((L, D), jnp.float32), 'g1': jnp.ones((L, D), jnp.float32), 'be1': jnp.zeros((L, D), jnp.float32), 'g2': jnp.ones((L, D), jnp.float32), 'be2': jnp.zeros((L, D), jnp.float32)}
    _L0_txt_all = _L0_txt_setup()
    _L0_txt_in = {k: v for k, v in _L0_txt_all.items() if k in ('emb', 'Wq', 'Wk', 'Wv', 'Wc', 'W1', 'b1', 'W2', 'b2', 'g1', 'be1', 'g2', 'be2')}
    del _L0_txt_all

    def _L0_attn_setup():
        import jax, jax.numpy as jnp
        import numpy as np
        B, S, D = (1, 1024, 256)
        H, KV, WIN = (8, 2, 64)
        HD = D // H
        FP16_MIN = -65504.0
        key = jax.random.key(seed)
        ks = jax.random.split(key, 10)
        sc = 0.02
        return {'x': jax.random.normal(ks[0], (B, S, D), dtype=jnp.float32), 'sink_bias': jnp.float32(0.0), 'Wq': jax.random.normal(ks[1], (H * HD, D), dtype=jnp.float32) * sc, 'bq': jnp.zeros((H * HD,), dtype=jnp.float32), 'Wk': jax.random.normal(ks[2], (KV * HD, D), dtype=jnp.float32) * sc, 'bk': jnp.zeros((KV * HD,), dtype=jnp.float32), 'Wv': jax.random.normal(ks[3], (KV * HD, D), dtype=jnp.float32) * sc, 'bv': jnp.zeros((KV * HD,), dtype=jnp.float32), 'Wo': jax.random.normal(ks[4], (D, H * HD), dtype=jnp.float32) * sc, 'bo': jnp.zeros((D,), dtype=jnp.float32)}
    _L0_attn_all = _L0_attn_setup()
    _L0_attn_in = {k: v for k, v in _L0_attn_all.items() if k in ('sink_bias', 'Wq', 'bq', 'Wk', 'bk', 'Wv', 'bv', 'Wo', 'bo')}
    del _L0_attn_all

    def _L0_ffn_setup():
        import jax, jax.numpy as jnp
        import numpy as np
        import math
        BETA = 0.9
        THRESHOLD = 1.0
        NUM_STEPS = 5
        ALPHA = 2.0

        @jax.custom_vjp
        def spike_fn(u):
            return (u > 0).astype(u.dtype)

        def _spike_fwd(u):
            return (spike_fn(u), u)

        def _spike_bwd(u, g):
            s = jnp.pi / 2.0 * ALPHA * u
            return (g * (ALPHA / 2.0) / (1.0 + s * s),)
        spike_fn.defvjp(_spike_fwd, _spike_bwd)
        key = jax.random.key(seed)
        k1, k2, k3 = jax.random.split(key, 3)
        n_embd = 256
        x = jax.random.normal(k1, (4, 512, n_embd), dtype=jnp.float32)
        W_fc = jax.random.normal(k2, (4 * n_embd, n_embd), dtype=jnp.float32) / math.sqrt(n_embd)
        W_proj = jax.random.normal(k3, (n_embd, 4 * n_embd), dtype=jnp.float32) / math.sqrt(4 * n_embd)
        return {'x': x, 'W_fc': W_fc, 'W_proj': W_proj}
    _L0_ffn_all = _L0_ffn_setup()
    _L0_ffn_in = {k: v for k, v in _L0_ffn_all.items() if k in ('W_fc', 'W_proj')}
    del _L0_ffn_all
    return {'x': x, 'x_txt': x_txt, 'L0_tok_vector_field': _L0_tok_in['vector_field'], 'L0_tok_nabla_w': _L0_tok_in['nabla_w'], 'L0_tok_div_w': _L0_tok_in['div_w'], 'L0_txt_emb': _L0_txt_in['emb'], 'L0_txt_Wq': _L0_txt_in['Wq'], 'L0_txt_Wk': _L0_txt_in['Wk'], 'L0_txt_Wv': _L0_txt_in['Wv'], 'L0_txt_Wc': _L0_txt_in['Wc'], 'L0_txt_W1': _L0_txt_in['W1'], 'L0_txt_b1': _L0_txt_in['b1'], 'L0_txt_W2': _L0_txt_in['W2'], 'L0_txt_b2': _L0_txt_in['b2'], 'L0_txt_g1': _L0_txt_in['g1'], 'L0_txt_be1': _L0_txt_in['be1'], 'L0_txt_g2': _L0_txt_in['g2'], 'L0_txt_be2': _L0_txt_in['be2'], 'L0_attn_sink_bias': _L0_attn_in['sink_bias'], 'L0_attn_Wq': _L0_attn_in['Wq'], 'L0_attn_bq': _L0_attn_in['bq'], 'L0_attn_Wk': _L0_attn_in['Wk'], 'L0_attn_bk': _L0_attn_in['bk'], 'L0_attn_Wv': _L0_attn_in['Wv'], 'L0_attn_bv': _L0_attn_in['bv'], 'L0_attn_Wo': _L0_attn_in['Wo'], 'L0_attn_bo': _L0_attn_in['bo'], 'L0_ffn_W_fc': _L0_ffn_in['W_fc'], 'L0_ffn_W_proj': _L0_ffn_in['W_proj']}

def reference(x, x_txt, L0_tok_vector_field, L0_tok_nabla_w, L0_tok_div_w, L0_txt_emb, L0_txt_Wq, L0_txt_Wk, L0_txt_Wv, L0_txt_Wc, L0_txt_W1, L0_txt_b1, L0_txt_W2, L0_txt_b2, L0_txt_g1, L0_txt_be1, L0_txt_g2, L0_txt_be2, L0_attn_sink_bias, L0_attn_Wq, L0_attn_bq, L0_attn_Wk, L0_attn_bk, L0_attn_Wv, L0_attn_bv, L0_attn_Wo, L0_attn_bo, L0_ffn_W_fc, L0_ffn_W_proj):
    import jax
    import jax.numpy as jnp

    def _L0_tok_ref(o, vector_field, nabla_w, div_w):
        import jax, jax.numpy as jnp
        import numpy as np
        EPS = 0.5
        TAU = 0.5
        MAXITER = 10
        NABLA_W = np.array([[[[0.0, 0.0, 0.0], [0.0, -1.0, 0.0], [0.0, 1.0, 0.0]]], [[[0.0, 0.0, 0.0], [0.0, -1.0, 1.0], [0.0, 0.0, 0.0]]]], dtype=np.float32)
        DIV_W = np.array([[[[0.0, -1.0, 0.0], [0.0, 1.0, 0.0], [0.0, 0.0, 0.0]], [[0.0, 0.0, 0.0], [-1.0, 1.0, 0.0], [0.0, 0.0, 0.0]]]], dtype=np.float32)

        def _conv(x, w):
            return jax.lax.conv_general_dilated(x, w, window_strides=(1, 1), padding='SAME', dimension_numbers=('NCHW', 'OIHW', 'NCHW'))
        o = o[:, 0]
        vf1 = vector_field[:, :, 1]
        vf0 = vector_field[:, :, 0]
        u = jax.nn.sigmoid(o / EPS)
        q = jnp.zeros_like(o)
        Tq = jnp.zeros_like(o)
        for _ in range(MAXITER):
            u_nabla = _conv(u[:, None], nabla_w)
            q = q - TAU * (u_nabla[:, 0] * vf1 + u_nabla[:, 1] * vf0)
            q = jnp.maximum(q, 0.0)
            Tq = _conv(jnp.stack([vf1 * q, vf0 * q], axis=1), div_w)[:, 0]
            u = jax.nn.sigmoid((o - Tq) / EPS)
        u1 = (o - Tq) / EPS
        return u1

    def _L0_txt_ref(x, emb, Wq, Wk, Wv, Wc, W1, b1, W2, b2, g1, be1, g2, be2):
        import jax, jax.numpy as jnp
        import numpy as np
        VOCAB, D, H, M, L, NMAX = (8000, 256, 16, 1024, 4, 256)
        KD = D // H
        EPS = 1e-05

        def positional_encoding(n, d):
            pos = jnp.arange(n, dtype=jnp.float32)[:, None]
            div = jnp.exp(jnp.arange(0, d, 2, dtype=jnp.float32) * (-jnp.log(10000.0) / d))
            ang = pos * div
            enc = jnp.zeros((n, d), dtype=jnp.float32)
            enc = enc.at[:, 0::2].set(jnp.sin(ang))
            enc = enc.at[:, 1::2].set(jnp.cos(ang))
            return enc

        def _layernorm(z, g, b):
            mu = jnp.mean(z, axis=-1, keepdims=True)
            var = jnp.mean((z - mu) ** 2, axis=-1, keepdims=True)
            return (z - mu) * jax.lax.rsqrt(var + EPS) * g + b

        def _block(h, p):
            wq, wk, wv, wc, w1, bb1, w2, bb2, gg1, e1, gg2, e2 = p
            B, n, d = h.shape

            def heads(w):
                return (h @ w).reshape(B, n, H, KD).transpose(0, 2, 1, 3)
            Q, K, V = (heads(wq), heads(wk), heads(wv))
            scores = jnp.einsum('bhqk,bhlk->bhql', Q, K) / np.sqrt(KD).astype(np.float32)
            attn = jax.nn.softmax(scores, axis=-1)
            out = jnp.einsum('bhql,bhlv->bhqv', attn, V)
            out = out.transpose(0, 2, 1, 3).reshape(B, n, d) @ wc
            h = _layernorm(h + out, gg1, e1)
            ff = jax.nn.relu(h @ w1 + bb1) @ w2 + bb2
            return _layernorm(h + ff, gg2, e2)
        B, n = x.shape
        h = emb[x] + positional_encoding(n, D)[None]

        def step(h, p):
            return (_block(h, p), None)
        h, _ = jax.lax.scan(step, h, (Wq, Wk, Wv, Wc, W1, b1, W2, b2, g1, be1, g2, be2))
        return h

    def _L0_attn_ref(x, sink_bias, Wq, bq, Wk, bk, Wv, bv, Wo, bo):
        import jax, jax.numpy as jnp
        import numpy as np
        B, S, D = (1, 1024, 256)
        H, KV, WIN = (8, 2, 64)
        HD = D // H
        FP16_MIN = -65504.0
        b, s, d = x.shape
        q = (x @ Wq.T + bq).reshape(b, s, H, HD).transpose(0, 2, 1, 3)
        k = (x @ Wk.T + bk).reshape(b, s, KV, HD).transpose(0, 2, 1, 3)
        v = (x @ Wv.T + bv).reshape(b, s, KV, HD).transpose(0, 2, 1, 3)
        k = jnp.repeat(k, H // KV, axis=1)
        v = jnp.repeat(v, H // KV, axis=1)
        scores = jnp.einsum('bhqd,bhkd->bhqk', q, k) / jnp.sqrt(jnp.float32(HD))
        i = jnp.arange(s)[:, None]
        j = jnp.arange(s)[None, :]
        mask = (j <= i) & (j > i - WIN)
        scores = jnp.where(mask, scores, FP16_MIN)
        m = jnp.maximum(scores.max(axis=-1, keepdims=True), sink_bias)
        e = jnp.exp(scores - m)
        sink = jnp.exp(sink_bias - m)
        attn = e / (e.sum(axis=-1, keepdims=True) + sink)
        out = jnp.einsum('bhqk,bhkd->bhqd', attn, v)
        out = out.transpose(0, 2, 1, 3).reshape(b, s, H * HD)
        return out @ Wo.T + bo

    def _L0_ffn_ref(x, W_fc, W_proj):
        import jax, jax.numpy as jnp
        import numpy as np
        import math
        BETA = 0.9
        THRESHOLD = 1.0
        NUM_STEPS = 5
        ALPHA = 2.0

        @jax.custom_vjp
        def spike_fn(u):
            return (u > 0).astype(u.dtype)

        def _spike_fwd(u):
            return (spike_fn(u), u)

        def _spike_bwd(u, g):
            s = jnp.pi / 2.0 * ALPHA * u
            return (g * (ALPHA / 2.0) / (1.0 + s * s),)
        spike_fn.defvjp(_spike_fwd, _spike_bwd)
        h = jnp.square(jax.nn.relu(jnp.einsum('bsd,fd->bsf', x, W_fc)))
        y = jnp.einsum('bsf,df->bsd', h, W_proj)

        def step(mem, _):
            reset = jax.lax.stop_gradient(spike_fn(mem - THRESHOLD))
            mem_new = BETA * mem + y - reset * THRESHOLD
            spk = spike_fn(mem_new - THRESHOLD)
            return (mem_new, spk)
        mem0 = jnp.zeros_like(y)
        _, spks = jax.lax.scan(step, mem0, None, length=NUM_STEPS)
        return jnp.sum(spks, axis=0) / NUM_STEPS
    h = _L0_tok_ref(x, L0_tok_vector_field, L0_tok_nabla_w, L0_tok_div_w)
    h = jnp.concatenate([h, _L0_txt_ref(x_txt, L0_txt_emb, L0_txt_Wq, L0_txt_Wk, L0_txt_Wv, L0_txt_Wc, L0_txt_W1, L0_txt_b1, L0_txt_W2, L0_txt_b2, L0_txt_g1, L0_txt_be1, L0_txt_g2, L0_txt_be2)], axis=1)
    h = h + _L0_attn_ref(_layernorm(h, axis=-1), L0_attn_sink_bias, L0_attn_Wq, L0_attn_bq, L0_attn_Wk, L0_attn_bk, L0_attn_Wv, L0_attn_bv, L0_attn_Wo, L0_attn_bo)
    h = h + _L0_ffn_ref(_layernorm(h, axis=-1), L0_ffn_W_fc, L0_ffn_W_proj)
    return h

_drawn_inputs = setup_inputs


def setup_inputs(seed=0):
    import zlib

    import numpy as np

    out = dict(_drawn_inputs(seed))
    spreads = {'L0_txt_b1': (0.0, 0.1),
     'L0_txt_b2': (0.0, 0.1),
     'L0_txt_g1': (1.0, 0.2),
     'L0_txt_be1': (0.0, 0.1),
     'L0_txt_g2': (1.0, 0.2),
     'L0_txt_be2': (0.0, 0.1),
     'L0_attn_bq': (0.0, 0.8),
     'L0_attn_bk': (0.0, 0.8),
     'L0_attn_bv': (0.0, 0.281),
     'L0_attn_bo': (0.0, 0.1)}
    factors = {'L0_txt_emb': 3.33,
     'L0_txt_Wq': 8.0,
     'L0_txt_Wk': 8.0,
     'L0_attn_Wq': 8.0,
     'L0_attn_Wk': 8.0}
    for name, (base, spread) in spreads.items():
        noise = np.random.default_rng([zlib.crc32(name.encode()), seed]).standard_normal(out[name].shape)
        drawn = base * np.exp(spread * noise) if base else spread * noise
        out[name] = jnp.asarray(drawn.astype(out[name].dtype))
    for name, factor in factors.items():
        out[name] = (out[name] * factor).astype(out[name].dtype)
    return out
```

```python
from contextlib import ExitStack

import concourse.bass as bass
from concourse import mybir

F32 = mybir.dt.float32
BF16 = mybir.dt.bfloat16
I32 = mybir.dt.int32
U32 = mybir.dt.uint32
ALU = mybir.AluOpType
ACT = mybir.ActivationFunctionType
AX = mybir.AxisListType

P = 128
B, IMG = 8, 256
D, KC = 256, 2
SEQ = 128
VOCAB = 8000
LAYERS, TH, TKD, M = 4, 16, 16, 1024
MC = M // P
TOK = IMG + SEQ
TT = TOK // P
WIN, FH, FKV, HD = 64, 8, 2, 32
EPS = 1e-5
ITERS = 10
PAIRS = B // 2
RPP = IMG // 64
SLOTS = 2 * ITERS
HALF = 8
MASKED = -65536.0
STEPS = 5
SCALE_T = float(TKD) ** -0.5
SCALE_F = float(HD) ** -0.5
ORDER = [("A", 0), ("A", 1), ("F", 0), ("A", 2), ("F", 1), ("A", 3), ("F", 2), ("F", 3)]


def build(nc, d, out):
    with ExitStack() as ctx:
        def sb(name, shape, dt=F32):
            return ctx.enter_context(nc.sbuf_tensor(name, shape, dt))

        def ps(name, shape, dt=F32):
            return ctx.enter_context(nc.psum_tensor(name, shape, dt))

        def sem(name):
            return ctx.enter_context(nc.semaphore(name))

        filtered = nc.dram_tensor("filtered", (2, B, IMG, IMG), F32, kind="Internal").ap()

        ident = sb("ident", [P, P])
        ident_h = sb("ident_h", [P, P], BF16)
        up_shift = sb("up_shift", [P, P])
        down_shift = sb("down_shift", [P, P])
        edge = sb("edge", [1, P])
        ones = sb("ones", [P, 4 * P])
        mask = sb("mask", [P, 2, 4, P], BF16)
        head_mask = sb("head_mask", [P, 2])
        pow_half = sb("pow_half", [P, 4])
        row_mask = sb("row_mask", [P, 4])
        bq_m = sb("bq_m", [P, KC, 4])
        eps_c = sb("eps_c", [P, 4])
        pe = sb("pe", [P, D])
        taps = sb("taps", [P, 36])
        taps_std = sb("taps_std", [P, 36])
        taps_diff = sb("taps_diff", [P, 36])
        general_f = sb("general_f", [P, 1])
        general = sb("general", [P, 1], I32)

        tokens = sb("tokens", [P, B], I32)
        tok_f = sb("tok_f", [P, B])
        tok_neg = sb("tok_neg", [P, B])
        tok_idx = sb("tok_idx", [P, B], U32)
        h = sb("h", [P, B, D])
        w_attn = sb("w_attn", [P, KC, 4 * D])
        w1 = sb("w1", [P, KC, M])
        w2 = sb("w2", [P, MC, D])
        vecs = sb("vecs", [P, 5, D])
        b1 = sb("b1", [P, MC])
        hT = sb("hT", [P, KC, D])
        qm = sb("qm", [P, 2, KC, D])
        kT = sb("kT", [P, KC, D])
        v = sb("v", [P, 2, TH, TKD + 1])
        prob = sb("prob", [P, 2, HALF, P])
        probT = sb("probT", [P, HALF, P])
        neg_max = sb("neg_max", [P, 2, HALF])
        rden = sb("rden", [P, TH])
        attn = sb("attn", [P, 2, D])
        attnT = sb("attnT", [P, KC, D])
        hidT = sb("hidT", [P, MC, D])
        stats = sb("stats", [P, TT, 6])
        mv = sb("mv", [P, TT, 2])
        var_eps = sb("var_eps", [P, TT])
        rstd = sb("rstd", [P, TT])

        o_all = sb("o_all", [P, PAIRS, RPP, IMG])
        vf = sb("vf", [P, 2, RPP, IMG])
        vq = sb("vq", [P, 2, RPP, IMG])
        u = sb("u", [P, RPP, IMG + 1])
        f3 = sb("f3", [P, 3, RPP, IMG])
        fa, fb, q_st = f3[:, 0], f3[:, 1], f3[:, 2]
        p1 = sb("p1", [P, RPP, IMG])
        p0 = sb("p0", [P, RPP, IMG + 1])
        f_out = sb("f_out", [P, RPP, IMG])

        wq_f = sb("wq_f", [P, KC, D])
        wk_f = sb("wk_f", [P, KC, FKV, P])
        wv_f = sb("wv_f", [P, KC, FKV * HD])
        wo_f = sb("wo_f", [P, KC, D])
        w_fc = sb("w_fc", [P, KC, M])
        w_pr = sb("w_pr", [P, MC, D])
        bq_f = sb("bq_f", [P, KC])
        bk_f = sb("bk_f", [P, FKV])
        bv_f = sb("bv_f", [P, FKV * HD])
        bo_f = sb("bo_f", [P, D])
        sink = sb("sink", [P, 1])
        x = sb("x", [P, 2, TT, D])
        xn = sb("xn", [P, TT, D])
        xnT = sb("xnT", [P, KC, WIN + TOK])
        kT_f = sb("kT_f", [P, FKV, WIN + TOK])
        v_f = sb("v_f", [P, 2 * TT, FKV, HD + 1])
        sink_e = sb("sink_e", [P, 2, FH])
        rmax = sb("rmax", [P, 2, FH])
        den = sb("den", [P, FH])
        rden_f = sb("rden_f", [P, FH])
        attn_f = sb("attn_f", [P, TT, D])
        attnT_f = sb("attnT_f", [P, KC, TOK])
        xn2 = sb("xn2", [P, 2, TT, D])
        xn2T = sb("xn2T", [P, KC, TOK])
        hid_f = o_all[:, :, :, :].rearrange("p a r c -> p (a r c)")[:, 0:MC * TOK].rearrange("p (m t) -> p m t", m=MC)
        qz = f3[:, :, :, :].rearrange("p a r c -> p (a r c)")[:, 0:4 * KC * TOK].rearrange("p (r c t) -> p r c t", r=4, c=KC)
        spare = vf[:, :, :, :].rearrange("p a r c -> p (a r c)")
        spare2 = vq[:, :, :, :].rearrange("p a r c -> p (a r c)")
        mem = spare[:, 0:TT * D]
        mem_t = spare[:, TT * D:2 * TT * D]
        spikes = spare2[:, 0:TT * D]

        def ringed(t):
            return t[:, 0:4 * (IMG + 2)].rearrange("p (r c) -> p r c", r=4)

        gen_u = ringed(x[:].rearrange("p a t n -> p (a t n)"))
        gen_p = [ringed(xn2[:].rearrange("p a t n -> p (a t n)")), ringed(prob[:].rearrange("p a h k -> p (a h k)"))]
        rows2 = lambda t: t.rearrange("p (r c) -> p r c", r=2)
        hid_flat = hidT[:].rearrange("p m n -> p (m n)")
        gen_vf = [rows2(hid_flat[:, 512 * k:512 * k + 512]) for k in range(2)]
        gen_q, gen_t = rows2(hid_flat[:, 1024:1536]), rows2(hid_flat[:, 1536:2048])
        qm_flat = qm[:].rearrange("p a c n -> p (a c n)")
        gen_g = [rows2(qm_flat[:, 512 * k:512 * k + 512]) for k in range(2)]
        probT_flat = probT[:].rearrange("p h k -> p (h k)")
        gen_o, gen_w = rows2(probT_flat[:, 0:512]), rows2(probT_flat[:, 512:1024])

        halo = ps("halo", [P, 2, IMG])
        ps_s = [ps(f"ps_s{i}", [P, HALF, P]) for i in range(2)]
        ps_t = ps("ps_t", [P, 2, 512])
        ps_m = ps("ps_m", [P, 512])
        s_flat = [t[:, :, :].rearrange("p h k -> p (h k)") for t in ps_s]
        quad = [s_flat[0][:, 0:512], s_flat[0][:, 512:1024], s_flat[1][:, 0:512], s_flat[1][:, 512:1024]]
        t_flat = ps_t[:, :, :].rearrange("p a n -> p (a n)")
        t_heads = t_flat.rearrange("p (h k) -> p h k", h=HALF)
        halo_flat = halo[:, :, :].rearrange("p a n -> p (a n)")

        names = [
            "l_vec", "l_attn", "l_w1", "l_w2", "l_bc", "l_tok", "l_img", "l_fus", "st_img", "st_out", "g_emb",
            "l_taps",
            "c_pool", "c_scaled", "c_idx", "c_general",
            "pe_hT", "pe_q", "pe_k", "pe_v", "pe_s", "pe_pT", "pe_o", "pe_oT", "pe_wc", "pe_h1T", "pe_ff1", "pe_ff2",
            "act_hT", "act_q", "act_k", "act_v", "act_exp", "act_pT", "act_oT", "act_h1T", "act_ff1",
            "dve_max", "dve_attn", "dve_wc", "dve_ln1", "dve_ff2", "h_ready", "dve_stat", "pool_rstd", "pool_eps",
            "pe_halo", "act_tanh", "act_img", "dve_flux", "dve_div",
            "f_xt", "f_xnT_ps", "f_xnT", "f_q_ps", "f_q", "f_k_ps", "f_k", "f_v_ps", "f_v", "f_s", "f_max", "f_exp", "f_sink",
            "f_pT_ps", "f_pT", "f_o", "f_attn", "f_oT_ps", "f_oT", "f_y_ps", "f_y", "f_xn", "f_xn2", "f_xn2T_ps", "f_xn2T",
            "f_h_ps", "f_relu", "f_sq", "f_z_ps", "f_z", "f_out", "f_stat", "f_rstd", "f_eps",
            "chain",
            "gen_vf_in", "gen_free", "gen_o_in", "gen_tanh", "gen_u_done", "gen_halo_u", "gen_flux", "gen_halo_p", "gen_div",
            "gen_out", "gen_st", "gen_zero",
        ]
        s = {n: sem(n) for n in names}

        l_x = [sem(f"l_x{j}") for j in range(2)]

        block = ctx.enter_context(nc.Block())

        def head_of(g, hh):
            return 8 * (hh // 2 % 2) + 2 * (2 * g + hh // 4) + hh % 2

        @block.sync
        def _(sp):
            sp.dma_start(taps[:, 0:18], d["nabla_w"].partition_broadcast(P)).then_inc(s["l_taps"], 16)
            sp.dma_start(taps[:, 18:36], d["div_w"].partition_broadcast(P)).then_inc(s["l_taps"], 16)
            sp.dma_start(tokens[:], d["tokens"]).then_inc(s["l_tok"], 16)
            sp.dma_start(pe[:], d["pe"]).then_inc(s["l_tok"], 16)
            for img in range(2):
                for comp in range(2):
                    sp.dma_start(vf[64 * img:64 * img + 64, comp], d["vf"][comp].rearrange("(p r) c -> p r c", r=RPP)).then_inc(s["l_img"], 16)
            for pair in range(PAIRS):
                sp.dma_start(o_all[:, pair], d["o"][2 * pair:2 * pair + 2].rearrange("b (p r) c -> (b p) r c", r=RPP)).then_inc(s["l_img"], 16)
            sp.dma_start(w_attn[:], d["w_attn"][0]).then_inc(s["l_attn"], 16)
            sp.dma_start(b1[:], d["b1"][0]).then_inc(s["l_bc"], 16)
            sp.dma_start(vecs[:], d["vecs"][0].partition_broadcast(P)).then_inc(s["l_vec"], 16)
            sp.dma_start(w1[:], d["w1"][0]).then_inc(s["l_w1"], 16)
            sp.dma_start(w2[:], d["w2"][0]).then_inc(s["l_w2"], 16)
            for t, n in ((wq_f, "wq_f"), (wk_f, "wk_f"), (wv_f, "wv_f"), (wo_f, "wo_f"), (w_fc, "w_fc"), (w_pr, "w_pr"), (bq_f, "bq_f"), (bk_f, "bk_f")):
                sp.dma_start(t[:], d[n]).then_inc(s["l_fus"], 16)
            for t, n in ((bv_f, "bv_f"), (bo_f, "bo_f"), (sink, "sink")):
                sp.dma_start(t[:], d[n].partition_broadcast(P)).then_inc(s["l_fus"], 16)

            sp.wait_ge(s["c_general"], 1)
            which = sp.value_load(general[0:1, 0:1], min_val=0, max_val=1)
            with sp.If(which > 0):
                for k in range(2):
                    sp.dma_start(gen_vf[k], d["vf"][k].rearrange("(p r) c -> p r c", r=2)).then_inc(s["gen_vf_in"], 16)

                def ring_rows(t, done):
                    sp.dma_start(t[1:P, 0], t[0:P - 1, 2]).then_inc(done, 16)
                    sp.dma_start(t[0:P - 1, 3], t[1:P, 1]).then_inc(done, 16)

                with sp.Fori(0, B) as b:
                    sp.wait_ge(s["gen_free"], b + 1)
                    sp.dma_start(gen_o, d["o"][bass.ds(b, 1)].rearrange("b (p r) c -> p (b r) c", r=2)).then_inc(s["gen_o_in"], 16)
                    with sp.Fori(0, ITERS) as it:
                        sp.wait_ge(s["gen_u_done"], (ITERS + 1) * b + it + 2)
                        ring_rows(gen_u, s["gen_halo_u"])
                        sp.wait_ge(s["gen_flux"], ITERS * b + it + 1)
                        for k in range(2):
                            ring_rows(gen_p[k], s["gen_halo_p"])
                    sp.wait_ge(s["gen_out"], b + 1)
                    sp.dma_start(filtered[1][bass.ds(b, 1)].rearrange("b (p r) c -> p (b r) c", r=2), gen_w).then_inc(s["gen_st"], 16)
                sp.wait_ge(s["gen_st"], 16 * B)

            def store_pair(l):
                sp.wait_ge(s["act_img"], l + 1)
                dst = filtered[0].rearrange("(a b) (p r) c -> a (b p) r c", b=2, r=RPP)
                dst = dst[l] if isinstance(l, int) else dst[bass.ds(l, 1)].rearrange("a p r c -> p (a r) c")
                sp.dma_start(dst, f_out[:]).then_inc(s["st_img"], 16)

            with sp.Fori(0, LAYERS - 1) as l:
                sp.wait_ge(s["pe_wc"], 4 * l + 4)
                sp.dma_start(w_attn[:], d["w_attn"][bass.ds(l + 1, 1)].rearrange("a p c n -> p (a c) n")).then_inc(s["l_attn"], 16)
                sp.wait_ge(s["pe_ff1"], 16 * l + 16)
                sp.dma_start(w1[:], d["w1"][bass.ds(l + 1, 1)].rearrange("a p c n -> p (a c) n")).then_inc(s["l_w1"], 16)
                sp.wait_ge(s["pe_ff2"], 4 * l + 4)
                sp.dma_start(w2[:], d["w2"][bass.ds(l + 1, 1)].rearrange("a p c n -> p (a c) n")).then_inc(s["l_w2"], 16)
                sp.wait_ge(s["h_ready"], 4 * l + 8)
                sp.dma_start(vecs[:], d["vecs"][bass.ds(l + 1, 1)].partition_broadcast(P).rearrange("p a v n -> p (a v) n")).then_inc(s["l_vec"], 16)
                sp.wait_ge(s["act_ff1"], 16 * l + 16)
                sp.dma_start(b1[:], d["b1"][bass.ds(l + 1, 1)].rearrange("a p m -> p (a m)")).then_inc(s["l_bc"], 16)
                store_pair(l)
            store_pair(LAYERS - 1)

            sp.wait_ge(s["st_img"], 16 * PAIRS + 16)
            out_v = out.rearrange("b (t p) n -> b p t n", p=P)

            def load_x(b, j):
                src = filtered[bass.ds(which, 1), bass.ds(b, 1)].rearrange("w b (t p) c -> p (w b t) c", p=P)
                sp.dma_start(x[:, j, 0:2], src).then_inc(l_x[j], 16)

            def store(b, j):
                sp.wait_ge(s["f_out"], b + 1)
                sp.dma_start(out_v[bass.ds(b, 1)].rearrange("b p t n -> p (b t) n"), x[:, j]).then_inc(s["st_out"], 16)

            for j in range(2):
                load_x(j, j)
            with sp.Fori(0, B // 2 - 1) as g:
                for j in range(2):
                    store(2 * g + j, j)
                sp.wait_ge(s["st_out"], 32 * g + 48)
                for j in range(2):
                    load_x(2 * g + 2 + j, j)
            for j in range(2):
                store(B - 2 + j, j)
            sp.wait_ge(s["st_out"], 16 * B + 16)

        @block.gpsimd
        def _(pool):
            c = 0
            def const(ins):
                nonlocal c
                ins.then_inc(s["c_pool"], 1)
                c += 1
                pool.wait_ge(s["c_pool"], c)
            const(pool.memset(ones[:], 1.0))
            const(pool.memset(mask[:], 0.0))
            const(pool.affine_select(out=ident[:], in_=ones[:, 0:P], compare_op=ALU.is_equal, fill=0.0, base=0, pattern=[[-1, P]], channel_multiplier=1))
            const(pool.tensor_copy(ident_h[:], ident[:]))
            const(pool.affine_select(out=up_shift[:], in_=ones[:, 0:P], compare_op=ALU.is_equal, fill=0.0, base=-1, pattern=[[-1, P]], channel_multiplier=1))
            const(pool.affine_select(out=down_shift[:], in_=ones[:, 0:P], compare_op=ALU.is_equal, fill=0.0, base=1, pattern=[[-1, P]], channel_multiplier=1))
            const(pool.memset(up_shift[:, 63:64], 0.0))
            const(pool.memset(down_shift[:, 64:65], 0.0))
            const(pool.memset(edge[:], 0.0))
            const(pool.memset(edge[:, 63:64], -1.0))
            const(pool.memset(edge[:, 127:128], -1.0))
            const(pool.memset(pow_half[:], -0.5))
            const(pool.memset(eps_c[:], EPS))
            for first in range(2):
                for half in range(2):
                    m = mask[64 * half:64 * half + 64, first]
                    const(pool.affine_select(out=m, in_=m, compare_op=ALU.is_gt, fill=MASKED, base=0, pattern=[[0, 4], [1, P]], channel_multiplier=-1))
                    const(pool.affine_select(out=m, in_=m, compare_op=ALU.is_ge, fill=MASKED, base=WIN, pattern=[[0, 4], [-1, P]], channel_multiplier=1))
                    if first and half == 0:
                        const(pool.affine_select(out=m, in_=m, compare_op=ALU.is_ge, fill=MASKED, base=-WIN, pattern=[[0, 4], [1, P]], channel_multiplier=0))
            for t in (v[:, :, :, TKD:], v_f[:, :, :, HD:]):
                const(pool.memset(t, 1.0))
            for t in (xnT[:, :, 0:WIN], kT_f[:, :, 0:WIN], p0[:, :, 0:1]):
                const(pool.memset(t, 0.0))
            const(pool.memset(u[:, :, IMG:], -1.0))

            pool.wait_ge(s["c_idx"], 1)
            for b in range(B):
                pool.indirect_dma_start(h[:, b, :], None, d["emb"], bass.IndirectOffsetOnAxis(ap=tok_idx[:, b:b + 1], axis=0)).then_inc(s["g_emb"], 16)

            with pool.Fori(0, 2 * LAYERS * PAIRS) as n:
                pool.wait_ge(s["dve_stat"], n + 1)
                pool.tensor_tensor(var_eps[:, 0:2], mv[:, 0:2, 1], eps_c[:, 0:2], ALU.add).then_inc(s["pool_eps"], 1)
                pool.wait_ge(s["pool_eps"], n + 1)
                pool.tensor_tensor(rstd[:, 0:2], var_eps[:, 0:2], pow_half[:, 0:2], ALU.pow).then_inc(s["pool_rstd"], 1)
            with pool.Fori(0, 2 * B) as n:
                pool.wait_ge(s["f_stat"], n + 1)
                pool.tensor_tensor(var_eps[:], mv[:, :, 1], eps_c[:, 0:TT], ALU.add).then_inc(s["f_eps"], 1)
                pool.wait_ge(s["f_eps"], n + 1)
                pool.tensor_tensor(rstd[:], var_eps[:], pow_half[:, 0:TT], ALU.pow).then_inc(s["f_rstd"], 1)

        N_CONST = 13 + 9 + 2 + 3 + 1

        @block.tensor
        def _(pe_):
            mm, tr = pe_.matmul, pe_.transpose

            def filter_slot(l, k):
                if k % 2 == 0:
                    pe_.wait_ge(s["act_tanh"], ITERS * l + k // 2 + 1)
                    mm(halo[:, 0], up_shift[:], u[:, 0, 0:IMG], start=True, stop=False)
                    mm(halo[:, 0], edge[:], ones[0:1, 0:IMG], start=False, stop=True).then_inc(s["pe_halo"], 1)
                else:
                    pe_.wait_ge(s["dve_flux"], ITERS * l + k // 2 + 1)
                    mm(halo[:, 1], down_shift[:], p1[:, RPP - 1], start=True, stop=True).then_inc(s["pe_halo"], 1)

            def scores(l, i, n):
                t, g = n // 2, n % 2
                if n == 0:
                    pe_.wait_ge(s["act_q"], 4 * l + i + 1)
                    pe_.wait_ge(s["act_k"], 4 * l + i + 1)
                    pe_.wait_ge(s["act_v"], 4 * l + i + 1)
                for hh in (0, 4, 1, 5, 2, 6, 3, 7):
                    r, c, odd = 32 * (2 * g + hh // 4), hh // 2 % 2, hh % 2
                    last = mm(ps_s[g][:, hh], qm[r:r + 32, odd, c, P * t:P * t + P], kT[r:r + 32, c, P * t:P * t + P], start=True, stop=True)
                last.then_inc(s["pe_s"], 1)

            def turn_probs(l, i, n, done):
                pe_.wait_ge(s["act_exp"], 16 * l + 4 * i + n + 1)
                if n == 0:
                    pe_.wait_ge(s["dve_ff2"], 4 * l + done + 1)
                    pe_.wait_ge(s["dve_wc"], 4 * l + i + 1)
                for hh in range(HALF):
                    last = tr(t_heads[:, hh], prob[:, n % 2, hh], ident[:])
                last.then_inc(s["pe_pT"], 1)

            def attend(l, i, n):
                t, g = n // 2, n % 2
                pe_.wait_ge(s["act_pT"], 16 * l + 4 * i + n + 1)
                if n == 2:
                    pe_.wait_ge(s["dve_attn"], 8 * l + 2 * i + 1)
                for hh in range(HALF):
                    head = head_of(g, hh)
                    last = mm(ps_m[:, 17 * head:17 * head + 17], probT[:, hh], v[:, t, head], start=True, stop=True)
                if g == 1:
                    last.then_inc(s["pe_o"], 1)

            def part_a(l, i, done, slot):
                pe_.wait_ge(s["h_ready"], 4 * l + i + 1)
                pe_.wait_ge(s["l_attn"], 16 * l + 16)
                for t in range(2):
                    for c in range(KC):
                        last = tr(ps_m[:, D * c + P * t:D * c + P * t + P], h[:, 2 * i + t, P * c:P * c + P], ident[:])
                last.then_inc(s["pe_hT"], 1)
                pe_.wait_ge(s["act_hT"], 4 * l + i + 1)
                for w, dst, done_s in ((0, quad[0], s["pe_q"]), (1, quad[1], s["pe_k"])):
                    for m in range(KC):
                        for c in range(KC):
                            last = mm(dst[:, D * m:D * m + D], w_attn[:, c, D * w + P * m:D * w + P * m + P], hT[:, c], start=(c == 0), stop=(c == KC - 1))
                    last.then_inc(done_s, 1)
                for t in range(2):
                    for c in range(KC):
                        last = mm(quad[2][:, D * t:D * t + D], hT[:, c, P * t:P * t + P], w_attn[:, c, 2 * D:3 * D], start=(c == 0), stop=(c == KC - 1))
                last.then_inc(s["pe_v"], 1)
                scores(l, i, 0)
                scores(l, i, 1)
                filter_slot(l, slot)
                turn_probs(l, i, 0, done)
                attend(l, i, 0)
                scores(l, i, 2)
                filter_slot(l, slot + 1)
                turn_probs(l, i, 1, done)
                attend(l, i, 1)
                scores(l, i, 3)
                filter_slot(l, slot + 2)
                turn_probs(l, i, 2, done)
                attend(l, i, 2)
                turn_probs(l, i, 3, done)
                attend(l, i, 3)
                filter_slot(l, slot + 3)
                pe_.wait_ge(s["dve_attn"], 8 * l + 2 * i + 2)
                for t in range(2):
                    for c in range(KC):
                        last = tr(ps_m[:, D * c + P * t:D * c + P * t + P], attn[:, t, P * c:P * c + P], ident[:])
                last.then_inc(s["pe_oT"], 1)
                pe_.wait_ge(s["act_oT"], 4 * l + i + 1)
                for t in range(2):
                    for c in range(KC):
                        last = mm(ps_t[:, 1, D * t:D * t + D], attnT[:, c, P * t:P * t + P], w_attn[:, c, 3 * D:4 * D], start=(c == 0), stop=(c == KC - 1))
                last.then_inc(s["pe_wc"], 1)

            def part_f(l, i, slot):
                pe_.wait_ge(s["dve_ln1"], 4 * l + i + 1)
                for t in range(2):
                    for c in range(KC):
                        last = tr(ps_m[:, D * c + P * t:D * c + P * t + P], h[:, 2 * i + t, P * c:P * c + P], ident[:])
                last.then_inc(s["pe_h1T"], 1)
                pe_.wait_ge(s["act_h1T"], 4 * l + i + 1)
                pe_.wait_ge(s["l_w1"], 16 * l + 16)
                for m in range(MC):
                    for c in range(KC):
                        last = mm(quad[m // 2][:, D * (m % 2):D * (m % 2) + D], w1[:, c, P * m:P * m + P], hT[:, c], start=(c == 0), stop=(c == KC - 1))
                    if m % 2:
                        last.then_inc(s["pe_ff1"], 1)
                pe_.wait_ge(s["l_w2"], 16 * l + 16)
                pe_.wait_ge(s["dve_ff2"], 4 * l + i + 1)
                for t in range(2):
                    for m in range(MC):
                        if t == 0 and m % 2 == 0:
                            pe_.wait_ge(s["act_ff1"], 16 * l + 4 * i + m // 2 + 1)
                        last = mm(ps_t[:, 0, D * t:D * t + D], hidT[:, m, P * t:P * t + P], w2[:, m], start=(m == 0), stop=(m == MC - 1))
                last.then_inc(s["pe_ff2"], 1)
                filter_slot(l, slot)

            pe_.wait_ge(s["c_pool"], N_CONST)
            with pe_.Fori(0, LAYERS) as l:
                slot = done = 0
                for what, i in ORDER:
                    if what == "A":
                        part_a(l, i, done, slot)
                        slot += 4
                    else:
                        part_f(l, i, slot)
                        slot += 1
                        done += 1

            def tile_scores(n, t):
                bank = ps_s[t % 2]
                if t == 2:
                    pe_.wait_ge(s["f_exp"], TT * n + 1)
                m = mask[:, 1 if t == 0 else 0].rearrange("p a k -> p (a k)")
                for hb in range(2):
                    flat = bank[:, 4 * hb:4 * hb + 4].rearrange("p h k -> p (h k)")
                    mm(flat, ident_h[:], m, start=True, stop=False, skip_group_check=True)
                    for hh in range(4 * hb, 4 * hb + 4):
                        r, c = hh % 4, hh // 4
                        for half in range(2):
                            at = P * t + WIN * half
                            last = mm(bank[WIN * half:WIN * half + WIN, hh], qz[:, r, c, at:at + WIN], kT_f[:, c, at:at + P],
                                      start=False, stop=(hh % 4 == 3), skip_group_check=True)
                last.then_inc(s["f_s"], 1)

            def tile_attend(n, t):
                pe_.wait_ge(s["f_exp"], TT * n + t + 1)
                if t == 0:
                    pe_.wait_ge(s["f_v"], n + 1)
                for hh in range(FH):
                    last = tr(t_heads[:, hh], prob[:, t % 2, hh], ident[:])
                last.then_inc(s["f_pT_ps"], 1)
                pe_.wait_ge(s["f_pT"], TT * n + t + 1)
                if t:
                    pe_.wait_ge(s["f_attn"], TT * n + t)
                for hh in range(FH):
                    for half in range(2):
                        last = mm(ps_m[WIN * half:WIN * half + WIN, 33 * hh:33 * hh + 33], probT[:, hh, WIN * half:WIN * half + WIN],
                                  v_f[:, 2 * t + half, hh // 4], start=True, stop=True)
                last.then_inc(s["f_o"], 1)

            def fuse_a(n, j):
                pe_.wait_ge(s["f_xn"], n + 1)
                for c in range(KC):
                    bank = ps_m if c == 0 else halo_flat
                    for t in range(TT):
                        last = tr(bank[:, P * t:P * t + P], xn[:, t, P * c:P * c + P], ident[:])
                last.then_inc(s["f_xnT_ps"], 1)
                pe_.wait_ge(s["f_xnT"], n + 1)
                for m in range(KC):
                    for c in range(KC):
                        last = mm(quad[m][:, 0:TOK], wq_f[:, c, P * m:P * m + P], xnT[:, c, WIN:], start=(c == 0), stop=(c == KC - 1))
                last.then_inc(s["f_q_ps"], 1)
                for m in range(FKV):
                    for c in range(KC):
                        last = mm(quad[2 + m][:, 0:TOK], wk_f[:, c, m], xnT[:, c, WIN:], start=(c == 0), stop=(c == KC - 1))
                last.then_inc(s["f_k_ps"], 1)
                pe_.wait_ge(s["f_z"], n - j + 1)
                pe_.wait_ge(s["f_y"], n + 1)
                for w in range(2 * TT):
                    for c in range(KC):
                        last = mm(ps_t[:, 0, 64 * w:64 * w + 64], xnT[:, c, WIN * w:WIN * w + P], wv_f[:, c], start=(c == 0), stop=(c == KC - 1))
                last.then_inc(s["f_v_ps"], 1)
                pe_.wait_ge(s["f_q"], n + 1)
                pe_.wait_ge(s["f_k"], n + 1)
                tile_scores(n, 0)
                tile_scores(n, 1)
                tile_attend(n, 0)
                tile_scores(n, 2)
                tile_attend(n, 1)
                tile_attend(n, 2)
                pe_.wait_ge(s["f_attn"], TT * n + TT)
                for c in range(KC):
                    bank = ps_m if c == 0 else halo_flat
                    for t in range(TT):
                        last = tr(bank[:, P * t:P * t + P], attn_f[:, t, P * c:P * c + P], ident[:])
                last.then_inc(s["f_oT_ps"], 1)
                pe_.wait_ge(s["f_oT"], n + 1)
                for t in range(TT):
                    for c in range(KC):
                        last = mm(t_flat[:, D * t:D * t + D], attnT_f[:, c, P * t:P * t + P], wo_f[:, c], start=(c == 0), stop=(c == KC - 1))
                last.then_inc(s["f_y_ps"], 1)

            def fuse_f(n, j):
                pe_.wait_ge(s["f_xn2"], n + 1)
                for c in range(KC):
                    bank = ps_m if c == 0 else halo_flat
                    for t in range(TT):
                        last = tr(bank[:, P * t:P * t + P], xn2[:, j, t, P * c:P * c + P], ident[:])
                last.then_inc(s["f_xn2T_ps"], 1)
                pe_.wait_ge(s["f_xn2T"], n + 1)
                for m in range(MC):
                    if m >= 4:
                        pe_.wait_ge(s["f_relu"], MC * n + m - 3)
                    for c in range(KC):
                        last = mm(quad[m % 4][:, 0:TOK], w_fc[:, c, P * m:P * m + P], xn2T[:, c], start=(c == 0), stop=(c == KC - 1))
                    last.then_inc(s["f_h_ps"], 1)
                pe_.wait_ge(s["f_y"], n + 3 - j)
                for t in range(TT):
                    for m in range(MC):
                        if t == 0:
                            pe_.wait_ge(s["f_sq"], MC * n + m + 1)
                        if t == 0 and m == 0 and j == 1:
                            pe_.wait_ge(s["f_z"], n + 1)
                        last = mm(t_flat[:, D * t:D * t + D], hid_f[:, m, P * t:P * t + P], w_pr[:, m], start=(m == 0), stop=(m == MC - 1))
                last.then_inc(s["f_z_ps"], 1)

            pe_.wait_ge(s["l_fus"], 16 * 11)
            with pe_.Fori(0, B // 2) as g:
                for j in range(2):
                    fuse_a(2 * g + j, j)
                for j in range(2):
                    fuse_f(2 * g + j, j)

        @block.scalar
        def _(act):
            A = act.activation
            pending = []

            def flush():
                while pending:
                    pending.pop(0)()

            def filter_slot(l, k):
                if k % 2 == 0:
                    return

                def later():
                    act.wait_ge(s["dve_div"], ITERS * l + k // 2 + 1)
                    if k < SLOTS - 1:
                        A(u[:, :, 0:IMG], fa, ACT.Tanh).then_inc(s["act_tanh"], 1)
                    else:
                        act.wait_ge(s["st_img"], 16 * l + 16)
                        A(f_out[:], fa, ACT.Copy, scale=2.0).then_inc(s["act_img"], 1)
                pending.append(later)

            def exps(l, i, n):
                act.wait_ge(s["dve_max"], 16 * l + 4 * i + n + 1)
                for hh in range(HALF):
                    last = A(prob[:, n % 2, hh], ps_s[n % 2][:, hh], ACT.Exp, bias=neg_max[:, n % 2, hh:hh + 1])
                last.then_inc(s["act_exp"], 1)

            def probs_out(l, i, n):
                act.wait_ge(s["pe_pT"], 16 * l + 4 * i + n + 1)
                A(probT[:].rearrange("p h k -> p (h k)"), t_flat, ACT.Copy).then_inc(s["act_pT"], 1)

            def part_a(l, i, slot):
                n = 4 * l + i + 1
                act.wait_ge(s["pe_hT"], n)
                A(hT[:].rearrange("p c n -> p (c n)"), ps_m[:], ACT.Copy).then_inc(s["act_hT"], 1)
                act.wait_ge(s["pe_q"], n)
                for odd in range(2):
                    last = A(qm[:, odd].rearrange("p c n -> p (c n)"), quad[0], ACT.Copy, scale=head_mask[:, odd:odd + 1])
                last.then_inc(s["act_q"], 1)
                act.wait_ge(s["pe_k"], n)
                A(kT[:].rearrange("p c n -> p (c n)"), quad[1], ACT.Copy).then_inc(s["act_k"], 1)
                act.wait_ge(s["pe_v"], n)
                for t in range(2):
                    last = A(v[:, t, :, 0:TKD], quad[2][:, D * t:D * t + D].rearrange("p (h k) -> p h k", h=TH), ACT.Copy)
                last.then_inc(s["act_v"], 1)
                flush()
                exps(l, i, 0)
                exps(l, i, 1)
                filter_slot(l, slot)
                probs_out(l, i, 0)
                flush()
                exps(l, i, 2)
                filter_slot(l, slot + 1)
                probs_out(l, i, 1)
                flush()
                exps(l, i, 3)
                filter_slot(l, slot + 2)
                probs_out(l, i, 2)
                probs_out(l, i, 3)
                flush()
                filter_slot(l, slot + 3)
                act.wait_ge(s["pe_oT"], n)
                A(attnT[:].rearrange("p c n -> p (c n)"), ps_m[:], ACT.Copy).then_inc(s["act_oT"], 1)

            def part_f(l, i, slot):
                n = 4 * l + i + 1
                act.wait_ge(s["l_bc"], 16 * l + 16)
                act.wait_ge(s["pe_h1T"], n)
                A(hT[:].rearrange("p c n -> p (c n)"), ps_m[:], ACT.Copy).then_inc(s["act_h1T"], 1)
                for m in range(MC):
                    if m % 2 == 0:
                        act.wait_ge(s["pe_ff1"], 16 * l + 4 * i + m // 2 + 1)
                    last = A(hidT[:, m], quad[m // 2][:, D * (m % 2):D * (m % 2) + D], ACT.Relu, bias=b1[:, m:m + 1])
                    if m % 2:
                        last.then_inc(s["act_ff1"], 1)
                flush()
                filter_slot(l, slot)

            act.wait_ge(s["c_general"], 1)
            with act.If(act.value_load(general[0:1, 0:1], min_val=0, max_val=1) > 0):
                own = gen_u[:, 1:3, 1:IMG + 1]

                def sigmoid(src, count):
                    act.wait_ge(s["gen_u_done"], count)
                    A(own, src, ACT.Tanh).then_inc(s["gen_tanh"], 1)
                    act.wait_ge(s["gen_tanh"], count)
                    A(own, own, ACT.Copy, scale=0.5, bias=0.5).then_inc(s["gen_u_done"], 1)

                act.wait_ge(s["gen_zero"], 1)
                with act.Fori(0, B) as b:
                    act.wait_ge(s["gen_o_in"], 16 * b + 16)
                    sigmoid(gen_o, (ITERS + 1) * b + 1)
                    with act.Fori(0, ITERS) as it:
                        act.wait_ge(s["gen_div"], ITERS * b + it + 1)
                        sigmoid(gen_w, (ITERS + 1) * b + it + 2)
                act.wait_ge(s["gen_out"], B)
                act.wait_ge(s["gen_st"], 16 * B)

            act.wait_ge(s["c_pool"], N_CONST)
            act.wait_ge(s["l_img"], 16 * 8)
            act.wait_ge(s["c_scaled"], 3)
            with act.Fori(0, LAYERS) as l:

                A(u[:, :, 0:IMG], o_all[:, bass.ds(l, 1)].rearrange("p a r c -> p (a r) c"), ACT.Tanh).then_inc(s["act_tanh"], 1)
                slot = 0
                for what, i in ORDER:
                    if what == "A":
                        part_a(l, i, slot)
                        slot += 4
                    else:
                        part_f(l, i, slot)
                        slot += 1
                flush()

            def tile_exps(n, t):
                act.wait_ge(s["f_max"], TT * n + t + 1)
                for hh in range(FH):
                    last = A(prob[:, t % 2, hh], ps_s[t % 2][:, hh], ACT.Exp, bias=neg_max[:, t % 2, hh:hh + 1])
                last.then_inc(s["f_exp"], 1)
                A(sink_e[:, t % 2], neg_max[:, t % 2], ACT.Exp, bias=sink[:]).then_inc(s["f_sink"], 1)

            def tile_probs(n, t):
                act.wait_ge(s["f_pT_ps"], TT * n + t + 1)
                A(probT[:].rearrange("p h k -> p (h k)"), t_flat, ACT.Copy).then_inc(s["f_pT"], 1)

            def halves(dst, n_sem, n, done):
                act.wait_ge(n_sem, n + 1)
                A(dst[0], ps_m[:, 0:TOK], ACT.Copy)
                A(dst[1], halo_flat[:, 0:TOK], ACT.Copy).then_inc(done, 1)

            def fuse_a(n, j):
                halves([xnT[:, c, WIN:] for c in range(KC)], s["f_xnT_ps"], n, s["f_xnT"])
                act.wait_ge(s["f_q_ps"], n + 1)
                for m in range(KC):
                    for r in range(4):
                        last = A(qz[:, r, m], quad[m][:, 0:TOK], ACT.Identity, scale=row_mask[:, r:r + 1], bias=bq_m[:, m, r:r + 1])
                last.then_inc(s["f_q"], 1)
                act.wait_ge(s["f_k_ps"], n + 1)
                for m in range(FKV):
                    last = A(kT_f[:, m, WIN:], quad[2 + m][:, 0:TOK], ACT.Identity, bias=bk_f[:, m:m + 1])
                last.then_inc(s["f_k"], 1)
                tile_exps(n, 0)
                tile_exps(n, 1)
                tile_probs(n, 0)
                tile_exps(n, 2)
                tile_probs(n, 1)
                tile_probs(n, 2)
                halves([attnT_f[:, c] for c in range(KC)], s["f_oT_ps"], n, s["f_oT"])

            def fuse_f(n):
                halves([xn2T[:, c] for c in range(KC)], s["f_xn2T_ps"], n, s["f_xn2T"])
                for m in range(MC):
                    act.wait_ge(s["f_h_ps"], MC * n + m + 1)
                    A(hid_f[:, m], quad[m % 4][:, 0:TOK], ACT.Relu).then_inc(s["f_relu"], 1)

            with act.Fori(0, B // 2) as g:
                for j in range(2):
                    fuse_a(2 * g + j, j)
                for j in range(2):
                    fuse_f(2 * g + j)

        @block.vector
        def _(dve):
            chain = [0]

            def tick(ins):
                chain[0] += 1
                ins.then_inc(s["chain"], 1)
                return chain[0]

            def link(ins):
                dve.wait_ge(s["chain"], tick(ins))

            def restart():
                dve.wait_ge(s["chain"], chain[0])
                dve.sem_clear(s["chain"])
                chain[0] = 0

            tt, ts, stt = dve.tensor_tensor, dve.tensor_scalar, dve.scalar_tensor_tensor

            for free in (s["dve_ff2"], s["dve_wc"], s["f_z"], s["f_y"]):
                dve.sem_inc(free, 1)
            for free in (s["st_img"], s["st_out"]):
                dve.sem_inc(free, 16)

            dve.wait_ge(s["l_tok"], 32)
            link(dve.tensor_copy(tok_f[:], tokens[:]))
            link(ts(tok_f[:], tok_f[:], float(-VOCAB), float(VOCAB - 1), ALU.max, ALU.min))
            link(ts(tok_neg[:], tok_f[:], 0.0, float(VOCAB), ALU.is_lt, ALU.mult))
            tt(tok_idx[:], tok_f[:], tok_neg[:], ALU.add).then_inc(s["c_idx"], 1)

            link(dve.memset(taps_std[:], 0.0))
            for at, val in ((4, -1.0), (7, 1.0), (13, -1.0), (14, 1.0), (19, -1.0), (22, 1.0), (30, -1.0), (31, 1.0)):
                link(dve.memset(taps_std[:, at:at + 1], val))
            dve.wait_ge(s["l_taps"], 32)
            link(tt(taps_diff[:], taps[:], taps_std[:], ALU.not_equal))
            link(dve.tensor_reduce(general_f[:], taps_diff[:], AX.X, ALU.max))
            dve.tensor_copy(general[:], general_f[:]).then_inc(s["c_general"], 1)
            dve.wait_ge(s["c_general"], 1)
            restart()
            with dve.If(dve.value_load(general[0:1, 0:1], min_val=0, max_val=1) > 0):
                def taps9(dst, src, at, more):
                    for k in range(9):
                        view = src[:, k // 3:k // 3 + 2, k % 3:k % 3 + IMG]
                        if k == 0 and not more:
                            link(ts(dst, view, taps[:, at:at + 1], None, ALU.mult))
                        else:
                            link(stt(dst, view, taps[:, at + k:at + k + 1], dst, ALU.mult, ALU.add))

                dve.sem_inc(s["gen_free"], 1)
                dve.sem_inc(s["gen_u_done"], 1)
                for t in (*gen_p, gen_u):
                    last = dve.memset(t, 0.0)
                    tick(last) if t is not gen_u else last.then_inc(s["gen_zero"], 1)
                dve.wait_ge(s["gen_zero"], 1)
                dve.wait_ge(s["gen_vf_in"], 32)
                restart()
                with dve.Fori(0, B) as b:
                    dve.wait_ge(s["gen_o_in"], 16 * b + 16)
                    link(dve.memset(gen_q, 0.0))
                    restart()
                    with dve.Fori(0, ITERS) as it:
                        n = ITERS * b + it + 1
                        dve.wait_ge(s["gen_halo_u"], 32 * n)
                        for k in range(2):
                            taps9(gen_g[k], gen_u, 9 * k, False)
                            link(tt(gen_g[k], gen_g[k], gen_vf[k], ALU.mult))
                        link(tt(gen_g[0], gen_g[0], gen_g[1], ALU.add))
                        link(stt(gen_q, gen_g[0], -0.5, gen_q, ALU.mult, ALU.add))
                        link(ts(gen_q, gen_q, 0.0, None, ALU.max))
                        tick(tt(gen_p[0][:, 1:3, 1:IMG + 1], gen_q, gen_vf[0], ALU.mult))
                        tt(gen_p[1][:, 1:3, 1:IMG + 1], gen_q, gen_vf[1], ALU.mult).then_inc(s["gen_flux"], 1)
                        dve.wait_ge(s["gen_halo_p"], 64 * n)
                        taps9(gen_t, gen_p[0], 18, False)
                        taps9(gen_t, gen_p[1], 27, True)
                        tt(gen_w, gen_o, gen_t, ALU.subtract).then_inc(s["gen_div"], 1)
                        restart()
                    dve.wait_ge(s["gen_u_done"], (ITERS + 1) * (b + 1) + 1)
                    ts(gen_w, gen_w, 2.0, None, ALU.mult).then_inc(s["gen_out"], 1)
                    dve.wait_ge(s["gen_st"], 16 * b + 16)
                    dve.sem_inc(s["gen_free"], 1)

            dve.wait_ge(s["l_img"], 16 * 8)
            link(ts(vq[:], vf[:], 0.25, None, ALU.mult))
            dve.wait_ge(s["c_pool"], N_CONST)
            for odd in range(2):
                hm = ident[:, :].rearrange("p (g o r) -> p g o r", o=2, r=TKD)[:, :, odd]
                tick(dve.tensor_reduce(head_mask[:, odd:odd + 1], hm, AX.XY, ALU.add))
            for r in range(4):
                tick(dve.tensor_reduce(row_mask[:, r:r + 1], ident[:, 32 * r:32 * r + 32], AX.X, ALU.add))
            dve.wait_ge(s["chain"], chain[0])
            link(ts(row_mask[:], row_mask[:], SCALE_F, None, ALU.mult))
            ts(head_mask[:], head_mask[:], SCALE_T, None, ALU.mult).then_inc(s["c_scaled"], 1)
            dve.wait_ge(s["l_fus"], 16 * 11)
            for m in range(KC):
                ts(bq_m[:, m], row_mask[:], bq_f[:, m:m + 1], None, ALU.mult).then_inc(s["c_scaled"], 1)
            dve.wait_ge(s["g_emb"], 16 * B)
            tt(h[:], h[:], pe[:].unsqueeze(1).to_broadcast([P, B, D]), ALU.add).then_inc(s["h_ready"], 4)
            dve.wait_ge(s["h_ready"], 4)

            def flux(l, k):
                dve.wait_ge(s["pe_halo"], SLOTS * l + k + 1)
                tt(fa[:, 0:RPP - 1], u[:, 1:RPP, 0:IMG], u[:, 0:RPP - 1, 0:IMG], ALU.subtract)
                ta = tick(tt(fa[:, RPP - 1], halo[:, 0], u[:, RPP - 1, 0:IMG], ALU.subtract))
                tb = tick(tt(fb, u[:, :, 1:], u[:, :, 0:IMG], ALU.subtract))
                dve.wait_ge(s["chain"], ta)
                tick(tt(fa, fa, vq[:, 0], ALU.mult))
                dve.wait_ge(s["chain"], tb)
                link(tt(fb, fb, vq[:, 1], ALU.mult))
                link(tt(fa, fa, fb, ALU.add))
                link(stt(q_st, q_st, 0.0, fa, ALU.max, ALU.subtract))
                stt(p1[:], q_st, 0.0, vf[:, 0], ALU.max, ALU.mult).then_inc(s["dve_flux"], 1)
                link(stt(p0[:, :, 1:], q_st, 0.0, vf[:, 1], ALU.max, ALU.mult))

            def divergence(l, k):
                dve.wait_ge(s["dve_flux"], ITERS * l + k // 2 + 1)
                dve.wait_ge(s["pe_halo"], SLOTS * l + k + 1)
                tick(tt(fa[:, 1:RPP], p1[:, 1:RPP], p1[:, 0:RPP - 1], ALU.subtract))
                link(tt(fa[:, 0], p1[:, 0], halo[:, 1], ALU.subtract))
                link(tt(fa, fa, p0[:, :, 1:], ALU.add))
                link(tt(fa, fa, p0[:, :, 0:IMG], ALU.subtract))
                tt(fa, o_all[:, bass.ds(l, 1)].rearrange("p a r c -> p (a r) c"), fa, ALU.subtract).then_inc(s["dve_div"], 1)

            def filter_slot(l, k):
                if k % 2 == 0:
                    flux(l, k)
                else:
                    divergence(l, k)

            def head_max(l, i, n):
                dve.wait_ge(s["pe_s"], 16 * l + 4 * i + n + 1)
                link(dve.tensor_reduce(rmax[:, n % 2], ps_s[n % 2][:], AX.X, ALU.max))
                ts(neg_max[:, n % 2], rmax[:, n % 2], -1.0, None, ALU.mult).then_inc(s["dve_max"], 1)

            def normalise(l, i, t):
                dve.wait_ge(s["pe_o"], 8 * l + 2 * i + t + 1)
                o = ps_m[:, 0:17 * TH].rearrange("p (h k) -> p h k", h=TH)
                link(dve.reciprocal(rden[:].unsqueeze(2), o[:, :, TKD:]))
                tt(attn[:, t].rearrange("p (h k) -> p h k", h=TH), o[:, :, 0:TKD], rden[:].unsqueeze(2).to_broadcast([P, TH, TKD]), ALU.mult).then_inc(s["dve_attn"], 1)

            def moments(src, n, done):
                for t in range(n):
                    tick(dve.bn_stats(stats[:, t], src[:, t]))
                dve.wait_ge(s["chain"], chain[0])
                for t in range(n):
                    last = dve.bn_aggr(mv[:, t], stats[:, t])
                    tick(last) if t < n - 1 else last.then_inc(done, 1)

            def text_residual(n, i, ps_in, add, freed):
                hp = h[:, 2 * i:2 * i + 2]
                wide = lambda r: vecs[:, r].unsqueeze(1).to_broadcast([P, 2, D])
                tt(hp, ps_in.rearrange("p (t n) -> p t n", t=2), hp, ALU.add).then_inc(freed, 1)
                dve.wait_ge(freed, n + 1)
                if add is not None:
                    link(tt(hp, hp, wide(add), ALU.add))
                return hp, wide

            def finish_norm(l, i, order, hp, wide, gain, bias, done):
                moments(hp, 2, s["dve_stat"])
                dve.wait_ge(s["dve_stat"], 8 * l + order)
                dve.wait_ge(s["pool_rstd"], 8 * l + order)
                for t in range(2):
                    tick(ts(hp[:, t], hp[:, t], mv[:, t, 0:1], rstd[:, t:t + 1], ALU.subtract, ALU.mult))
                dve.wait_ge(s["chain"], chain[0])
                link(tt(hp, hp, wide(gain), ALU.mult))
                tt(hp, hp, wide(bias), ALU.add).then_inc(done, 1)

            restart()
            with dve.Fori(0, LAYERS) as l:
                link(dve.memset(q_st, 0.0))
                slot = order = 0
                for what, i in ORDER:
                    n = 4 * l + i + 1
                    order += 1
                    if what == "A":
                        head_max(l, i, 0)
                        head_max(l, i, 1)
                        filter_slot(l, slot)
                        head_max(l, i, 2)
                        filter_slot(l, slot + 1)
                        normalise(l, i, 0)
                        head_max(l, i, 3)
                        filter_slot(l, slot + 2)
                        normalise(l, i, 1)
                        filter_slot(l, slot + 3)
                        slot += 4
                        dve.wait_ge(s["l_vec"], 16 * l + 16)
                        dve.wait_ge(s["pe_wc"], n)
                        hp, wide = text_residual(n, i, ps_t[:, 1], None, s["dve_wc"])
                        finish_norm(l, i, order, hp, wide, 0, 1, s["dve_ln1"])
                    else:
                        filter_slot(l, slot)
                        slot += 1
                        dve.wait_ge(s["pe_ff2"], n)
                        dve.wait_ge(s["dve_ln1"], n)
                        hp, wide = text_residual(n, i, ps_t[:, 0], 2, s["dve_ff2"])
                        finish_norm(l, i, order, hp, wide, 3, 4, s["h_ready"])
                restart()

            def joined_norm(n, src, dst, count, done):
                moments(src, TT, s["f_stat"])
                dve.wait_ge(s["f_stat"], count)
                dve.wait_ge(s["f_rstd"], count)
                for t in range(TT):
                    last = ts(dst[:, t], src[:, t], mv[:, t, 0:1], rstd[:, t:t + 1], ALU.subtract, ALU.mult)
                    tick(last) if t < TT - 1 else last.then_inc(done, 1)

            def tile_max(n, t):
                dve.wait_ge(s["f_s"], TT * n + t + 1)
                link(dve.tensor_reduce(rmax[:, t % 2], ps_s[t % 2][:], AX.X, ALU.max))
                ts(neg_max[:, t % 2], rmax[:, t % 2], sink[:], -1.0, ALU.max, ALU.mult).then_inc(s["f_max"], 1)

            def tile_normalise(n, t):
                dve.wait_ge(s["f_o"], TT * n + t + 1)
                dve.wait_ge(s["f_sink"], TT * n + t + 1)
                o = ps_m[:, 0:33 * FH].rearrange("p (h k) -> p h k", h=FH)
                link(tt(den[:].unsqueeze(2), o[:, :, HD:], sink_e[:, t % 2].unsqueeze(2), ALU.add))
                link(dve.reciprocal(rden_f[:], den[:]))
                tt(attn_f[:, t].rearrange("p (h k) -> p h k", h=FH), o[:, :, 0:HD], rden_f[:].unsqueeze(2).to_broadcast([P, FH, HD]), ALU.mult).then_inc(s["f_attn"], 1)

            def fuse_a(g, n, j):
                dve.wait_ge(l_x[j], 16 * g + 16)
                dve.wait_ge(s["st_out"], 32 * g + 16)
                ts(x[:, j, 2], h[:, bass.ds(n, 1)].rearrange("p a n -> p (a n)"), 1.0, None, ALU.mult).then_inc(s["f_xt"], 1)
                dve.wait_ge(s["f_xt"], n + 1)
                joined_norm(n, x[:, j], xn, 4 * g + 2 * j + 1, s["f_xn"])
                dve.wait_ge(s["f_v_ps"], n + 1)
                tt(v_f[:, :, :, 0:HD], ps_t[:, 0, 0:64 * 2 * TT].rearrange("p (w j k) -> p w j k", w=2 * TT, j=FKV),
                   bv_f[:].rearrange("p (j k) -> p j k", j=FKV).unsqueeze(1).to_broadcast([P, 2 * TT, FKV, HD]), ALU.add).then_inc(s["f_v"], 1)
                tile_max(n, 0)
                tile_max(n, 1)
                tile_normalise(n, 0)
                tile_max(n, 2)
                tile_normalise(n, 1)
                tile_normalise(n, 2)
                dve.wait_ge(s["f_y_ps"], n + 1)
                xj = x[:, j]
                tt(xj, t_flat[:, 0:TT * D].rearrange("p (t n) -> p t n", t=TT), xj, ALU.add).then_inc(s["f_y"], 1)
                dve.wait_ge(s["f_y"], n + 2)
                link(tt(xj, xj, bo_f[:].unsqueeze(1).to_broadcast([P, TT, D]), ALU.add))
                joined_norm(n, xj, xn2[:, j], 4 * g + 2 * j + 2, s["f_xn2"])

            def fuse_f(n, j):
                for m in range(MC):
                    dve.wait_ge(s["f_relu"], MC * n + m + 1)
                    tt(hid_f[:, m], hid_f[:, m], hid_f[:, m], ALU.mult).then_inc(s["f_sq"], 1)
                dve.wait_ge(s["f_z_ps"], n + 1)
                y = t_flat[:, 0:TT * D]
                flat = lambda a: a.rearrange("p t n -> p (t n)")
                xj = flat(x[:, j])
                tick(dve.tensor_copy(mem, y))
                link(ts(spikes, y, 1.0, None, ALU.is_gt))
                for step in range(1, STEPS):
                    last = stt(mem_t, mem, 0.9, y, ALU.mult, ALU.add)
                    if step == STEPS - 1:
                        last.then_inc(s["f_z"], 1)
                        dve.wait_ge(s["f_z"], n + 2)
                    else:
                        link(last)
                    link(stt(mem, mem, 1.0, mem_t, ALU.is_gt, ALU.subtract, reverse1=True))
                    link(stt(spikes, mem, 1.0, spikes, ALU.is_gt, ALU.add))
                stt(xj, spikes, 1.0 / STEPS, xj, ALU.mult, ALU.add).then_inc(s["f_out"], 1)

            with dve.Fori(0, B // 2) as g:
                for j in range(2):
                    fuse_a(g, 2 * g + j, j)
                for j in range(2):
                    fuse_f(2 * g + j, j)
                restart()


def kernel(**inputs):
    import numpy as np
    import concourse.bacc as _bacc
    from concourse import mybir as _mybir
    from concourse.bass_utils import run_bass_kernel_spmd as _run

    I = {k: np.asarray(v) for k, v in inputs.items()}

    def chunks(w):
        return np.ascontiguousarray(np.swapaxes(w.reshape(*w.shape[:-2], -1, P, w.shape[-1]), -3, -2))

    t = {n: I["L0_txt_" + n] for n in ("Wq", "Wk", "Wv", "Wc", "W1", "b1", "W2", "b2", "g1", "be1", "g2", "be2")}
    a = {n: I["L0_attn_" + n] for n in ("Wq", "bq", "Wk", "bk", "Wv", "bv", "Wo", "bo")}
    pos = np.arange(SEQ, dtype=np.float32)[:, None]
    div = np.exp(np.arange(0, D, 2, dtype=np.float32) * np.float32(-np.log(np.float32(10000.0)) / np.float32(D)))
    pe = np.zeros((SEQ, D), np.float32)
    pe[:, 0::2], pe[:, 1::2] = np.sin(pos * div), np.cos(pos * div)
    wk4 = np.stack([np.concatenate([a["Wk"][HD * j:HD * j + HD]] * 4, 0) for j in range(FKV)], 0).reshape(FKV * P, D).T
    arrays = {
        "o": I["x"].reshape(B, IMG, IMG),
        "tokens": I["x_txt"].T,
        "vf": np.transpose(I["L0_tok_vector_field"], (2, 0, 1))[::-1],
        "nabla_w": I["L0_tok_nabla_w"].reshape(18),
        "div_w": I["L0_tok_div_w"].reshape(18),
        "pe": pe,
        "emb": I["L0_txt_emb"],
        "w_attn": chunks(np.concatenate([t["Wq"], t["Wk"], t["Wv"], t["Wc"]], -1)),
        "w1": chunks(t["W1"]),
        "w2": chunks(t["W2"]),
        "vecs": np.stack([t["g1"], t["be1"], t["b2"], t["g2"], t["be2"]], 1),
        "b1": np.transpose(t["b1"].reshape(LAYERS, MC, P), (0, 2, 1)),
        "wq_f": chunks(a["Wq"].T),
        "wk_f": chunks(wk4).reshape(P, KC, FKV, P),
        "wv_f": chunks(a["Wv"].T),
        "wo_f": chunks(a["Wo"].T),
        "w_fc": chunks(I["L0_ffn_W_fc"].T),
        "w_pr": chunks(I["L0_ffn_W_proj"].T),
        "bq_f": a["bq"].reshape(KC, P).T,
        "bk_f": np.tile(a["bk"].reshape(FKV, HD), (1, 4)).T,
        "bv_f": a["bv"],
        "bo_f": a["bo"],
        "sink": I["L0_attn_sink_bias"].reshape(1),
    }
    nc = _bacc.Bacc("TRN2", target_bir_lowering=False, num_devices=1)
    feeds, d = {}, {}
    for name, arr in arrays.items():
        arr = np.ascontiguousarray(arr)
        feeds["in_" + name] = arr
        d[name] = nc.dram_tensor("in_" + name, arr.shape, _mybir.dt.from_np(arr.dtype), kind="ExternalInput").ap()
    out = nc.dram_tensor("out", (B, TOK, D), F32, kind="ExternalOutput").ap()
    build(nc, d, out)
    r = _run(nc, [feeds], core_ids=[0])
    return r.results[0]["out"]
```

```python
from contextlib import ExitStack

import concourse.bass as bass
from concourse import mybir

F32 = mybir.dt.float32
BF16 = mybir.dt.bfloat16
I32 = mybir.dt.int32
U32 = mybir.dt.uint32
ALU = mybir.AluOpType
ACT = mybir.ActivationFunctionType
AX = mybir.AxisListType

P = 128
B, IMG = 8, 256
D, KC = 256, 2
SEQ = 128
VOCAB = 8000
LAYERS, TH, TKD, M = 4, 16, 16, 1024
MC = M // P
TOK = IMG + SEQ
TT = TOK // P
WIN, FH, FKV, HD = 64, 8, 2, 32
EPS = 1e-5
ITERS = 10
PAIRS = B // 2
RPP = IMG // 64
SLOTS = 2 * ITERS
HALF = 8
MASKED = -65536.0
STEPS = 5
SCALE_T = float(TKD) ** -0.5
SCALE_F = float(HD) ** -0.5
ORDER = [("A", 0), ("A", 1), ("F", 0), ("A", 2), ("F", 1), ("A", 3), ("F", 2), ("F", 3)]
SLOTS_IN = {"A": 3, "F": 2}


def build(nc, d, out):
    with ExitStack() as ctx:
        def sb(name, shape, dt=F32):
            return ctx.enter_context(nc.sbuf_tensor(name, shape, dt))

        def ps(name, shape, dt=F32):
            return ctx.enter_context(nc.psum_tensor(name, shape, dt))

        def sem(name):
            return ctx.enter_context(nc.semaphore(name))

        filtered = nc.dram_tensor("filtered", (2, B, IMG, IMG), F32, kind="Internal").ap()

        ident = sb("ident", [P, P])
        ident_h = sb("ident_h", [P, P], BF16)
        up_shift = sb("up_shift", [P, P])
        down_shift = sb("down_shift", [P, P])
        edge = sb("edge", [1, P])
        ones = sb("ones", [P, 4 * P])
        mask = sb("mask", [P, 2, 4, P], BF16)
        head_mask = sb("head_mask", [P, HALF])
        ones_pad = sb("ones_pad", [P, 2, 2 * TKD])
        pow_half = sb("pow_half", [P, 4])
        row_mask = sb("row_mask", [P, 4])
        bq_m = sb("bq_m", [P, KC, 4])
        eps_c = sb("eps_c", [P, 4])
        pe = sb("pe", [P, D])
        taps = sb("taps", [P, 36])
        taps_std = sb("taps_std", [P, 36])
        taps_diff = sb("taps_diff", [P, 36])
        general_f = sb("general_f", [P, 1])
        general = sb("general", [P, 1], I32)

        tokens = sb("tokens", [P, B], I32)
        tok_f = sb("tok_f", [P, B])
        tok_neg = sb("tok_neg", [P, B])
        tok_idx = sb("tok_idx", [P, B], U32)
        h = sb("h", [P, B, D])
        w_attn = sb("w_attn", [P, KC, 4 * D])
        w1 = sb("w1", [P, KC, M])
        w2 = sb("w2", [P, MC, D])
        vecs = sb("vecs", [P, 5, D])
        b1 = sb("b1", [P, MC])
        hT = sb("hT", [P, KC, D])
        qT = sb("qT", [P, KC, D])
        km_all = sb("km", [P, KC * 2 * HALF * P])
        km = km_all[:].rearrange("p (g t h k) -> p g t h k", g=KC, t=2, h=HALF)
        v = sb("v", [P, 2, TH, 2 * TKD])
        prob = sb("prob", [P, 2, HALF, P])
        probT = sb("probT", [P, HALF, P])
        neg_max = sb("neg_max", [P, TT, HALF])
        rden = sb("rden", [P, 2, KC, P])
        attnT = sb("attnT", [P, KC, D])
        hidT = sb("hidT", [P, MC, D])
        stats = sb("stats", [P, TT, 6])
        mv = sb("mv", [P, TT, 2])
        var_eps = sb("var_eps", [P, TT])
        rstd = sb("rstd", [P, TT])

        o_all = sb("o_all", [P, PAIRS, RPP, IMG])
        vf = sb("vf", [P, 2, RPP, IMG])
        vq = sb("vq", [P, 2, RPP, IMG])
        u = sb("u", [P, RPP, IMG + 1])
        f3 = sb("f3", [P, 3, RPP, IMG])
        fa, fb, q_st = f3[:, 0], f3[:, 1], f3[:, 2]
        p1 = sb("p1", [P, RPP, IMG])
        p0 = sb("p0", [P, RPP, IMG + 1])
        f_out = sb("f_out", [P, RPP, IMG])

        wq_f = sb("wq_f", [P, KC, D])
        wk_f = sb("wk_f", [P, KC, FKV, P])
        wv_f = sb("wv_f", [P, KC, FKV * HD])
        wo_f = sb("wo_f", [P, KC, D])
        w_fc = sb("w_fc", [P, KC, M])
        w_pr = sb("w_pr", [P, MC, D])
        bq_f = sb("bq_f", [P, KC])
        bk_f = sb("bk_f", [P, FKV])
        bv_f = sb("bv_f", [P, FKV * HD])
        bo_f = sb("bo_f", [P, D])
        sink = sb("sink", [P, 1])
        x = sb("x", [P, 2, TT, D])
        km_as = lambda k: km_all[:, k * TT * D:(k + 1) * TT * D]
        xn = km_as(0).rearrange("p (t n) -> p t n", t=TT)
        attn_f = km_as(1).rearrange("p (t n) -> p t n", t=TT)
        attnT_f = km_as(2).rearrange("p (c n) -> p c n", c=KC)
        xn2T = km_as(3).rearrange("p (c n) -> p c n", c=KC)
        xnT = sb("xnT", [P, KC, WIN + TOK])
        kT_f = sb("kT_f", [P, FKV, WIN + TOK])
        v_f = sb("v_f", [P, 2 * TT, FKV, HD + 1])
        sink_e = sb("sink_e", [P, TT, FH])
        rmax = sb("rmax", [P, 2, FH])
        den = sb("den", [P, FH])
        rden_f = sb("rden_f", [P, FH])
        xn2 = sb("xn2", [P, 2, TT, D])
        hid_f = o_all[:, :, :, :].rearrange("p a r c -> p (a r c)")[:, 0:MC * TOK].rearrange("p (m t) -> p m t", m=MC)
        qz = f3[:, :, :, :].rearrange("p a r c -> p (a r c)")[:, 0:4 * KC * TOK].rearrange("p (r c t) -> p r c t", r=4, c=KC)
        spare = vf[:, :, :, :].rearrange("p a r c -> p (a r c)")
        spare2 = vq[:, :, :, :].rearrange("p a r c -> p (a r c)")
        mem = spare[:, 0:TT * D]
        mem_t = spare[:, TT * D:2 * TT * D]
        spikes = spare2[:, 0:TT * D]
        res = w2[:].rearrange("p m n -> p (m n)")[:, 0:2 * TT * D].rearrange("p (j t n) -> p j t n", j=2, t=TT)
        y_in = w_attn[:].rearrange("p c n -> p (c n)")[:, 0:2 * TT * D].rearrange("p (j n) -> p j n", j=2)

        def ringed(t):
            return t[:, 0:4 * (IMG + 2)].rearrange("p (r c) -> p r c", r=4)

        gen_u = ringed(x[:].rearrange("p a t n -> p (a t n)"))
        gen_p = [ringed(xn2[:].rearrange("p a t n -> p (a t n)")), ringed(prob[:].rearrange("p a h k -> p (a h k)"))]
        rows2 = lambda t: t.rearrange("p (r c) -> p r c", r=2)
        hid_flat = hidT[:].rearrange("p m n -> p (m n)")
        gen_vf = [rows2(hid_flat[:, 512 * k:512 * k + 512]) for k in range(2)]
        gen_q, gen_t = rows2(hid_flat[:, 1024:1536]), rows2(hid_flat[:, 1536:2048])
        gen_g = [rows2(km_all[:, 512 * k:512 * k + 512]) for k in range(2)]
        probT_flat = probT[:].rearrange("p h k -> p (h k)")
        gen_o, gen_w = rows2(probT_flat[:, 0:512]), rows2(probT_flat[:, 512:1024])

        halo = ps("halo", [P, 2, IMG])
        ps_s = [ps(f"ps_s{i}", [P, HALF, P]) for i in range(2)]
        ps_t = ps("ps_t", [P, 2, 512])
        ps_m = ps("ps_m", [P, 512])
        s_flat = [t[:, :, :].rearrange("p h k -> p (h k)") for t in ps_s]
        quad = [s_flat[0][:, 0:512], s_flat[0][:, 512:1024], s_flat[1][:, 0:512], s_flat[1][:, 512:1024]]
        sums = [ps_m, quad[0]]
        t_flat = ps_t[:, :, :].rearrange("p a n -> p (a n)")
        t_heads = t_flat.rearrange("p (h k) -> p h k", h=HALF)
        halo_flat = halo[:, :, :].rearrange("p a n -> p (a n)")

        names = [
            "l_vec", "l_attn", "l_w1", "l_w2", "l_bc", "l_tok", "l_img", "l_fus", "st_img", "st_out", "g_emb",
            "l_taps",
            "c_pool", "c_scaled", "c_idx", "c_general",
            "pe_hT", "pe_q", "pe_k", "pe_v", "pe_s", "pe_pT", "pe_o", "pe_wc", "pe_ff1", "pe_ff2",
            "act_hT", "act_q", "act_k", "act_v", "act_exp", "act_pT", "act_ff1",
            "dve_max", "dve_attn", "dve_wc", "dve_ln1", "dve_ff2", "h_ready", "dve_stat", "pool_rstd", "pool_eps",
            "pe_halo", "act_tanh", "act_img", "dve_flux", "dve_div",
            "f_xt", "f_xnT_ps", "f_xnT", "f_q_ps", "f_q", "f_k_ps", "f_k", "f_v_ps", "f_v", "f_s", "f_max", "f_exp", "f_sink",
            "f_pT_ps", "f_pT", "f_o", "f_attn", "f_oT_ps", "f_oT", "f_y_ps", "f_y", "f_xn", "f_xn2", "f_xn2T_ps", "f_xn2T",
            "f_h_ps", "f_relu", "f_sq", "f_z_ps", "f_z", "f_out", "f_stat", "f_rstd", "f_eps",
            "chain",
            "gen_vf_in", "gen_free", "gen_o_in", "gen_tanh", "gen_u_done", "gen_halo_u", "gen_flux", "gen_halo_p", "gen_div",
            "gen_out", "gen_st", "gen_zero",
        ]
        s = {n: sem(n) for n in names}

        l_x = [sem(f"l_x{j}") for j in range(2)]

        block = ctx.enter_context(nc.Block())

        @block.sync
        def _(sp):
            sp.dma_start(taps[:, 0:18], d["nabla_w"].partition_broadcast(P)).then_inc(s["l_taps"], 16)
            sp.dma_start(taps[:, 18:36], d["div_w"].partition_broadcast(P)).then_inc(s["l_taps"], 16)
            sp.dma_start(tokens[:], d["tokens"]).then_inc(s["l_tok"], 16)
            sp.dma_start(pe[:], d["pe"]).then_inc(s["l_tok"], 16)
            for img in range(2):
                for comp in range(2):
                    sp.dma_start(vf[64 * img:64 * img + 64, comp], d["vf"][comp].rearrange("(p r) c -> p r c", r=RPP)).then_inc(s["l_img"], 16)
            for pair in range(PAIRS):
                sp.dma_start(o_all[:, pair], d["o"][2 * pair:2 * pair + 2].rearrange("b (p r) c -> (b p) r c", r=RPP)).then_inc(s["l_img"], 16)
            sp.dma_start(w_attn[:], d["w_attn"][0]).then_inc(s["l_attn"], 16)
            sp.dma_start(b1[:], d["b1"][0]).then_inc(s["l_bc"], 16)
            sp.dma_start(vecs[:], d["vecs"][0].partition_broadcast(P)).then_inc(s["l_vec"], 16)
            sp.dma_start(w1[:], d["w1"][0]).then_inc(s["l_w1"], 16)
            sp.dma_start(w2[:], d["w2"][0]).then_inc(s["l_w2"], 16)
            for t, n in ((wq_f, "wq_f"), (wk_f, "wk_f"), (wv_f, "wv_f"), (wo_f, "wo_f"), (w_fc, "w_fc"), (w_pr, "w_pr"), (bq_f, "bq_f"), (bk_f, "bk_f")):
                sp.dma_start(t[:], d[n]).then_inc(s["l_fus"], 16)
            for t, n in ((bv_f, "bv_f"), (bo_f, "bo_f"), (sink, "sink")):
                sp.dma_start(t[:], d[n].partition_broadcast(P)).then_inc(s["l_fus"], 16)

            sp.wait_ge(s["c_general"], 1)
            which = sp.value_load(general[0:1, 0:1], min_val=0, max_val=1)
            with sp.If(which > 0):
                for k in range(2):
                    sp.dma_start(gen_vf[k], d["vf"][k].rearrange("(p r) c -> p r c", r=2)).then_inc(s["gen_vf_in"], 16)

                def ring_rows(t, done):
                    sp.dma_start(t[1:P, 0], t[0:P - 1, 2]).then_inc(done, 16)
                    sp.dma_start(t[0:P - 1, 3], t[1:P, 1]).then_inc(done, 16)

                with sp.Fori(0, B) as b:
                    sp.wait_ge(s["gen_free"], b + 1)
                    sp.dma_start(gen_o, d["o"][bass.ds(b, 1)].rearrange("b (p r) c -> p (b r) c", r=2)).then_inc(s["gen_o_in"], 16)
                    with sp.Fori(0, ITERS) as it:
                        sp.wait_ge(s["gen_u_done"], (ITERS + 1) * b + it + 2)
                        ring_rows(gen_u, s["gen_halo_u"])
                        sp.wait_ge(s["gen_flux"], ITERS * b + it + 1)
                        for k in range(2):
                            ring_rows(gen_p[k], s["gen_halo_p"])
                    sp.wait_ge(s["gen_out"], b + 1)
                    sp.dma_start(filtered[1][bass.ds(b, 1)].rearrange("b (p r) c -> p (b r) c", r=2), gen_w).then_inc(s["gen_st"], 16)
                sp.wait_ge(s["gen_st"], 16 * B)

            def store_pair(l):
                sp.wait_ge(s["act_img"], l + 1)
                dst = filtered[0].rearrange("(a b) (p r) c -> a (b p) r c", b=2, r=RPP)
                dst = dst[l] if isinstance(l, int) else dst[bass.ds(l, 1)].rearrange("a p r c -> p (a r) c")
                sp.dma_start(dst, f_out[:]).then_inc(s["st_img"], 16)

            with sp.Fori(0, LAYERS - 1) as l:
                sp.wait_ge(s["pe_wc"], 4 * l + 4)
                sp.dma_start(w_attn[:], d["w_attn"][bass.ds(l + 1, 1)].rearrange("a p c n -> p (a c) n")).then_inc(s["l_attn"], 16)
                sp.wait_ge(s["pe_ff1"], 16 * l + 16)
                sp.dma_start(w1[:], d["w1"][bass.ds(l + 1, 1)].rearrange("a p c n -> p (a c) n")).then_inc(s["l_w1"], 16)
                sp.wait_ge(s["pe_ff2"], 4 * l + 4)
                sp.dma_start(w2[:], d["w2"][bass.ds(l + 1, 1)].rearrange("a p c n -> p (a c) n")).then_inc(s["l_w2"], 16)
                sp.wait_ge(s["h_ready"], 4 * l + 8)
                sp.dma_start(vecs[:], d["vecs"][bass.ds(l + 1, 1)].partition_broadcast(P).rearrange("p a v n -> p (a v) n")).then_inc(s["l_vec"], 16)
                sp.wait_ge(s["act_ff1"], 16 * l + 16)
                sp.dma_start(b1[:], d["b1"][bass.ds(l + 1, 1)].rearrange("a p m -> p (a m)")).then_inc(s["l_bc"], 16)
                store_pair(l)
            store_pair(LAYERS - 1)

            sp.wait_ge(s["st_img"], 16 * PAIRS + 16)
            out_v = out.rearrange("b (t p) n -> b p t n", p=P)

            def load_x(b, j):
                src = filtered[bass.ds(which, 1), bass.ds(b, 1)].rearrange("w b (t p) c -> p (w b t) c", p=P)
                sp.dma_start(x[:, j, 0:2], src).then_inc(l_x[j], 16)

            def store(b, j):
                sp.wait_ge(s["f_out"], b + 3)
                sp.dma_start(out_v[bass.ds(b, 1)].rearrange("b p t n -> p (b t) n"), res[:, j]).then_inc(s["st_out"], 16)

            for j in range(2):
                load_x(j, j)
            with sp.Fori(0, B // 2 - 1) as g:
                for j in range(2):
                    sp.wait_ge(s["f_y"], 2 * g + j + 2)
                    load_x(2 * g + 2 + j, j)
                for j in range(2):
                    store(2 * g + j, j)
            for j in range(2):
                store(B - 2 + j, j)
            sp.wait_ge(s["st_out"], 16 * B + 16)

        @block.gpsimd
        def _(pool):
            c = 0
            def const(ins):
                nonlocal c
                ins.then_inc(s["c_pool"], 1)
                c += 1
                pool.wait_ge(s["c_pool"], c)
            const(pool.memset(ones[:], 1.0))
            const(pool.memset(mask[:], 0.0))
            const(pool.affine_select(out=ident[:], in_=ones[:, 0:P], compare_op=ALU.is_equal, fill=0.0, base=0, pattern=[[-1, P]], channel_multiplier=1))
            const(pool.tensor_copy(ident_h[:], ident[:]))
            const(pool.affine_select(out=up_shift[:], in_=ones[:, 0:P], compare_op=ALU.is_equal, fill=0.0, base=-1, pattern=[[-1, P]], channel_multiplier=1))
            const(pool.affine_select(out=down_shift[:], in_=ones[:, 0:P], compare_op=ALU.is_equal, fill=0.0, base=1, pattern=[[-1, P]], channel_multiplier=1))
            const(pool.memset(up_shift[:, 63:64], 0.0))
            const(pool.memset(down_shift[:, 64:65], 0.0))
            const(pool.memset(edge[:], 0.0))
            const(pool.memset(edge[:, 63:64], -1.0))
            const(pool.memset(edge[:, 127:128], -1.0))
            const(pool.memset(pow_half[:], -0.5))
            const(pool.memset(eps_c[:], EPS))
            for first in range(2):
                for half in range(2):
                    m = mask[64 * half:64 * half + 64, first]
                    const(pool.affine_select(out=m, in_=m, compare_op=ALU.is_gt, fill=MASKED, base=0, pattern=[[0, 4], [1, P]], channel_multiplier=-1))
                    const(pool.affine_select(out=m, in_=m, compare_op=ALU.is_ge, fill=MASKED, base=WIN, pattern=[[0, 4], [-1, P]], channel_multiplier=1))
                    if first and half == 0:
                        const(pool.affine_select(out=m, in_=m, compare_op=ALU.is_ge, fill=MASKED, base=-WIN, pattern=[[0, 4], [1, P]], channel_multiplier=0))
            const(pool.memset(v_f[:, :, :, HD:], 1.0))
            const(pool.memset(v[:], 0.0))
            const(pool.memset(ones_pad[:], 0.0))
            for o in range(2):
                const(pool.memset(ones_pad[:, o, TKD * o:TKD * o + TKD], 1.0))
            for t in (xnT[:, :, 0:WIN], kT_f[:, :, 0:WIN], p0[:, :, 0:1]):
                const(pool.memset(t, 0.0))
            const(pool.memset(u[:, :, IMG:], -1.0))

            pool.wait_ge(s["c_idx"], 1)
            for b in range(B):
                pool.indirect_dma_start(h[:, b, :], None, d["emb"], bass.IndirectOffsetOnAxis(ap=tok_idx[:, b:b + 1], axis=0)).then_inc(s["g_emb"], 16)

            with pool.Fori(0, 2 * LAYERS * PAIRS) as n:
                pool.wait_ge(s["dve_stat"], n + 1)
                pool.tensor_tensor(var_eps[:, 0:2], mv[:, 0:2, 1], eps_c[:, 0:2], ALU.add).then_inc(s["pool_eps"], 1)
                pool.wait_ge(s["pool_eps"], n + 1)
                pool.tensor_tensor(rstd[:, 0:2], var_eps[:, 0:2], pow_half[:, 0:2], ALU.pow).then_inc(s["pool_rstd"], 1)
            with pool.Fori(0, 2 * B) as n:
                pool.wait_ge(s["f_stat"], n + 1)
                pool.tensor_tensor(var_eps[:], mv[:, :, 1], eps_c[:, 0:TT], ALU.add).then_inc(s["f_eps"], 1)
                pool.wait_ge(s["f_eps"], n + 1)
                pool.tensor_tensor(rstd[:], var_eps[:], pow_half[:, 0:TT], ALU.pow).then_inc(s["f_rstd"], 1)

        N_CONST = 13 + 9 + 5 + 3 + 1

        @block.tensor
        def _(pe_):
            mm, tr = pe_.matmul, pe_.transpose

            def filter_slot(l, k):
                if k % 2 == 0:
                    pe_.wait_ge(s["act_tanh"], ITERS * l + k // 2 + 1)
                    mm(halo[:, 0], up_shift[:], u[:, 0, 0:IMG], start=True, stop=False)
                    mm(halo[:, 0], edge[:], ones[0:1, 0:IMG], start=False, stop=True).then_inc(s["pe_halo"], 1)
                else:
                    pe_.wait_ge(s["dve_flux"], ITERS * l + k // 2 + 1)
                    mm(halo[:, 1], down_shift[:], p1[:, RPP - 1], start=True, stop=True).then_inc(s["pe_halo"], 1)

            def turn_h(l, place, bank):
                what, i = ORDER[place]
                pe_.wait_ge(s["h_ready"] if what == "A" else s["dve_ln1"], 4 * l + i + 1)
                for t in range(2):
                    for c in range(KC):
                        last = tr(bank[:, D * c + P * t:D * c + P * t + P], h[:, 2 * i + t, P * c:P * c + P], ident[:])
                last.then_inc(s["pe_hT"], 1)

            def scores(l, i, n):
                t, g = n // 2, n % 2
                if n == 0:
                    pe_.wait_ge(s["act_q"], 4 * l + i + 1)
                if n == 1:
                    pe_.wait_ge(s["act_v"], 4 * l + i + 1)
                if n < 2:
                    pe_.wait_ge(s["act_k"], 8 * l + 2 * i + g + 1)
                for half in range(2):
                    last = mm(ps_s[g][:, 4 * half:4 * half + 4].rearrange("p h k -> p (h k)"), qT[:, g, P * t:P * t + P],
                              km[:, g, t, 4 * half:4 * half + 4].rearrange("p h k -> p (h k)"), start=True, stop=True)
                last.then_inc(s["pe_s"], 1)

            def turn_probs(l, i, n, done):
                pe_.wait_ge(s["act_exp"], 16 * l + 4 * i + n + 1)
                if n == 0:
                    pe_.wait_ge(s["dve_ff2"], 4 * l + done + 1)
                    pe_.wait_ge(s["dve_wc"], 4 * l + i + 1)
                for hh in range(HALF):
                    last = tr(t_heads[:, hh], prob[:, n % 2, hh], ident[:])
                last.then_inc(s["pe_pT"], 1)

            def attend(l, i, n):
                t, g = n // 2, n % 2
                pe_.wait_ge(s["act_pT"], 16 * l + 4 * i + n + 1)
                for den in range(2):
                    for o in range(2):
                        for j in range(4):
                            hh = 2 * j + o
                            w = ones_pad[:, o] if den else v[:, t, HALF * g + hh]
                            last = mm(sums[t][32 * j:32 * j + 32, D * den + P * g:D * den + P * g + P], w, probT[:, hh],
                                      start=(o == 0), stop=(o == 1), skip_group_check=True)
                if g == 1:
                    last.then_inc(s["pe_o"], 1)

            def project(dst, w, m):
                for c in range(KC):
                    last = mm(dst, w_attn[:, c, D * w + P * m:D * w + P * m + P], hT[:, c], start=(c == 0), stop=(c == KC - 1))
                return last

            def ff1(l, i, ms):
                for m in ms:
                    for c in range(KC):
                        last = mm(quad[(m // 2 + 1) % 4][:, D * (m % 2):D * (m % 2) + D], w1[:, c, P * m:P * m + P], hT[:, c], start=(c == 0), stop=(c == KC - 1))
                    if m % 2:
                        last.then_inc(s["pe_ff1"], 1)

            def head(l, place):
                what, i = ORDER[place]
                pe_.wait_ge(s["act_hT"], 8 * l + place + 1)
                if what == "A":
                    if i == 0:
                        pe_.wait_ge(s["l_attn"], 16 * l + 16)
                    project(quad[2][:, 0:D], 1, 0).then_inc(s["pe_k"], 1)
                    project(quad[1][:, 0:D], 0, 0)
                    project(quad[1][:, D:2 * D], 0, 1).then_inc(s["pe_q"], 1)
                else:
                    if i == 0:
                        pe_.wait_ge(s["l_w1"], 16 * l + 16)
                    ff1(l, i, range(4))

            def part_a(l, i, place, done, slot, after_f):
                if place == 0 or after_f:
                    head(l, place)
                if after_f:
                    filter_slot(l, slot)
                project(quad[3][:, 0:D], 1, 1).then_inc(s["pe_k"], 1)
                for t in range(2):
                    for c in range(KC):
                        last = mm(quad[0][:, D * t:D * t + D], hT[:, c, P * t:P * t + P], w_attn[:, c, 2 * D:3 * D], start=(c == 0), stop=(c == KC - 1))
                last.then_inc(s["pe_v"], 1)
                pe_.wait_ge(s["act_v"], 4 * l + i + 1)
                scores(l, i, 0)
                scores(l, i, 1)
                filter_slot(l, slot + 1)
                turn_probs(l, i, 0, done)
                scores(l, i, 2)
                attend(l, i, 0)
                turn_probs(l, i, 1, done)
                scores(l, i, 3)
                attend(l, i, 1)
                filter_slot(l, slot + 2)
                turn_probs(l, i, 2, done)
                attend(l, i, 2)
                turn_probs(l, i, 3, done)
                turn_h(l, place + 1, quad[3])
                attend(l, i, 3)
                filter_slot(l, slot + 3)
                head(l, place + 1)
                pe_.wait_ge(s["dve_attn"], 8 * l + 2 * i + 2)
                for t in range(2):
                    for c in range(KC):
                        last = mm(ps_t[:, 1, D * t:D * t + D], attnT[:, c, P * t:P * t + P], w_attn[:, c, 3 * D:4 * D], start=(c == 0), stop=(c == KC - 1))
                last.then_inc(s["pe_wc"], 1)

            def part_f(l, i, place, slot, after_f):
                if after_f:
                    head(l, place)
                    filter_slot(l, slot)
                ff1(l, i, range(4, MC))
                filter_slot(l, slot + 1)
                if place + 1 < len(ORDER):
                    turn_h(l, place + 1, ps_m)
                if i == 0:
                    pe_.wait_ge(s["l_w2"], 16 * l + 16)
                pe_.wait_ge(s["dve_ff2"], 4 * l + i + 1)
                for t in range(2):
                    for m in range(MC):
                        if t == 0 and m % 2 == 0:
                            pe_.wait_ge(s["act_ff1"], 16 * l + 4 * i + m // 2 + 1)
                        last = mm(ps_t[:, 0, D * t:D * t + D], hidT[:, m, P * t:P * t + P], w2[:, m], start=(m == 0), stop=(m == MC - 1))
                last.then_inc(s["pe_ff2"], 1)

            pe_.wait_ge(s["c_pool"], N_CONST)
            with pe_.Fori(0, LAYERS) as l:
                turn_h(l, 0, ps_m)
                filter_slot(l, 0)
                slot = done = 0
                for place, (what, i) in enumerate(ORDER):
                    after_f = place > 0 and ORDER[place - 1][0] == "F"
                    if what == "A":
                        part_a(l, i, place, done, slot, after_f)
                    else:
                        part_f(l, i, place, slot, after_f)
                        done += 1
                    slot += SLOTS_IN[what]

            def tile_scores(n, t):
                bank = ps_s[t % 2]
                if t == 2:
                    pe_.wait_ge(s["f_exp"], TT * n + 1)
                m = mask[:, 1 if t == 0 else 0].rearrange("p a k -> p (a k)")
                for hb in range(2):
                    flat = bank[:, 4 * hb:4 * hb + 4].rearrange("p h k -> p (h k)")
                    mm(flat, ident_h[:], m, start=True, stop=False, skip_group_check=True)
                    for hh in range(4 * hb, 4 * hb + 4):
                        r, c = hh % 4, hh // 4
                        for half in range(2):
                            at = P * t + WIN * half
                            last = mm(bank[WIN * half:WIN * half + WIN, hh], qz[:, r, c, at:at + WIN], kT_f[:, c, at:at + P],
                                      start=False, stop=(hh % 4 == 3), skip_group_check=True)
                last.then_inc(s["f_s"], 1)

            def tile_turn(n, t):
                pe_.wait_ge(s["f_exp"], TT * n + t + 1)
                if t == 0:
                    pe_.wait_ge(s["f_v"], n + 1)
                for hh in range(FH):
                    last = tr(t_heads[:, hh], prob[:, t % 2, hh], ident[:])
                last.then_inc(s["f_pT_ps"], 1)

            def tile_attend(n, t):
                pe_.wait_ge(s["f_pT"], TT * n + t + 1)
                if t:
                    pe_.wait_ge(s["f_attn"], TT * n + t)
                for hh in range(FH):
                    for half in range(2):
                        last = mm(ps_m[WIN * half:WIN * half + WIN, 33 * hh:33 * hh + 33], probT[:, hh, WIN * half:WIN * half + WIN],
                                  v_f[:, 2 * t + half, hh // 4], start=True, stop=True)
                last.then_inc(s["f_o"], 1)

            def fuse_a(n, j):
                pe_.wait_ge(s["f_xn"], n + 1)
                for c in range(KC):
                    bank = ps_m if c == 0 else halo_flat
                    for t in range(TT):
                        last = tr(bank[:, P * t:P * t + P], xn[:, t, P * c:P * c + P], ident[:])
                last.then_inc(s["f_xnT_ps"], 1)
                pe_.wait_ge(s["f_xnT"], n + 1)
                for m in range(KC):
                    for c in range(KC):
                        last = mm(quad[m][:, 0:TOK], wq_f[:, c, P * m:P * m + P], xnT[:, c, WIN:], start=(c == 0), stop=(c == KC - 1))
                last.then_inc(s["f_q_ps"], 1)
                for m in range(FKV):
                    for c in range(KC):
                        last = mm(quad[2 + m][:, 0:TOK], wk_f[:, c, m], xnT[:, c, WIN:], start=(c == 0), stop=(c == KC - 1))
                last.then_inc(s["f_k_ps"], 1)
                pe_.wait_ge(s["f_z"], n - j + 1)
                pe_.wait_ge(s["f_y"], n + 1)
                for w in range(2 * TT):
                    for c in range(KC):
                        last = mm(ps_t[:, 0, 64 * w:64 * w + 64], xnT[:, c, WIN * w:WIN * w + P], wv_f[:, c], start=(c == 0), stop=(c == KC - 1))
                last.then_inc(s["f_v_ps"], 1)
                pe_.wait_ge(s["f_q"], n + 1)
                pe_.wait_ge(s["f_k"], n + 1)
                tile_scores(n, 0)
                tile_scores(n, 1)
                tile_turn(n, 0)
                tile_scores(n, 2)
                tile_attend(n, 0)
                tile_turn(n, 1)
                tile_attend(n, 1)
                tile_turn(n, 2)
                tile_attend(n, 2)
                pe_.wait_ge(s["f_attn"], TT * n + TT)
                for c in range(KC):
                    bank = ps_m if c == 0 else halo_flat
                    for t in range(TT):
                        last = tr(bank[:, P * t:P * t + P], attn_f[:, t, P * c:P * c + P], ident[:])
                last.then_inc(s["f_oT_ps"], 1)
                pe_.wait_ge(s["f_oT"], n + 1)
                for t in range(TT):
                    for c in range(KC):
                        last = mm(t_flat[:, D * t:D * t + D], attnT_f[:, c, P * t:P * t + P], wo_f[:, c], start=(c == 0), stop=(c == KC - 1))
                last.then_inc(s["f_y_ps"], 1)

            def fuse_f(n, j):
                pe_.wait_ge(s["f_xn2"], n + 1)
                for c in range(KC):
                    bank = ps_m if c == 0 else halo_flat
                    for t in range(TT):
                        last = tr(bank[:, P * t:P * t + P], xn2[:, j, t, P * c:P * c + P], ident[:])
                last.then_inc(s["f_xn2T_ps"], 1)
                pe_.wait_ge(s["f_xn2T"], n + 1)
                for m in range(MC):
                    if m >= 4:
                        pe_.wait_ge(s["f_relu"], MC * n + m - 3)
                    for c in range(KC):
                        last = mm(quad[m % 4][:, 0:TOK], w_fc[:, c, P * m:P * m + P], xn2T[:, c], start=(c == 0), stop=(c == KC - 1))
                    last.then_inc(s["f_h_ps"], 1)
                pe_.wait_ge(s["f_y"], n + 3 - j)
                for t in range(TT):
                    for m in range(MC):
                        if t == 0:
                            pe_.wait_ge(s["f_sq"], MC * n + m + 1)
                        if t == 0 and m == 0 and j == 1:
                            pe_.wait_ge(s["f_z"], n + 1)
                        last = mm(t_flat[:, D * t:D * t + D], hid_f[:, m, P * t:P * t + P], w_pr[:, m], start=(m == 0), stop=(m == MC - 1))
                last.then_inc(s["f_z_ps"], 1)

            pe_.wait_ge(s["l_fus"], 16 * 11)
            with pe_.Fori(0, B // 2) as g:
                for j in range(2):
                    fuse_a(2 * g + j, j)
                for j in range(2):
                    fuse_f(2 * g + j, j)

        @block.scalar
        def _(act):
            A = act.activation
            pending = []

            def flush():
                while pending:
                    pending.pop(0)()

            def filter_slot(l, k):
                if k % 2 == 0:
                    return

                def later():
                    act.wait_ge(s["dve_div"], ITERS * l + k // 2 + 1)
                    if k < SLOTS - 1:
                        A(u[:, :, 0:IMG], fa, ACT.Tanh).then_inc(s["act_tanh"], 1)
                    else:
                        act.wait_ge(s["st_img"], 16 * l + 16)
                        A(f_out[:], fa, ACT.Copy, scale=2.0).then_inc(s["act_img"], 1)
                pending.append(later)

            def exps(l, i, n):
                act.wait_ge(s["dve_max"], 16 * l + 4 * i + n + 1)
                for hh in range(HALF):
                    last = A(prob[:, n % 2, hh], ps_s[n % 2][:, hh], ACT.Exp, bias=neg_max[:, n % 2, hh:hh + 1])
                last.then_inc(s["act_exp"], 1)

            def probs_out(l, i, n):
                act.wait_ge(s["pe_pT"], 16 * l + 4 * i + n + 1)
                A(probT[:].rearrange("p h k -> p (h k)"), t_flat, ACT.Copy).then_inc(s["act_pT"], 1)

            def h_out(l, place, bank):
                act.wait_ge(s["pe_hT"], 8 * l + place + 1)
                A(hT[:].rearrange("p c n -> p (c n)"), bank, ACT.Copy).then_inc(s["act_hT"], 1)

            def keys_out(l, i, g):
                act.wait_ge(s["pe_k"], 8 * l + 2 * i + g + 1)
                for hh in range(HALF):
                    last = A(km[:, g, :, hh], quad[2 + g][:, 0:D].rearrange("p (t k) -> p t k", t=2), ACT.Copy, scale=head_mask[:, hh:hh + 1])
                last.then_inc(s["act_k"], 1)

            def part_a(l, i, place, slot):
                n = 4 * l + i + 1
                keys_out(l, i, 0)
                act.wait_ge(s["pe_q"], n)
                A(qT[:].rearrange("p c n -> p (c n)"), quad[1], ACT.Copy, scale=SCALE_T).then_inc(s["act_q"], 1)
                flush()
                act.wait_ge(s["pe_v"], n)
                for t in range(2):
                    src = quad[0][:, D * t:D * t + D].rearrange("p (j o k) -> p j o k", o=2, k=TKD)
                    dst = v[:, t].rearrange("p (j o) k -> p j o k", o=2)
                    for o in range(2):
                        last = A(dst[:, :, o, TKD * o:TKD * o + TKD], src[:, :, o], ACT.Copy)
                last.then_inc(s["act_v"], 1)
                keys_out(l, i, 1)
                filter_slot(l, slot)
                flush()
                exps(l, i, 0)
                exps(l, i, 1)
                probs_out(l, i, 0)
                probs_out(l, i, 1)
                filter_slot(l, slot + 1)
                flush()
                exps(l, i, 2)
                exps(l, i, 3)
                probs_out(l, i, 2)
                probs_out(l, i, 3)
                h_out(l, place + 1, quad[3])
                filter_slot(l, slot + 2)
                flush()

            def part_f(l, i, place, slot):
                act.wait_ge(s["l_bc"], 16 * l + 16)
                for m in range(MC):
                    if m == 4:
                        flush()
                    if m % 2 == 0:
                        act.wait_ge(s["pe_ff1"], 16 * l + 4 * i + m // 2 + 1)
                    last = A(hidT[:, m], quad[(m // 2 + 1) % 4][:, D * (m % 2):D * (m % 2) + D], ACT.Relu, bias=b1[:, m:m + 1])
                    if m % 2:
                        last.then_inc(s["act_ff1"], 1)
                filter_slot(l, slot)
                flush()
                if place + 1 < len(ORDER):
                    h_out(l, place + 1, ps_m[:])
                filter_slot(l, slot + 1)

            act.wait_ge(s["c_general"], 1)
            with act.If(act.value_load(general[0:1, 0:1], min_val=0, max_val=1) > 0):
                own = gen_u[:, 1:3, 1:IMG + 1]

                def sigmoid(src, count):
                    act.wait_ge(s["gen_u_done"], count)
                    A(own, src, ACT.Tanh).then_inc(s["gen_tanh"], 1)
                    act.wait_ge(s["gen_tanh"], count)
                    A(own, own, ACT.Copy, scale=0.5, bias=0.5).then_inc(s["gen_u_done"], 1)

                act.wait_ge(s["gen_zero"], 1)
                with act.Fori(0, B) as b:
                    act.wait_ge(s["gen_o_in"], 16 * b + 16)
                    sigmoid(gen_o, (ITERS + 1) * b + 1)
                    with act.Fori(0, ITERS) as it:
                        act.wait_ge(s["gen_div"], ITERS * b + it + 1)
                        sigmoid(gen_w, (ITERS + 1) * b + it + 2)
                act.wait_ge(s["gen_out"], B)
                act.wait_ge(s["gen_st"], 16 * B)

            act.wait_ge(s["c_pool"], N_CONST)
            act.wait_ge(s["l_img"], 16 * 8)
            act.wait_ge(s["c_scaled"], 3)
            with act.Fori(0, LAYERS) as l:

                A(u[:, :, 0:IMG], o_all[:, bass.ds(l, 1)].rearrange("p a r c -> p (a r) c"), ACT.Tanh).then_inc(s["act_tanh"], 1)
                h_out(l, 0, ps_m[:])
                slot = 0
                for place, (what, i) in enumerate(ORDER):
                    (part_a if what == "A" else part_f)(l, i, place, slot)
                    slot += SLOTS_IN[what]
                flush()

            def tile_exps(n, t):
                act.wait_ge(s["f_max"], TT * n + t + 1)
                for hh in range(FH):
                    last = A(prob[:, t % 2, hh], ps_s[t % 2][:, hh], ACT.Exp, bias=neg_max[:, t, hh:hh + 1])
                last.then_inc(s["f_exp"], 1)
                A(sink_e[:, t], neg_max[:, t], ACT.Exp, bias=sink[:]).then_inc(s["f_sink"], 1)

            def tile_probs(n, t):
                act.wait_ge(s["f_pT_ps"], TT * n + t + 1)
                A(probT[:].rearrange("p h k -> p (h k)"), t_flat, ACT.Copy).then_inc(s["f_pT"], 1)

            def halves(dst, n_sem, n, done):
                act.wait_ge(n_sem, n + 1)
                A(dst[0], ps_m[:, 0:TOK], ACT.Copy)
                A(dst[1], halo_flat[:, 0:TOK], ACT.Copy).then_inc(done, 1)

            def fuse_a(n, j):
                halves([xnT[:, c, WIN:] for c in range(KC)], s["f_xnT_ps"], n, s["f_xnT"])
                act.wait_ge(s["f_q_ps"], n + 1)
                for m in range(KC):
                    for r in range(4):
                        last = A(qz[:, r, m], quad[m][:, 0:TOK], ACT.Identity, scale=row_mask[:, r:r + 1], bias=bq_m[:, m, r:r + 1])
                last.then_inc(s["f_q"], 1)
                act.wait_ge(s["f_k_ps"], n + 1)
                for m in range(FKV):
                    last = A(kT_f[:, m, WIN:], quad[2 + m][:, 0:TOK], ACT.Identity, bias=bk_f[:, m:m + 1])
                last.then_inc(s["f_k"], 1)
                tile_exps(n, 0)
                tile_exps(n, 1)
                tile_probs(n, 0)
                tile_probs(n, 1)
                tile_exps(n, 2)
                tile_probs(n, 2)
                halves([attnT_f[:, c] for c in range(KC)], s["f_oT_ps"], n, s["f_oT"])

            def fuse_f(n, j):
                halves([xn2T[:, c] for c in range(KC)], s["f_xn2T_ps"], n, s["f_xn2T"])
                for m in range(MC + j):
                    if m < MC:
                        act.wait_ge(s["f_h_ps"], MC * n + m + 1)
                        A(hid_f[:, m], quad[m % 4][:, 0:TOK], ACT.Relu).then_inc(s["f_relu"], 1)
                    if j and m:
                        act.wait_ge(s["f_relu"], MC * n + m)
                        A(hid_f[:, m - 1], hid_f[:, m - 1], ACT.Square).then_inc(s["f_sq"], 1)
                act.wait_ge(s["f_z_ps"], n + 1)
                act.wait_ge(s["f_out"], n + 1)
                A(y_in[:, j], t_flat[:, 0:TT * D], ACT.Copy).then_inc(s["f_z"], 1)

            with act.Fori(0, B // 2) as g:
                for j in range(2):
                    fuse_a(2 * g + j, j)
                for j in range(2):
                    fuse_f(2 * g + j, j)

        @block.vector
        def _(dve):
            chain = [0]

            def tick(ins):
                chain[0] += 1
                ins.then_inc(s["chain"], 1)
                return chain[0]

            def link(ins):
                dve.wait_ge(s["chain"], tick(ins))

            def restart():
                dve.wait_ge(s["chain"], chain[0])
                dve.sem_clear(s["chain"])
                chain[0] = 0

            tt, ts, stt = dve.tensor_tensor, dve.tensor_scalar, dve.scalar_tensor_tensor

            for free in (s["dve_ff2"], s["dve_wc"], s["f_z"], s["f_y"]):
                dve.sem_inc(free, 1)
            for free in (s["st_img"], s["st_out"]):
                dve.sem_inc(free, 16)
            dve.sem_inc(s["f_out"], 2)

            dve.wait_ge(s["l_tok"], 32)
            link(dve.tensor_copy(tok_f[:], tokens[:]))
            link(ts(tok_f[:], tok_f[:], float(-VOCAB), float(VOCAB - 1), ALU.max, ALU.min))
            link(ts(tok_neg[:], tok_f[:], 0.0, float(VOCAB), ALU.is_lt, ALU.mult))
            tt(tok_idx[:], tok_f[:], tok_neg[:], ALU.add).then_inc(s["c_idx"], 1)

            link(dve.memset(taps_std[:], 0.0))
            for at, val in ((4, -1.0), (7, 1.0), (13, -1.0), (14, 1.0), (19, -1.0), (22, 1.0), (30, -1.0), (31, 1.0)):
                link(dve.memset(taps_std[:, at:at + 1], val))
            dve.wait_ge(s["l_taps"], 32)
            link(tt(taps_diff[:], taps[:], taps_std[:], ALU.not_equal))
            link(dve.tensor_reduce(general_f[:], taps_diff[:], AX.X, ALU.max))
            dve.tensor_copy(general[:], general_f[:]).then_inc(s["c_general"], 1)
            dve.wait_ge(s["c_general"], 1)
            restart()
            with dve.If(dve.value_load(general[0:1, 0:1], min_val=0, max_val=1) > 0):
                def taps9(dst, src, at, more):
                    for k in range(9):
                        view = src[:, k // 3:k // 3 + 2, k % 3:k % 3 + IMG]
                        if k == 0 and not more:
                            link(ts(dst, view, taps[:, at:at + 1], None, ALU.mult))
                        else:
                            link(stt(dst, view, taps[:, at + k:at + k + 1], dst, ALU.mult, ALU.add))

                dve.sem_inc(s["gen_free"], 1)
                dve.sem_inc(s["gen_u_done"], 1)
                for t in (*gen_p, gen_u):
                    last = dve.memset(t, 0.0)
                    tick(last) if t is not gen_u else last.then_inc(s["gen_zero"], 1)
                dve.wait_ge(s["gen_zero"], 1)
                dve.wait_ge(s["gen_vf_in"], 32)
                restart()
                with dve.Fori(0, B) as b:
                    dve.wait_ge(s["gen_o_in"], 16 * b + 16)
                    link(dve.memset(gen_q, 0.0))
                    restart()
                    with dve.Fori(0, ITERS) as it:
                        n = ITERS * b + it + 1
                        dve.wait_ge(s["gen_halo_u"], 32 * n)
                        for k in range(2):
                            taps9(gen_g[k], gen_u, 9 * k, False)
                            link(tt(gen_g[k], gen_g[k], gen_vf[k], ALU.mult))
                        link(tt(gen_g[0], gen_g[0], gen_g[1], ALU.add))
                        link(stt(gen_q, gen_g[0], -0.5, gen_q, ALU.mult, ALU.add))
                        link(ts(gen_q, gen_q, 0.0, None, ALU.max))
                        tick(tt(gen_p[0][:, 1:3, 1:IMG + 1], gen_q, gen_vf[0], ALU.mult))
                        tt(gen_p[1][:, 1:3, 1:IMG + 1], gen_q, gen_vf[1], ALU.mult).then_inc(s["gen_flux"], 1)
                        dve.wait_ge(s["gen_halo_p"], 64 * n)
                        taps9(gen_t, gen_p[0], 18, False)
                        taps9(gen_t, gen_p[1], 27, True)
                        tt(gen_w, gen_o, gen_t, ALU.subtract).then_inc(s["gen_div"], 1)
                        restart()
                    dve.wait_ge(s["gen_u_done"], (ITERS + 1) * (b + 1) + 1)
                    ts(gen_w, gen_w, 2.0, None, ALU.mult).then_inc(s["gen_out"], 1)
                    dve.wait_ge(s["gen_st"], 16 * b + 16)
                    dve.sem_inc(s["gen_free"], 1)

            dve.wait_ge(s["l_img"], 16 * 8)
            link(ts(vq[:], vf[:], 0.25, None, ALU.mult))
            dve.wait_ge(s["c_pool"], N_CONST)
            for hh in range(HALF):
                tick(dve.tensor_reduce(head_mask[:, hh:hh + 1], ident[:, TKD * hh:TKD * hh + TKD], AX.X, ALU.add))
            for r in range(4):
                tick(dve.tensor_reduce(row_mask[:, r:r + 1], ident[:, 32 * r:32 * r + 32], AX.X, ALU.add))
            dve.wait_ge(s["chain"], chain[0])
            ts(row_mask[:], row_mask[:], SCALE_F, None, ALU.mult).then_inc(s["c_scaled"], 1)
            dve.wait_ge(s["c_scaled"], 1)
            dve.wait_ge(s["l_fus"], 16 * 11)
            for m in range(KC):
                ts(bq_m[:, m], row_mask[:], bq_f[:, m:m + 1], None, ALU.mult).then_inc(s["c_scaled"], 1)
            dve.wait_ge(s["g_emb"], 16 * B)
            tt(h[:], h[:], pe[:].unsqueeze(1).to_broadcast([P, B, D]), ALU.add).then_inc(s["h_ready"], 4)
            dve.wait_ge(s["h_ready"], 4)

            p0_done = [0]

            def flux(l, k):
                dve.wait_ge(s["pe_halo"], SLOTS * l + k + 1)
                tt(fa[:, 0:RPP - 1], u[:, 1:RPP, 0:IMG], u[:, 0:RPP - 1, 0:IMG], ALU.subtract)
                ta = tick(tt(fa[:, RPP - 1], halo[:, 0], u[:, RPP - 1, 0:IMG], ALU.subtract))
                tb = tick(tt(fb, u[:, :, 1:], u[:, :, 0:IMG], ALU.subtract))
                dve.wait_ge(s["chain"], ta)
                tick(tt(fa, fa, vq[:, 0], ALU.mult))
                dve.wait_ge(s["chain"], tb)
                link(tt(fb, fb, vq[:, 1], ALU.mult))
                link(tt(fa, fa, fb, ALU.add))
                link(stt(q_st, q_st, 0.0, fa, ALU.max, ALU.subtract))
                stt(p1[:], q_st, 0.0, vf[:, 0], ALU.max, ALU.mult).then_inc(s["dve_flux"], 1)
                p0_done[0] = tick(stt(p0[:, :, 1:], q_st, 0.0, vf[:, 1], ALU.max, ALU.mult))
                dve.wait_ge(s["dve_flux"], ITERS * l + k // 2 + 1)

            def divergence(l, k):
                tick(tt(fa[:, 1:RPP], p1[:, 1:RPP], p1[:, 0:RPP - 1], ALU.subtract))
                dve.wait_ge(s["chain"], p0_done[0])
                tick(tt(fb, p0[:, :, 1:], p0[:, :, 0:IMG], ALU.subtract))
                dve.wait_ge(s["pe_halo"], SLOTS * l + k + 1)
                link(tt(fa[:, 0], p1[:, 0], halo[:, 1], ALU.subtract))
                link(tt(fa, fa, fb, ALU.add))
                tt(fa, o_all[:, bass.ds(l, 1)].rearrange("p a r c -> p (a r) c"), fa, ALU.subtract).then_inc(s["dve_div"], 1)

            def filter_slot(l, k):
                if k % 2 == 0:
                    flux(l, k)
                else:
                    divergence(l, k)

            def head_max(l, i, n):
                dve.wait_ge(s["pe_s"], 16 * l + 4 * i + n + 1)
                link(dve.tensor_reduce(rmax[:, n % 2], ps_s[n % 2][:], AX.X, ALU.max))
                ts(neg_max[:, n % 2], rmax[:, n % 2], -1.0, None, ALU.mult).then_inc(s["dve_max"], 1)

            def normalise(l, i, t):
                dve.wait_ge(s["pe_o"], 8 * l + 2 * i + t + 1)
                nums, dens = (sums[t][:, D * k:D * k + D].rearrange("p (c n) -> p c n", c=KC) for k in range(2))
                link(dve.reciprocal(rden[:, t], dens))
                tt(attnT[:, :, P * t:P * t + P], nums, rden[:, t], ALU.mult).then_inc(s["dve_attn"], 1)

            def moments(src, n, done):
                for t in range(n):
                    tick(dve.bn_stats(stats[:, t], src[:, t]))
                dve.wait_ge(s["chain"], chain[0])
                for t in range(n):
                    last = dve.bn_aggr(mv[:, t], stats[:, t])
                    tick(last) if t < n - 1 else last.then_inc(done, 1)

            def text_residual(n, i, ps_in, add, freed):
                hp = h[:, 2 * i:2 * i + 2]
                wide = lambda r: vecs[:, r].unsqueeze(1).to_broadcast([P, 2, D])
                tt(hp, ps_in.rearrange("p (t n) -> p t n", t=2), hp, ALU.add).then_inc(freed, 1)
                dve.wait_ge(freed, n + 1)
                if add is not None:
                    link(tt(hp, hp, wide(add), ALU.add))
                return hp, wide

            def norm_start(l, what, i, order):
                n = 4 * l + i + 1
                if what == "A":
                    dve.wait_ge(s["pe_wc"], n)
                    hp, wide = text_residual(n, i, ps_t[:, 1], None, s["dve_wc"])
                else:
                    dve.wait_ge(s["pe_ff2"], n)
                    dve.wait_ge(s["dve_ln1"], n)
                    dve.wait_ge(s["l_vec"], 16 * l + 16)
                    hp, wide = text_residual(n, i, ps_t[:, 0], 2, s["dve_ff2"])
                moments(hp, 2, s["dve_stat"])

                def norm_end():
                    dve.wait_ge(s["dve_stat"], 8 * l + order)
                    dve.wait_ge(s["pool_rstd"], 8 * l + order)
                    for t in range(2):
                        tick(ts(hp[:, t], hp[:, t], mv[:, t, 0:1], rstd[:, t:t + 1], ALU.subtract, ALU.mult))
                    dve.wait_ge(s["chain"], chain[0])
                    gain, bias, done = (0, 1, s["dve_ln1"]) if what == "A" else (3, 4, s["h_ready"])
                    dve.wait_ge(s["l_vec"], 16 * l + 16)
                    link(tt(hp, hp, wide(gain), ALU.mult))
                    tt(hp, hp, wide(bias), ALU.add).then_inc(done, 1)
                return norm_end

            restart()
            with dve.Fori(0, LAYERS) as l:
                link(dve.memset(q_st, 0.0))
                slot = 0
                norm_end = None
                for place, (what, i) in enumerate(ORDER):
                    before, i_before = ORDER[place - 1] if place else (None, None)
                    filter_slot(l, slot)
                    if before == "A":
                        norm_end = norm_start(l, before, i_before, place)
                    elif before == "F":
                        norm_end()
                    if what == "A":
                        head_max(l, i, 0)
                        head_max(l, i, 1)
                        if before == "A":
                            norm_end()
                        filter_slot(l, slot + 1)
                        head_max(l, i, 2)
                        head_max(l, i, 3)
                        filter_slot(l, slot + 2)
                        normalise(l, i, 0)
                        normalise(l, i, 1)
                    else:
                        if before == "A":
                            norm_end()
                        filter_slot(l, slot + 1)
                        norm_end = norm_start(l, what, i, place + 1)
                    slot += SLOTS_IN[what]
                norm_end()
                restart()

            def order_of(g, j, which):
                return 4 * g + {("x", 0): 1, ("x", 1): 2, ("res", 0): 3, ("res", 1): 4}[which, j]

            def joined_norm(n, src, dst, count, done):
                moments(src, TT, s["f_stat"])
                dve.wait_ge(s["f_stat"], count)
                dve.wait_ge(s["f_rstd"], count)
                for t in range(TT):
                    last = ts(dst[:, t], src[:, t], mv[:, t, 0:1], rstd[:, t:t + 1], ALU.subtract, ALU.mult)
                    tick(last) if t < TT - 1 else last.then_inc(done, 1)

            def tile_max(n, t):
                dve.wait_ge(s["f_s"], TT * n + t + 1)
                link(dve.tensor_reduce(rmax[:, t % 2], ps_s[t % 2][:], AX.X, ALU.max))
                ts(neg_max[:, t], rmax[:, t % 2], sink[:], -1.0, ALU.max, ALU.mult).then_inc(s["f_max"], 1)

            def tile_normalise(n, t):
                dve.wait_ge(s["f_o"], TT * n + t + 1)
                dve.wait_ge(s["f_sink"], TT * n + t + 1)
                o = ps_m[:, 0:33 * FH].rearrange("p (h k) -> p h k", h=FH)
                link(tt(den[:].unsqueeze(2), o[:, :, HD:], sink_e[:, t].unsqueeze(2), ALU.add))
                link(dve.reciprocal(rden_f[:], den[:]))
                tt(attn_f[:, t].rearrange("p (h k) -> p h k", h=FH), o[:, :, 0:HD], rden_f[:].unsqueeze(2).to_broadcast([P, FH, HD]), ALU.mult).then_inc(s["f_attn"], 1)

            def prepare(g, n, j):
                dve.wait_ge(l_x[j], 16 * g + 16)
                ts(x[:, j, 2], h[:, bass.ds(n, 1)].rearrange("p a n -> p (a n)"), 1.0, None, ALU.mult).then_inc(s["f_xt"], 1)
                dve.wait_ge(s["f_xt"], n + 1)
                joined_norm(n, x[:, j], xn, order_of(g, j, "x"), s["f_xn"])

            def fuse_a(g, n, j):
                dve.wait_ge(s["f_v_ps"], n + 1)
                tt(v_f[:, :, :, 0:HD], ps_t[:, 0, 0:64 * 2 * TT].rearrange("p (w j k) -> p w j k", w=2 * TT, j=FKV),
                   bv_f[:].rearrange("p (j k) -> p j k", j=FKV).unsqueeze(1).to_broadcast([P, 2 * TT, FKV, HD]), ALU.add).then_inc(s["f_v"], 1)
                tile_max(n, 0)
                tile_max(n, 1)
                tile_max(n, 2)
                for t in range(TT):
                    tile_normalise(n, t)
                if j == 0:
                    prepare(g, n + 1, 1)
                dve.wait_ge(s["f_y_ps"], n + 1)
                dve.wait_ge(s["st_out"], 32 * g + 16)
                rj = res[:, j]
                tt(rj, t_flat[:, 0:TT * D].rearrange("p (t n) -> p t n", t=TT), x[:, j], ALU.add).then_inc(s["f_y"], 1)
                dve.wait_ge(s["f_y"], n + 2)
                link(tt(rj, rj, bo_f[:].unsqueeze(1).to_broadcast([P, TT, D]), ALU.add))
                joined_norm(n, rj, xn2[:, j], order_of(g, j, "res"), s["f_xn2"])

            def squares(n):
                for m in range(MC):
                    dve.wait_ge(s["f_relu"], MC * n + m + 1)
                    tt(hid_f[:, m], hid_f[:, m], hid_f[:, m], ALU.mult).then_inc(s["f_sq"], 1)

            def spike_steps(n, j):
                dve.wait_ge(s["f_z"], n + 2)
                dve.wait_ge(s["f_out"], n + 2)
                y = y_in[:, j]
                rj = res[:, j].rearrange("p t n -> p (t n)")
                tick(ts(mem, y, 1.0, None, ALU.mult))
                link(ts(spikes, y, 1.0, None, ALU.is_gt))
                for step in range(1, STEPS):
                    link(stt(mem_t, mem, 0.9, y, ALU.mult, ALU.add))
                    link(stt(mem, mem, 1.0, mem_t, ALU.is_gt, ALU.subtract, reverse1=True))
                    link(stt(spikes, mem, 1.0, spikes, ALU.is_gt, ALU.add))
                stt(rj, spikes, 1.0 / STEPS, rj, ALU.mult, ALU.add).then_inc(s["f_out"], 1)

            def two_batches(g, last):
                for j in range(2):
                    fuse_a(g, 2 * g + j, j)
                squares(2 * g)
                spike_steps(2 * g, 0)
                if not last:
                    prepare(g + 1, 2 * g + 2, 0)
                spike_steps(2 * g + 1, 1)
                restart()

            prepare(0, 0, 0)
            restart()
            with dve.Fori(0, B // 2 - 1) as g:
                two_batches(g, False)
            two_batches(B // 2 - 1, True)


def kernel(**inputs):
    import numpy as np
    import concourse.bacc as _bacc
    from concourse import mybir as _mybir
    from concourse.bass_utils import run_bass_kernel_spmd as _run

    I = {k: np.asarray(v) for k, v in inputs.items()}

    def chunks(w):
        return np.ascontiguousarray(np.swapaxes(w.reshape(*w.shape[:-2], -1, P, w.shape[-1]), -3, -2))

    t = {n: I["L0_txt_" + n] for n in ("Wq", "Wk", "Wv", "Wc", "W1", "b1", "W2", "b2", "g1", "be1", "g2", "be2")}
    a = {n: I["L0_attn_" + n] for n in ("Wq", "bq", "Wk", "bk", "Wv", "bv", "Wo", "bo")}
    pos = np.arange(SEQ, dtype=np.float32)[:, None]
    div = np.exp(np.arange(0, D, 2, dtype=np.float32) * np.float32(-np.log(np.float32(10000.0)) / np.float32(D)))
    pe = np.zeros((SEQ, D), np.float32)
    pe[:, 0::2], pe[:, 1::2] = np.sin(pos * div), np.cos(pos * div)
    wk4 = np.stack([np.concatenate([a["Wk"][HD * j:HD * j + HD]] * 4, 0) for j in range(FKV)], 0).reshape(FKV * P, D).T
    arrays = {
        "o": I["x"].reshape(B, IMG, IMG),
        "tokens": I["x_txt"].T,
        "vf": np.transpose(I["L0_tok_vector_field"], (2, 0, 1))[::-1],
        "nabla_w": I["L0_tok_nabla_w"].reshape(18),
        "div_w": I["L0_tok_div_w"].reshape(18),
        "pe": pe,
        "emb": I["L0_txt_emb"],
        "w_attn": chunks(np.concatenate([t["Wq"], t["Wk"], t["Wv"], t["Wc"]], -1)),
        "w1": chunks(t["W1"]),
        "w2": chunks(t["W2"]),
        "vecs": np.stack([t["g1"], t["be1"], t["b2"], t["g2"], t["be2"]], 1),
        "b1": np.transpose(t["b1"].reshape(LAYERS, MC, P), (0, 2, 1)),
        "wq_f": chunks(a["Wq"].T),
        "wk_f": chunks(wk4).reshape(P, KC, FKV, P),
        "wv_f": chunks(a["Wv"].T),
        "wo_f": chunks(a["Wo"].T),
        "w_fc": chunks(I["L0_ffn_W_fc"].T),
        "w_pr": chunks(I["L0_ffn_W_proj"].T),
        "bq_f": a["bq"].reshape(KC, P).T,
        "bk_f": np.tile(a["bk"].reshape(FKV, HD), (1, 4)).T,
        "bv_f": a["bv"],
        "bo_f": a["bo"],
        "sink": I["L0_attn_sink_bias"].reshape(1),
    }
    nc = _bacc.Bacc("TRN2", target_bir_lowering=False, num_devices=1)
    feeds, d = {}, {}
    for name, arr in arrays.items():
        arr = np.ascontiguousarray(arr)
        feeds["in_" + name] = arr
        d[name] = nc.dram_tensor("in_" + name, arr.shape, _mybir.dt.from_np(arr.dtype), kind="ExternalInput").ap()
    out = nc.dram_tensor("out", (B, TOK, D), F32, kind="ExternalOutput").ap()
    build(nc, d, out)
    r = _run(nc, [feeds], core_ids=[0])
    return r.results[0]["out"]
```

```python
from contextlib import ExitStack

import concourse.bass as bass
from concourse import mybir

F32 = mybir.dt.float32
BF16 = mybir.dt.bfloat16
I32 = mybir.dt.int32
U32 = mybir.dt.uint32
ALU = mybir.AluOpType
ACT = mybir.ActivationFunctionType
AX = mybir.AxisListType

P = 128
B, IMG = 8, 256
D, KC = 256, 2
SEQ = 128
VOCAB = 8000
LAYERS, TH, TKD, M = 4, 16, 16, 1024
MC = M // P
TOK = IMG + SEQ
TT = TOK // P
WIN, FH, FKV, HD = 64, 8, 2, 32
EPS = 1e-5
ITERS = 10
PAIRS = B // 2
RPP = IMG // 64
SLOTS = 2 * ITERS
HALF = 8
MASKED = -65536.0
STEPS = 5
SCALE_T = float(TKD) ** -0.5
SCALE_F = float(HD) ** -0.5
ORDER = [("A", 0), ("A", 1), ("F", 0), ("A", 2), ("F", 1), ("A", 3), ("F", 2), ("F", 3)]
SLOTS_IN = {"A": 3, "F": 2}


def build(nc, d, out):
    with ExitStack() as ctx:
        def sb(name, shape, dt=F32):
            return ctx.enter_context(nc.sbuf_tensor(name, shape, dt))

        def ps(name, shape, dt=F32):
            return ctx.enter_context(nc.psum_tensor(name, shape, dt))

        def sem(name):
            return ctx.enter_context(nc.semaphore(name))

        filtered = nc.dram_tensor("filtered", (2, B, IMG, IMG), F32, kind="Internal").ap()

        ident = sb("ident", [P, P])
        ident_h = sb("ident_h", [P, P], BF16)
        up_shift = sb("up_shift", [P, P])
        down_shift = sb("down_shift", [P, P])
        edge = sb("edge", [1, P])
        ones = sb("ones", [P, 4 * P])
        mask = sb("mask", [P, 2, 4, P], BF16)
        head_mask = sb("head_mask", [P, HALF])
        ones_pad = sb("ones_pad", [P, 2, 2 * TKD])
        pow_half = sb("pow_half", [P, 4])
        row_mask = sb("row_mask", [P, 4])
        bq_m = sb("bq_m", [P, KC, 4])
        eps_c = sb("eps_c", [P, 4])
        pe = sb("pe", [P, D])
        taps = sb("taps", [P, 36])
        taps_std = sb("taps_std", [P, 36])
        taps_diff = sb("taps_diff", [P, 36])
        general_f = sb("general_f", [P, 1])
        general = sb("general", [P, 1], I32)

        tokens = sb("tokens", [P, B], I32)
        tok_f = sb("tok_f", [P, B])
        tok_neg = sb("tok_neg", [P, B])
        tok_idx = sb("tok_idx", [P, B], U32)
        h = sb("h", [P, B, D])
        w_attn = sb("w_attn", [P, KC, 4 * D])
        w1 = sb("w1", [P, KC, M])
        w2 = sb("w2", [P, MC, D])
        vecs = sb("vecs", [P, 5, D])
        b1 = sb("b1", [P, MC])
        hT = sb("hT", [P, KC, D])
        qT = sb("qT", [P, KC, D])
        km_all = sb("km", [P, KC * 2 * HALF * P])
        km = km_all[:].rearrange("p (g t h k) -> p g t h k", g=KC, t=2, h=HALF)
        v = sb("v", [P, 2, TH, 2 * TKD])
        prob = sb("prob", [P, 2, HALF, P])
        probT = sb("probT", [P, HALF, P])
        neg_max = sb("neg_max", [P, TT, HALF])
        rden = sb("rden", [P, 2, KC, P])
        attnT = sb("attnT", [P, KC, D])
        hidT = sb("hidT", [P, MC, D])
        stats = sb("stats", [P, TT, 6])
        mv = sb("mv", [P, TT, 2])
        var_eps = sb("var_eps", [P, TT])
        rstd = sb("rstd", [P, TT])

        o_all = sb("o_all", [P, PAIRS, RPP, IMG])
        vf = sb("vf", [P, 2, RPP, IMG])
        vq = sb("vq", [P, 2, RPP, IMG])
        u = sb("u", [P, RPP, IMG + 1])
        f3 = sb("f3", [P, 3, RPP, IMG])
        fa, fb, q_st = f3[:, 0], f3[:, 1], f3[:, 2]
        p1 = sb("p1", [P, RPP, IMG])
        p0 = sb("p0", [P, RPP, IMG + 1])
        f_out = sb("f_out", [P, RPP, IMG])

        wq_f = sb("wq_f", [P, KC, D])
        wk_f = sb("wk_f", [P, KC, FKV, P])
        wv_f = sb("wv_f", [P, KC, FKV * HD])
        wo_f = sb("wo_f", [P, KC, D])
        w_fc = sb("w_fc", [P, KC, M])
        w_pr = sb("w_pr", [P, MC, D])
        bq_f = sb("bq_f", [P, KC])
        bk_f = sb("bk_f", [P, FKV])
        bv_f = sb("bv_f", [P, FKV * HD])
        bo_f = sb("bo_f", [P, D])
        sink = sb("sink", [P, 1])
        x = sb("x", [P, 2, TT, D])
        km_as = lambda k: km_all[:, k * TT * D:(k + 1) * TT * D]
        xn = km_as(0).rearrange("p (t n) -> p t n", t=TT)
        attn_f = km_as(1).rearrange("p (t n) -> p t n", t=TT)
        attnT_f = km_as(2).rearrange("p (c n) -> p c n", c=KC)
        xn2T = km_as(3).rearrange("p (c n) -> p c n", c=KC)
        xnT = sb("xnT", [P, KC, WIN + TOK])
        kT_f = sb("kT_f", [P, FKV, WIN + TOK])
        v_f = sb("v_f", [P, 2 * TT, FKV, HD + 1])
        sink_e = sb("sink_e", [P, TT, FH])
        rmax = sb("rmax", [P, 2, FH])
        den = sb("den", [P, FH])
        rden_f = sb("rden_f", [P, FH])
        xn2 = sb("xn2", [P, 2, TT, D])
        hid_f = o_all[:, :, :, :].rearrange("p a r c -> p (a r c)")[:, 0:MC * TOK].rearrange("p (m t) -> p m t", m=MC)
        qz = f3[:, :, :, :].rearrange("p a r c -> p (a r c)")[:, 0:4 * KC * TOK].rearrange("p (r c t) -> p r c t", r=4, c=KC)
        spare = vf[:, :, :, :].rearrange("p a r c -> p (a r c)")
        spare2 = vq[:, :, :, :].rearrange("p a r c -> p (a r c)")
        mem = spare[:, 0:TT * D]
        mem_t = spare[:, TT * D:2 * TT * D]
        spikes = spare2[:, 0:TT * D]
        res = w2[:].rearrange("p m n -> p (m n)")[:, 0:2 * TT * D].rearrange("p (j t n) -> p j t n", j=2, t=TT)
        y_in = w_attn[:].rearrange("p c n -> p (c n)")[:, 0:2 * TT * D].rearrange("p (j n) -> p j n", j=2)

        def ringed(t):
            return t[:, 0:4 * (IMG + 2)].rearrange("p (r c) -> p r c", r=4)

        gen_u = ringed(x[:].rearrange("p a t n -> p (a t n)"))
        gen_p = [ringed(xn2[:].rearrange("p a t n -> p (a t n)")), ringed(prob[:].rearrange("p a h k -> p (a h k)"))]
        rows2 = lambda t: t.rearrange("p (r c) -> p r c", r=2)
        hid_flat = hidT[:].rearrange("p m n -> p (m n)")
        gen_vf = [rows2(hid_flat[:, 512 * k:512 * k + 512]) for k in range(2)]
        gen_q, gen_t = rows2(hid_flat[:, 1024:1536]), rows2(hid_flat[:, 1536:2048])
        gen_g = [rows2(km_all[:, 512 * k:512 * k + 512]) for k in range(2)]
        probT_flat = probT[:].rearrange("p h k -> p (h k)")
        gen_o, gen_w = rows2(probT_flat[:, 0:512]), rows2(probT_flat[:, 512:1024])

        halo = ps("halo", [P, 2, IMG])
        ps_s = [ps(f"ps_s{i}", [P, HALF, P]) for i in range(2)]
        ps_t = ps("ps_t", [P, 2, 512])
        ps_m = ps("ps_m", [P, 512])
        s_flat = [t[:, :, :].rearrange("p h k -> p (h k)") for t in ps_s]
        quad = [s_flat[0][:, 0:512], s_flat[0][:, 512:1024], s_flat[1][:, 0:512], s_flat[1][:, 512:1024]]
        sums = [ps_m, quad[0]]
        t_flat = ps_t[:, :, :].rearrange("p a n -> p (a n)")
        t_heads = t_flat.rearrange("p (h k) -> p h k", h=HALF)
        halo_flat = halo[:, :, :].rearrange("p a n -> p (a n)")

        names = [
            "l_vec", "l_attn", "l_w1", "l_w2", "l_bc", "l_tok", "l_img", "l_fus", "st_img", "st_out", "g_emb", "g_emb_first", "l_img_rest",
            "l_taps",
            "c_pool", "c_scaled", "c_idx", "c_general",
            "pe_hT", "pe_q", "pe_k", "pe_v", "pe_s", "pe_pT", "pe_o", "pe_wc", "pe_ff1", "pe_ff2",
            "act_hT", "act_q", "act_k", "act_v", "act_exp", "act_pT", "act_ff1",
            "dve_max", "dve_attn", "dve_wc", "dve_ln1", "dve_ff2", "h_ready", "dve_stat", "pool_rstd", "pool_eps",
            "pe_halo", "act_tanh", "act_img", "dve_flux", "dve_div",
            "f_xt", "f_xnT_ps", "f_xnT", "f_q_ps", "f_q", "f_k_ps", "f_k", "f_v_ps", "f_v", "f_s", "f_max", "f_exp_4", "f_exp", "f_sink",
            "f_pT_ps_4", "f_pT_ps", "f_pT", "f_o", "f_attn", "f_oT_ps", "f_oT", "f_y_ps", "f_y", "f_xn", "f_xn2", "f_xn2T_ps", "f_xn2T",
            "f_h_ps", "f_relu", "f_sq", "f_z_ps_2", "f_z_ps", "f_z_2", "f_z", "f_out", "f_stat", "f_rstd", "f_eps",
            "chain",
            "gen_vf_in", "gen_free", "gen_o_in", "gen_tanh", "gen_u_done", "gen_halo_u", "gen_flux", "gen_halo_p", "gen_div",
            "gen_out", "gen_st", "gen_zero",
        ]
        s = {n: sem(n) for n in names}

        l_x = [sem(f"l_x{j}") for j in range(2)]

        block = ctx.enter_context(nc.Block())

        @block.sync
        def _(sp):
            sp.dma_start(taps[:, 0:18], d["nabla_w"].partition_broadcast(P)).then_inc(s["l_taps"], 16)
            sp.dma_start(taps[:, 18:36], d["div_w"].partition_broadcast(P)).then_inc(s["l_taps"], 16)
            sp.dma_start(tokens[:], d["tokens"]).then_inc(s["l_tok"], 16)
            sp.dma_start(pe[:], d["pe"]).then_inc(s["l_tok"], 16)
            sp.dma_start(w_attn[:], d["w_attn"][0]).then_inc(s["l_attn"], 16)
            load_images = lambda k: sp.dma_start(o_all[:, k], d["o"][2 * k:2 * k + 2].rearrange("b (p r) c -> (b p) r c", r=RPP))
            load_images(0).then_inc(s["l_img"], 16)
            for img in range(2):
                for comp in range(2):
                    sp.dma_start(vf[64 * img:64 * img + 64, comp], d["vf"][comp].rearrange("(p r) c -> p r c", r=RPP)).then_inc(s["l_img"], 16)
            sp.wait_ge(s["g_emb"], 16 * (B - 2))
            sp.dma_start(vecs[:], d["vecs"][0].partition_broadcast(P)).then_inc(s["l_vec"], 16)
            sp.dma_start(b1[:], d["b1"][0]).then_inc(s["l_bc"], 16)
            sp.dma_start(w1[:], d["w1"][0]).then_inc(s["l_w1"], 16)
            sp.dma_start(w2[:], d["w2"][0]).then_inc(s["l_w2"], 16)
            for pair in range(1, PAIRS):
                load_images(pair).then_inc(s["l_img_rest"], 16)
            for t, n in ((wq_f, "wq_f"), (wk_f, "wk_f"), (wv_f, "wv_f"), (wo_f, "wo_f"), (w_fc, "w_fc"), (w_pr, "w_pr"), (bq_f, "bq_f"), (bk_f, "bk_f")):
                sp.dma_start(t[:], d[n]).then_inc(s["l_fus"], 16)
            for t, n in ((bv_f, "bv_f"), (bo_f, "bo_f"), (sink, "sink")):
                sp.dma_start(t[:], d[n].partition_broadcast(P)).then_inc(s["l_fus"], 16)

            sp.wait_ge(s["c_general"], 1)
            which = sp.value_load(general[0:1, 0:1], min_val=0, max_val=1)
            with sp.If(which > 0):
                for k in range(2):
                    sp.dma_start(gen_vf[k], d["vf"][k].rearrange("(p r) c -> p r c", r=2)).then_inc(s["gen_vf_in"], 16)

                def ring_rows(t, done):
                    sp.dma_start(t[1:P, 0], t[0:P - 1, 2]).then_inc(done, 16)
                    sp.dma_start(t[0:P - 1, 3], t[1:P, 1]).then_inc(done, 16)

                with sp.Fori(0, B) as b:
                    sp.wait_ge(s["gen_free"], b + 1)
                    sp.dma_start(gen_o, d["o"][bass.ds(b, 1)].rearrange("b (p r) c -> p (b r) c", r=2)).then_inc(s["gen_o_in"], 16)
                    with sp.Fori(0, ITERS) as it:
                        sp.wait_ge(s["gen_u_done"], (ITERS + 1) * b + it + 2)
                        ring_rows(gen_u, s["gen_halo_u"])
                        sp.wait_ge(s["gen_flux"], ITERS * b + it + 1)
                        for k in range(2):
                            ring_rows(gen_p[k], s["gen_halo_p"])
                    sp.wait_ge(s["gen_out"], b + 1)
                    sp.dma_start(filtered[1][bass.ds(b, 1)].rearrange("b (p r) c -> p (b r) c", r=2), gen_w).then_inc(s["gen_st"], 16)
                sp.wait_ge(s["gen_st"], 16 * B)

            def store_pair(l):
                sp.wait_ge(s["act_img"], l + 1)
                dst = filtered[0].rearrange("(a b) (p r) c -> a (b p) r c", b=2, r=RPP)
                dst = dst[l] if isinstance(l, int) else dst[bass.ds(l, 1)].rearrange("a p r c -> p (a r) c")
                sp.dma_start(dst, f_out[:]).then_inc(s["st_img"], 16)

            with sp.Fori(0, LAYERS - 1) as l:
                sp.wait_ge(s["pe_wc"], 4 * l + 4)
                sp.dma_start(w_attn[:], d["w_attn"][bass.ds(l + 1, 1)].rearrange("a p c n -> p (a c) n")).then_inc(s["l_attn"], 16)
                sp.wait_ge(s["pe_ff1"], 16 * l + 16)
                sp.dma_start(w1[:], d["w1"][bass.ds(l + 1, 1)].rearrange("a p c n -> p (a c) n")).then_inc(s["l_w1"], 16)
                sp.wait_ge(s["pe_ff2"], 4 * l + 4)
                sp.dma_start(w2[:], d["w2"][bass.ds(l + 1, 1)].rearrange("a p c n -> p (a c) n")).then_inc(s["l_w2"], 16)
                sp.wait_ge(s["h_ready"], 4 * l + 8)
                sp.dma_start(vecs[:], d["vecs"][bass.ds(l + 1, 1)].partition_broadcast(P).rearrange("p a v n -> p (a v) n")).then_inc(s["l_vec"], 16)
                sp.wait_ge(s["act_ff1"], 16 * l + 16)
                sp.dma_start(b1[:], d["b1"][bass.ds(l + 1, 1)].rearrange("a p m -> p (a m)")).then_inc(s["l_bc"], 16)
                store_pair(l)

            out_v = out.rearrange("b (t p) n -> b p t n", p=P)

            def load_x(b, j):
                src = filtered[bass.ds(which, 1), bass.ds(b, 1)].rearrange("w b (t p) c -> p (w b t) c", p=P)
                sp.dma_start(x[:, j, 0:2], src).then_inc(l_x[j], 16)

            sp.wait_ge(s["st_img"], 16 * (LAYERS - 1) + 16)
            for j in range(2):
                load_x(j, j)
            store_pair(LAYERS - 1)
            sp.wait_ge(s["st_img"], 16 * LAYERS + 16)

            def store(b, j):
                sp.wait_ge(s["f_out"], b + 3)
                sp.dma_start(out_v[bass.ds(b, 1)].rearrange("b p t n -> p (b t) n"), res[:, j]).then_inc(s["st_out"], 16)

            with sp.Fori(0, B // 2 - 1) as g:
                for j in range(2):
                    sp.wait_ge(s["f_y"], 2 * g + j + 2)
                    load_x(2 * g + 2 + j, j)
                for j in range(2):
                    store(2 * g + j, j)
            for j in range(2):
                store(B - 2 + j, j)
            sp.wait_ge(s["st_out"], 16 * B + 16)

        N_CONST = 13 + 4
        N_CONST_ALL = N_CONST + 2 + 9 + 3

        @block.gpsimd
        def _(pool):
            c = 0
            def const(ins):
                nonlocal c
                ins.then_inc(s["c_pool"], 1)
                c += 1
                pool.wait_ge(s["c_pool"], c)
            const(pool.memset(ones[:], 1.0))
            const(pool.affine_select(out=ident[:], in_=ones[:, 0:P], compare_op=ALU.is_equal, fill=0.0, base=0, pattern=[[-1, P]], channel_multiplier=1))
            const(pool.affine_select(out=up_shift[:], in_=ones[:, 0:P], compare_op=ALU.is_equal, fill=0.0, base=-1, pattern=[[-1, P]], channel_multiplier=1))
            const(pool.affine_select(out=down_shift[:], in_=ones[:, 0:P], compare_op=ALU.is_equal, fill=0.0, base=1, pattern=[[-1, P]], channel_multiplier=1))
            const(pool.memset(up_shift[:, 63:64], 0.0))
            const(pool.memset(down_shift[:, 64:65], 0.0))
            const(pool.memset(edge[:], 0.0))
            const(pool.memset(edge[:, 63:64], -1.0))
            const(pool.memset(edge[:, 127:128], -1.0))
            const(pool.memset(pow_half[:], -0.5))
            const(pool.memset(eps_c[:], EPS))
            const(pool.memset(p0[:, :, 0:1], 0.0))
            const(pool.memset(u[:, :, IMG:], -1.0))

            pool.wait_ge(s["c_idx"], 1)
            for b in range(B):
                rows = pool.indirect_dma_start(h[:, b, :], None, d["emb"], bass.IndirectOffsetOnAxis(ap=tok_idx[:, b:b + 1], axis=0))
                rows.then_inc(s["g_emb_first" if b < 2 else "g_emb"], 16)
                if b == 1:
                    const(pool.memset(v[:], 0.0))
                    const(pool.memset(ones_pad[:], 0.0))
                    for o in range(2):
                        const(pool.memset(ones_pad[:, o, TKD * o:TKD * o + TKD], 1.0))
                    assert c == N_CONST

            pool.wait_ge(s["g_emb_first"], 32)
            pool.wait_ge(s["g_emb"], 16 * (B - 2))
            const(pool.memset(mask[:], 0.0))
            const(pool.tensor_copy(ident_h[:], ident[:]))
            for first in range(2):
                for half in range(2):
                    m = mask[64 * half:64 * half + 64, first]
                    const(pool.affine_select(out=m, in_=m, compare_op=ALU.is_gt, fill=MASKED, base=0, pattern=[[0, 4], [1, P]], channel_multiplier=-1))
                    const(pool.affine_select(out=m, in_=m, compare_op=ALU.is_ge, fill=MASKED, base=WIN, pattern=[[0, 4], [-1, P]], channel_multiplier=1))
                    if first and half == 0:
                        const(pool.affine_select(out=m, in_=m, compare_op=ALU.is_ge, fill=MASKED, base=-WIN, pattern=[[0, 4], [1, P]], channel_multiplier=0))
            const(pool.memset(v_f[:, :, :, HD:], 1.0))
            for t in (xnT[:, :, 0:WIN], kT_f[:, :, 0:WIN]):
                const(pool.memset(t, 0.0))
            assert c == N_CONST_ALL

            with pool.Fori(0, 2 * LAYERS * PAIRS) as n:
                pool.wait_ge(s["dve_stat"], n + 1)
                pool.tensor_tensor(var_eps[:, 0:2], mv[:, 0:2, 1], eps_c[:, 0:2], ALU.add).then_inc(s["pool_eps"], 1)
                pool.wait_ge(s["pool_eps"], n + 1)
                pool.tensor_tensor(rstd[:, 0:2], var_eps[:, 0:2], pow_half[:, 0:2], ALU.pow).then_inc(s["pool_rstd"], 1)
            with pool.Fori(0, 2 * B) as n:
                pool.wait_ge(s["f_stat"], n + 1)
                pool.tensor_tensor(var_eps[:], mv[:, :, 1], eps_c[:, 0:TT], ALU.add).then_inc(s["f_eps"], 1)
                pool.wait_ge(s["f_eps"], n + 1)
                pool.tensor_tensor(rstd[:], var_eps[:], pow_half[:, 0:TT], ALU.pow).then_inc(s["f_rstd"], 1)


        @block.tensor
        def _(pe_):
            mm, tr = pe_.matmul, pe_.transpose

            def filter_slot(l, k):
                if k % 2 == 0:
                    pe_.wait_ge(s["act_tanh"], ITERS * l + k // 2 + 1)
                    mm(halo[:, 0], up_shift[:], u[:, 0, 0:IMG], start=True, stop=False)
                    mm(halo[:, 0], edge[:], ones[0:1, 0:IMG], start=False, stop=True).then_inc(s["pe_halo"], 1)
                else:
                    pe_.wait_ge(s["dve_flux"], ITERS * l + k // 2 + 1)
                    mm(halo[:, 1], down_shift[:], p1[:, RPP - 1], start=True, stop=True).then_inc(s["pe_halo"], 1)

            def turn_h(l, place, bank):
                what, i = ORDER[place]
                pe_.wait_ge(s["h_ready"] if what == "A" else s["dve_ln1"], 4 * l + i + 1)
                for t in range(2):
                    for c in range(KC):
                        last = tr(bank[:, D * c + P * t:D * c + P * t + P], h[:, 2 * i + t, P * c:P * c + P], ident[:])
                last.then_inc(s["pe_hT"], 1)

            def scores(l, i, n):
                t, g = n // 2, n % 2
                if n == 0:
                    pe_.wait_ge(s["act_q"], 4 * l + i + 1)
                if n < 2:
                    pe_.wait_ge(s["act_k"], 8 * l + 2 * i + g + 1)
                for half in range(2):
                    last = mm(ps_s[g][:, 4 * half:4 * half + 4].rearrange("p h k -> p (h k)"), qT[:, g, P * t:P * t + P],
                              km[:, g, t, 4 * half:4 * half + 4].rearrange("p h k -> p (h k)"), start=True, stop=True)
                last.then_inc(s["pe_s"], 1)

            def turn_probs(l, i, n, done):
                pe_.wait_ge(s["act_exp"], 16 * l + 4 * i + n + 1)
                if n == 0:
                    pe_.wait_ge(s["dve_ff2"], 4 * l + done + 1)
                    pe_.wait_ge(s["dve_wc"], 4 * l + i + 1)
                for hh in range(HALF):
                    last = tr(t_heads[:, hh], prob[:, n % 2, hh], ident[:])
                last.then_inc(s["pe_pT"], 1)

            def attend(l, i, n):
                t, g = n // 2, n % 2
                pe_.wait_ge(s["act_pT"], 16 * l + 4 * i + n + 1)
                if n == 0:
                    pe_.wait_ge(s["act_v"], 4 * l + i + 1)
                for den in range(2):
                    for o in range(2):
                        for j in range(4):
                            hh = 2 * j + o
                            w = ones_pad[:, o] if den else v[:, t, HALF * g + hh]
                            last = mm(sums[t][32 * j:32 * j + 32, D * den + P * g:D * den + P * g + P], w, probT[:, hh],
                                      start=(o == 0), stop=(o == 1), skip_group_check=True)
                if g == 1:
                    last.then_inc(s["pe_o"], 1)

            def project(dst, w, m):
                for c in range(KC):
                    last = mm(dst, w_attn[:, c, D * w + P * m:D * w + P * m + P], hT[:, c], start=(c == 0), stop=(c == KC - 1))
                return last

            def ff1(l, i, ms):
                for m in ms:
                    for c in range(KC):
                        last = mm(quad[(m // 2 + 1) % 4][:, D * (m % 2):D * (m % 2) + D], w1[:, c, P * m:P * m + P], hT[:, c], start=(c == 0), stop=(c == KC - 1))
                    if m % 2:
                        last.then_inc(s["pe_ff1"], 1)

            def head(l, place):
                what, i = ORDER[place]
                pe_.wait_ge(s["act_hT"], 8 * l + place + 1)
                if what == "A":
                    if i == 0:
                        pe_.wait_ge(s["l_attn"], 16 * l + 16)
                    project(quad[2][:, 0:D], 1, 0).then_inc(s["pe_k"], 1)
                    project(quad[1][:, 0:D], 0, 0)
                    project(quad[1][:, D:2 * D], 0, 1).then_inc(s["pe_q"], 1)
                else:
                    if i == 0:
                        pe_.wait_ge(s["l_w1"], 16 * l + 16)
                    ff1(l, i, range(4))

            def part_a(l, i, place, done, slot, after_f):
                if place == 0 or after_f:
                    head(l, place)
                if place == 0 or after_f:
                    filter_slot(l, slot)
                project(quad[3][:, 0:D], 1, 1).then_inc(s["pe_k"], 1)
                for t in range(2):
                    for c in range(KC):
                        last = mm(ps_m[:, D * t:D * t + D], hT[:, c, P * t:P * t + P], w_attn[:, c, 2 * D:3 * D], start=(c == 0), stop=(c == KC - 1))
                last.then_inc(s["pe_v"], 1)
                scores(l, i, 0)
                scores(l, i, 1)
                filter_slot(l, slot + 1)
                turn_probs(l, i, 0, done)
                scores(l, i, 2)
                attend(l, i, 0)
                turn_probs(l, i, 1, done)
                scores(l, i, 3)
                attend(l, i, 1)
                filter_slot(l, slot + 2)
                turn_probs(l, i, 2, done)
                attend(l, i, 2)
                turn_probs(l, i, 3, done)
                turn_h(l, place + 1, quad[3])
                attend(l, i, 3)
                filter_slot(l, slot + 3)
                head(l, place + 1)
                pe_.wait_ge(s["dve_attn"], 8 * l + 2 * i + 2)
                for t in range(2):
                    for c in range(KC):
                        last = mm(ps_t[:, 1, D * t:D * t + D], attnT[:, c, P * t:P * t + P], w_attn[:, c, 3 * D:4 * D], start=(c == 0), stop=(c == KC - 1))
                last.then_inc(s["pe_wc"], 1)

            def part_f(l, i, place, slot, after_f):
                if after_f:
                    filter_slot(l, slot)
                    turn_h(l, place, ps_m)
                    head(l, place)
                ff1(l, i, range(4, MC))
                filter_slot(l, slot + 1)
                if place + 1 < len(ORDER) and ORDER[place + 1][0] == "A":
                    turn_h(l, place + 1, ps_m)
                if i == 0:
                    pe_.wait_ge(s["l_w2"], 16 * l + 16)
                pe_.wait_ge(s["dve_ff2"], 4 * l + i + 1)
                if i == 0:
                    pe_.wait_ge(s["l_vec"], 16 * l + 16)
                for t in range(2):
                    mm(ps_t[:, 0, D * t:D * t + D], ones[0:1, 0:P], vecs[0:1, 2], start=True, stop=False)
                    for m in range(MC):
                        if t == 0 and m % 2 == 0:
                            pe_.wait_ge(s["act_ff1"], 16 * l + 4 * i + m // 2 + 1)
                        last = mm(ps_t[:, 0, D * t:D * t + D], hidT[:, m, P * t:P * t + P], w2[:, m], start=False, stop=(m == MC - 1))
                last.then_inc(s["pe_ff2"], 1)

            pe_.wait_ge(s["c_pool"], N_CONST)
            with pe_.Fori(0, LAYERS) as l:
                turn_h(l, 0, ps_m)
                slot = done = 0
                for place, (what, i) in enumerate(ORDER):
                    after_f = place > 0 and ORDER[place - 1][0] == "F"
                    if what == "A":
                        part_a(l, i, place, done, slot, after_f)
                    else:
                        part_f(l, i, place, slot, after_f)
                        done += 1
                    slot += SLOTS_IN[what]

            def tile_scores(n, t):
                bank = ps_s[t % 2]
                if t == 2:
                    pe_.wait_ge(s["f_exp"], TT * n + 1)
                m = mask[:, 1 if t == 0 else 0].rearrange("p a k -> p (a k)")
                for hb in range(2):
                    flat = bank[:, 4 * hb:4 * hb + 4].rearrange("p h k -> p (h k)")
                    mm(flat, ident_h[:], m, start=True, stop=False, skip_group_check=True)
                    for hh in range(4 * hb, 4 * hb + 4):
                        r, c = hh % 4, hh // 4
                        for half in range(2):
                            at = P * t + WIN * half
                            last = mm(bank[WIN * half:WIN * half + WIN, hh], qz[:, r, c, at:at + WIN], kT_f[:, c, at:at + P],
                                      start=False, stop=(hh % 4 == 3), skip_group_check=True)
                last.then_inc(s["f_s"], 1)

            def tile_turn(n, t):
                pe_.wait_ge(s["f_exp_4"], TT * n + t + 1)
                if t == 0:
                    pe_.wait_ge(s["f_v"], n + 1)
                for hh in range(FH):
                    if hh == 4:
                        pe_.wait_ge(s["f_exp"], TT * n + t + 1)
                    last = tr(t_heads[:, hh], prob[:, t % 2, hh], ident[:])
                    if hh == 3:
                        last.then_inc(s["f_pT_ps_4"], 1)
                last.then_inc(s["f_pT_ps"], 1)

            def tile_attend(n, t):
                pe_.wait_ge(s["f_pT"], TT * n + t + 1)
                if t:
                    pe_.wait_ge(s["f_attn"], TT * n + t)
                for hh in range(FH):
                    for half in range(2):
                        last = mm(ps_m[WIN * half:WIN * half + WIN, 33 * hh:33 * hh + 33], probT[:, hh, WIN * half:WIN * half + WIN],
                                  v_f[:, 2 * t + half, hh // 4], start=True, stop=True)
                last.then_inc(s["f_o"], 1)

            def turn_rows(n, src, made, done):
                pe_.wait_ge(made, n + 1)
                for c in range(KC):
                    for t in range(TT):
                        last = tr(quad[2 + c][:, P * t:P * t + P], src[:, t, P * c:P * c + P], ident[:])
                last.then_inc(done, 1)

            def turn_x(n):
                turn_rows(n, xn, s["f_xn"], s["f_xnT_ps"])

            def turn_x2(n, j):
                turn_rows(n, xn2[:, j], s["f_xn2"], s["f_xn2T_ps"])

            def fuse_a(n, j):
                pe_.wait_ge(s["f_xnT"], n + 1)
                for m in range(KC):
                    for c in range(KC):
                        last = mm(quad[m][:, 0:TOK], wq_f[:, c, P * m:P * m + P], xnT[:, c, WIN:], start=(c == 0), stop=(c == KC - 1))
                last.then_inc(s["f_q_ps"], 1)
                for m in range(FKV):
                    for c in range(KC):
                        last = mm(quad[2 + m][:, 0:TOK], wk_f[:, c, m], xnT[:, c, WIN:], start=(c == 0), stop=(c == KC - 1))
                last.then_inc(s["f_k_ps"], 1)
                pe_.wait_ge(s["f_z"], n - j + 1)
                pe_.wait_ge(s["f_y"], n + 1)
                for w in range(2 * TT):
                    for c in range(KC):
                        last = mm(ps_t[:, 0, 64 * w:64 * w + 64], xnT[:, c, WIN * w:WIN * w + P], wv_f[:, c], start=(c == 0), stop=(c == KC - 1))
                last.then_inc(s["f_v_ps"], 1)
                pe_.wait_ge(s["f_q"], n + 1)
                pe_.wait_ge(s["f_k"], n + 1)
                tile_scores(n, 0)
                tile_scores(n, 1)
                tile_turn(n, 0)
                tile_scores(n, 2)
                tile_attend(n, 0)
                tile_turn(n, 1)
                tile_attend(n, 1)
                tile_turn(n, 2)
                tile_attend(n, 2)
                if j == 0:
                    turn_x(n + 1)
                else:
                    turn_x2(n - 1, 0)
                pe_.wait_ge(s["f_attn"], TT * n + TT)
                for c in range(KC):
                    bank = ps_m if c == 0 else halo_flat
                    for t in range(TT):
                        last = tr(bank[:, P * t:P * t + P], attn_f[:, t, P * c:P * c + P], ident[:])
                last.then_inc(s["f_oT_ps"], 1)
                pe_.wait_ge(s["f_oT"], n + 1)
                for t in range(TT):
                    for c in range(KC):
                        last = mm(t_flat[:, D * t:D * t + D], attnT_f[:, c, P * t:P * t + P], wo_f[:, c], start=(c == 0), stop=(c == KC - 1))
                last.then_inc(s["f_y_ps"], 1)

            def fuse_f(n, j, last_two):
                pe_.wait_ge(s["f_xn2T"], n + 1)
                for m in range(MC):
                    if m >= 4:
                        pe_.wait_ge(s["f_relu"], MC * n + m - 3)
                    for c in range(KC):
                        last = mm(quad[m % 4][:, 0:TOK], w_fc[:, c, P * m:P * m + P], xn2T[:, c], start=(c == 0), stop=(c == KC - 1))
                    last.then_inc(s["f_h_ps"], 1)
                pe_.wait_ge(s["f_y"], n + 3 - j)
                for t in range(TT):
                    for m in range(MC):
                        if t == 0:
                            pe_.wait_ge(s["f_sq"], MC * n + m + 1)
                        if t == 0 and m == 0 and j == 1:
                            pe_.wait_ge(s["f_z"], n + 1)
                        last = mm(t_flat[:, D * t:D * t + D], hid_f[:, m, P * t:P * t + P], w_pr[:, m], start=(m == 0), stop=(m == MC - 1))
                    if t == 1:
                        last.then_inc(s["f_z_ps_2"], 1)
                    if t == 0 and j == 0:
                        turn_x2(n + 1, 1)
                    if t == 1 and j == 1 and not last_two:
                        turn_x(n + 1)
                last.then_inc(s["f_z_ps"], 1)

            pe_.wait_ge(s["l_fus"], 16 * 11)
            pe_.wait_ge(s["c_pool"], N_CONST_ALL)
            def two_batches(g, last_two):
                for j in range(2):
                    fuse_a(2 * g + j, j)
                for j in range(2):
                    fuse_f(2 * g + j, j, last_two)

            turn_x(0)
            with pe_.Fori(0, B // 2 - 1) as g:
                two_batches(g, False)
            two_batches(B // 2 - 1, True)

        @block.scalar
        def _(act):
            A = act.activation
            pending = []

            def flush():
                while pending:
                    pending.pop(0)()

            def filter_slot(l, k):
                if k % 2 == 0:
                    return

                def later():
                    act.wait_ge(s["dve_div"], ITERS * l + k // 2 + 1)
                    if k < SLOTS - 1:
                        A(u[:, :, 0:IMG], fa, ACT.Tanh).then_inc(s["act_tanh"], 1)
                    else:
                        act.wait_ge(s["st_img"], 16 * l + 16)
                        A(f_out[:], fa, ACT.Copy, scale=2.0).then_inc(s["act_img"], 1)
                pending.append(later)

            def exps(l, i, n):
                act.wait_ge(s["dve_max"], 16 * l + 4 * i + n + 1)
                for hh in range(HALF):
                    last = A(prob[:, n % 2, hh], ps_s[n % 2][:, hh], ACT.Exp, scale=-1.0, bias=neg_max[:, n % 2, hh:hh + 1])
                last.then_inc(s["act_exp"], 1)

            def probs_out(l, i, n):
                act.wait_ge(s["pe_pT"], 16 * l + 4 * i + n + 1)
                A(probT[:].rearrange("p h k -> p (h k)"), t_flat, ACT.Copy).then_inc(s["act_pT"], 1)

            def h_out(l, place, bank):
                act.wait_ge(s["pe_hT"], 8 * l + place + 1)
                A(hT[:].rearrange("p c n -> p (c n)"), bank, ACT.Copy).then_inc(s["act_hT"], 1)

            def keys_out(l, i, g):
                act.wait_ge(s["pe_k"], 8 * l + 2 * i + g + 1)
                for hh in range(HALF):
                    last = A(km[:, g, :, hh], quad[2 + g][:, 0:D].rearrange("p (t k) -> p t k", t=2), ACT.Copy, scale=head_mask[:, hh:hh + 1])
                last.then_inc(s["act_k"], 1)

            def part_a(l, i, place, slot):
                n = 4 * l + i + 1
                keys_out(l, i, 0)
                act.wait_ge(s["pe_q"], n)
                A(qT[:].rearrange("p c n -> p (c n)"), quad[1], ACT.Copy, scale=-SCALE_T).then_inc(s["act_q"], 1)
                flush()
                keys_out(l, i, 1)
                act.wait_ge(s["pe_v"], n)
                for t in range(2):
                    src = ps_m[:, D * t:D * t + D].rearrange("p (j o k) -> p j o k", o=2, k=TKD)
                    dst = v[:, t].rearrange("p (j o) k -> p j o k", o=2)
                    for o in range(2):
                        last = A(dst[:, :, o, TKD * o:TKD * o + TKD], src[:, :, o], ACT.Copy)
                last.then_inc(s["act_v"], 1)
                filter_slot(l, slot)
                flush()
                exps(l, i, 0)
                exps(l, i, 1)
                probs_out(l, i, 0)
                probs_out(l, i, 1)
                filter_slot(l, slot + 1)
                flush()
                exps(l, i, 2)
                if slot % 2:
                    probs_out(l, i, 2)
                    exps(l, i, 3)
                else:
                    exps(l, i, 3)
                    probs_out(l, i, 2)
                probs_out(l, i, 3)
                h_out(l, place + 1, quad[3])
                filter_slot(l, slot + 2)
                flush()

            def part_f(l, i, place, slot):
                act.wait_ge(s["l_bc"], 16 * l + 16)
                for m in range(MC):
                    if m == 4:
                        flush()
                    if m % 2 == 0:
                        act.wait_ge(s["pe_ff1"], 16 * l + 4 * i + m // 2 + 1)
                    last = A(hidT[:, m], quad[(m // 2 + 1) % 4][:, D * (m % 2):D * (m % 2) + D], ACT.Relu, bias=b1[:, m:m + 1])
                    if m % 2:
                        last.then_inc(s["act_ff1"], 1)
                filter_slot(l, slot)
                flush()
                next_a = place + 1 < len(ORDER) and ORDER[place + 1][0] == "A"
                if next_a:
                    h_out(l, place + 1, ps_m[:])
                filter_slot(l, slot + 1)
                flush()
                if place + 1 < len(ORDER) and not next_a:
                    h_out(l, place + 1, ps_m[:])

            act.wait_ge(s["c_general"], 1)
            with act.If(act.value_load(general[0:1, 0:1], min_val=0, max_val=1) > 0):
                own = gen_u[:, 1:3, 1:IMG + 1]

                def sigmoid(src, count):
                    act.wait_ge(s["gen_u_done"], count)
                    A(own, src, ACT.Tanh).then_inc(s["gen_tanh"], 1)
                    act.wait_ge(s["gen_tanh"], count)
                    A(own, own, ACT.Copy, scale=0.5, bias=0.5).then_inc(s["gen_u_done"], 1)

                act.wait_ge(s["gen_zero"], 1)
                with act.Fori(0, B) as b:
                    act.wait_ge(s["gen_o_in"], 16 * b + 16)
                    sigmoid(gen_o, (ITERS + 1) * b + 1)
                    with act.Fori(0, ITERS) as it:
                        act.wait_ge(s["gen_div"], ITERS * b + it + 1)
                        sigmoid(gen_w, (ITERS + 1) * b + it + 2)
                act.wait_ge(s["gen_out"], B)
                act.wait_ge(s["gen_st"], 16 * B)

            act.wait_ge(s["c_pool"], N_CONST)
            act.wait_ge(s["l_img"], 16 * 5)
            act.wait_ge(s["c_scaled"], 1)
            with act.Fori(0, LAYERS) as l:
                h_out(l, 0, ps_m[:])
                A(u[:, :, 0:IMG], o_all[:, bass.ds(l, 1)].rearrange("p a r c -> p (a r) c"), ACT.Tanh).then_inc(s["act_tanh"], 1)
                slot = 0
                for place, (what, i) in enumerate(ORDER):
                    (part_a if what == "A" else part_f)(l, i, place, slot)
                    slot += SLOTS_IN[what]
                flush()
                act.wait_ge(s["l_img_rest"], 16 * (PAIRS - 1))

            act.wait_ge(s["c_pool"], N_CONST_ALL)

            def tile_exps(n, t):
                act.wait_ge(s["f_max"], TT * n + t + 1)
                for hh in range(FH):
                    last = A(prob[:, t % 2, hh], ps_s[t % 2][:, hh], ACT.Exp, bias=neg_max[:, t, hh:hh + 1])
                    if hh == 3:
                        last.then_inc(s["f_exp_4"], 1)
                last.then_inc(s["f_exp"], 1)
                A(sink_e[:, t], neg_max[:, t], ACT.Exp, bias=sink[:]).then_inc(s["f_sink"], 1)

            def tile_probs(n, t):
                for half, made in enumerate((s["f_pT_ps_4"], s["f_pT_ps"])):
                    act.wait_ge(made, TT * n + t + 1)
                    last = A(probT[:, 4 * half:4 * half + 4].rearrange("p h k -> p (h k)"), ps_t[:, half], ACT.Copy)
                last.then_inc(s["f_pT"], 1)

            def halves(dst, src, n_sem, n, done):
                act.wait_ge(n_sem, n + 1)
                A(dst[0], src[0][:, 0:TOK], ACT.Copy)
                A(dst[1], src[1][:, 0:TOK], ACT.Copy).then_inc(done, 1)

            def x_out(n):
                halves([xnT[:, c, WIN:] for c in range(KC)], quad[2:4], s["f_xnT_ps"], n, s["f_xnT"])

            def x2_out(n):
                halves([xn2T[:, c] for c in range(KC)], quad[2:4], s["f_xn2T_ps"], n, s["f_xn2T"])

            def fuse_a(n, j):
                act.wait_ge(s["f_q_ps"], n + 1)
                for m in range(KC):
                    for r in range(4):
                        last = A(qz[:, r, m], quad[m][:, 0:TOK], ACT.Identity, scale=row_mask[:, r:r + 1], bias=bq_m[:, m, r:r + 1])
                last.then_inc(s["f_q"], 1)
                act.wait_ge(s["f_k_ps"], n + 1)
                for m in range(FKV):
                    last = A(kT_f[:, m, WIN:], quad[2 + m][:, 0:TOK], ACT.Identity, bias=bk_f[:, m:m + 1])
                last.then_inc(s["f_k"], 1)
                tile_exps(n, 0)
                tile_exps(n, 1)
                tile_probs(n, 0)
                tile_probs(n, 1)
                tile_exps(n, 2)
                tile_probs(n, 2)
                if j == 0:
                    x_out(n + 1)
                else:
                    x2_out(n - 1)
                halves([attnT_f[:, c] for c in range(KC)], [ps_m, halo_flat], s["f_oT_ps"], n, s["f_oT"])

            def fuse_f(n, j, last_two):
                for m in range(MC + j):
                    if m < MC:
                        act.wait_ge(s["f_h_ps"], MC * n + m + 1)
                        A(hid_f[:, m], quad[m % 4][:, 0:TOK], ACT.Relu).then_inc(s["f_relu"], 1)
                    if j and m:
                        act.wait_ge(s["f_relu"], MC * n + m)
                        A(hid_f[:, m - 1], hid_f[:, m - 1], ACT.Square).then_inc(s["f_sq"], 1)
                act.wait_ge(s["f_out"], n + 1)
                act.wait_ge(s["f_z_ps_2"], n + 1)
                A(y_in[:, j, 0:2 * D], t_flat[:, 0:2 * D], ACT.Copy).then_inc(s["f_z_2"], 1)
                if j == 0:
                    x2_out(n + 1)
                elif not last_two:
                    x_out(n + 1)
                act.wait_ge(s["f_z_ps"], n + 1)
                A(y_in[:, j, 2 * D:], t_flat[:, 2 * D:TT * D], ACT.Copy).then_inc(s["f_z"], 1)

            def two_batches(g, last_two):
                for j in range(2):
                    fuse_a(2 * g + j, j)
                for j in range(2):
                    fuse_f(2 * g + j, j, last_two)

            x_out(0)
            act.wait_ge(s["c_scaled"], 3)
            with act.Fori(0, B // 2 - 1) as g:
                two_batches(g, False)
            two_batches(B // 2 - 1, True)

        @block.vector
        def _(dve):
            chain = [0]

            def tick(ins):
                chain[0] += 1
                ins.then_inc(s["chain"], 1)
                return chain[0]

            def link(ins):
                dve.wait_ge(s["chain"], tick(ins))

            def restart():
                dve.wait_ge(s["chain"], chain[0])
                dve.sem_clear(s["chain"])
                chain[0] = 0

            tt, ts, stt = dve.tensor_tensor, dve.tensor_scalar, dve.scalar_tensor_tensor

            for free in (s["dve_ff2"], s["dve_wc"], s["f_z"], s["f_y"]):
                dve.sem_inc(free, 1)
            for free in (s["st_img"], s["st_out"]):
                dve.sem_inc(free, 16)
            dve.sem_inc(s["f_out"], 2)

            dve.wait_ge(s["l_tok"], 32)
            link(dve.tensor_copy(tok_f[:], tokens[:]))
            link(ts(tok_f[:], tok_f[:], float(-VOCAB), float(VOCAB - 1), ALU.max, ALU.min))
            link(ts(tok_neg[:], tok_f[:], 0.0, float(VOCAB), ALU.is_lt, ALU.mult))
            tt(tok_idx[:], tok_f[:], tok_neg[:], ALU.add).then_inc(s["c_idx"], 1)

            link(dve.memset(taps_std[:], 0.0))
            for at, val in ((4, -1.0), (7, 1.0), (13, -1.0), (14, 1.0), (19, -1.0), (22, 1.0), (30, -1.0), (31, 1.0)):
                link(dve.memset(taps_std[:, at:at + 1], val))
            dve.wait_ge(s["l_taps"], 32)
            link(tt(taps_diff[:], taps[:], taps_std[:], ALU.not_equal))
            link(dve.tensor_reduce(general_f[:], taps_diff[:], AX.X, ALU.max))
            dve.tensor_copy(general[:], general_f[:]).then_inc(s["c_general"], 1)
            dve.wait_ge(s["c_general"], 1)
            restart()
            with dve.If(dve.value_load(general[0:1, 0:1], min_val=0, max_val=1) > 0):
                def taps9(dst, src, at, more):
                    for k in range(9):
                        view = src[:, k // 3:k // 3 + 2, k % 3:k % 3 + IMG]
                        if k == 0 and not more:
                            link(ts(dst, view, taps[:, at:at + 1], None, ALU.mult))
                        else:
                            link(stt(dst, view, taps[:, at + k:at + k + 1], dst, ALU.mult, ALU.add))

                dve.sem_inc(s["gen_free"], 1)
                dve.sem_inc(s["gen_u_done"], 1)
                for t in (*gen_p, gen_u):
                    last = dve.memset(t, 0.0)
                    tick(last) if t is not gen_u else last.then_inc(s["gen_zero"], 1)
                dve.wait_ge(s["gen_zero"], 1)
                dve.wait_ge(s["gen_vf_in"], 32)
                restart()
                with dve.Fori(0, B) as b:
                    dve.wait_ge(s["gen_o_in"], 16 * b + 16)
                    link(dve.memset(gen_q, 0.0))
                    restart()
                    with dve.Fori(0, ITERS) as it:
                        n = ITERS * b + it + 1
                        dve.wait_ge(s["gen_halo_u"], 32 * n)
                        for k in range(2):
                            taps9(gen_g[k], gen_u, 9 * k, False)
                            link(tt(gen_g[k], gen_g[k], gen_vf[k], ALU.mult))
                        link(tt(gen_g[0], gen_g[0], gen_g[1], ALU.add))
                        link(stt(gen_q, gen_g[0], -0.5, gen_q, ALU.mult, ALU.add))
                        link(ts(gen_q, gen_q, 0.0, None, ALU.max))
                        tick(tt(gen_p[0][:, 1:3, 1:IMG + 1], gen_q, gen_vf[0], ALU.mult))
                        tt(gen_p[1][:, 1:3, 1:IMG + 1], gen_q, gen_vf[1], ALU.mult).then_inc(s["gen_flux"], 1)
                        dve.wait_ge(s["gen_halo_p"], 64 * n)
                        taps9(gen_t, gen_p[0], 18, False)
                        taps9(gen_t, gen_p[1], 27, True)
                        tt(gen_w, gen_o, gen_t, ALU.subtract).then_inc(s["gen_div"], 1)
                        restart()
                    dve.wait_ge(s["gen_u_done"], (ITERS + 1) * (b + 1) + 1)
                    ts(gen_w, gen_w, 2.0, None, ALU.mult).then_inc(s["gen_out"], 1)
                    dve.wait_ge(s["gen_st"], 16 * b + 16)
                    dve.sem_inc(s["gen_free"], 1)

            dve.wait_ge(s["l_img"], 16 * 5)
            link(ts(vq[:], vf[:], 0.25, None, ALU.mult))
            dve.wait_ge(s["c_pool"], N_CONST)
            for hh in range(HALF):
                tick(dve.tensor_reduce(head_mask[:, hh:hh + 1], ident[:, TKD * hh:TKD * hh + TKD], AX.X, ALU.add))
            for r in range(4):
                tick(dve.tensor_reduce(row_mask[:, r:r + 1], ident[:, 32 * r:32 * r + 32], AX.X, ALU.add))
            dve.wait_ge(s["chain"], chain[0])
            ts(row_mask[:], row_mask[:], SCALE_F, None, ALU.mult).then_inc(s["c_scaled"], 1)
            dve.wait_ge(s["c_scaled"], 1)
            pe_rows = pe[:].unsqueeze(1)
            dve.wait_ge(s["g_emb_first"], 32)
            tt(h[:, 0:2], h[:, 0:2], pe_rows.to_broadcast([P, 2, D]), ALU.add).then_inc(s["h_ready"], 1)
            dve.wait_ge(s["g_emb"], 16 * (B - 2))
            tt(h[:, 2:], h[:, 2:], pe_rows.to_broadcast([P, B - 2, D]), ALU.add).then_inc(s["h_ready"], 3)
            dve.wait_ge(s["h_ready"], 4)

            p0_done = [0]

            def flux(l, k, between=lambda: None):
                dve.wait_ge(s["pe_halo"], SLOTS * l + k + 1)
                tt(fa[:, 0:RPP - 1], u[:, 1:RPP, 0:IMG], u[:, 0:RPP - 1, 0:IMG], ALU.subtract)
                ta = tick(tt(fa[:, RPP - 1], halo[:, 0], u[:, RPP - 1, 0:IMG], ALU.subtract))
                tb = tick(tt(fb, u[:, :, 1:], u[:, :, 0:IMG], ALU.subtract))
                dve.wait_ge(s["chain"], ta)
                tick(tt(fa, fa, vq[:, 0], ALU.mult))
                dve.wait_ge(s["chain"], tb)
                ta = chain[0]
                flux_b = tick(tt(fb, fb, vq[:, 1], ALU.mult))
                between()
                dve.wait_ge(s["chain"], ta)
                link(stt(q_st, q_st, 0.0, fa, ALU.max, ALU.subtract))
                dve.wait_ge(s["chain"], flux_b)
                link(tt(q_st, q_st, fb, ALU.subtract))
                stt(p1[:], q_st, 0.0, vf[:, 0], ALU.max, ALU.mult).then_inc(s["dve_flux"], 1)
                p0_done[0] = tick(stt(p0[:, :, 1:], q_st, 0.0, vf[:, 1], ALU.max, ALU.mult))
                dve.wait_ge(s["dve_flux"], ITERS * l + k // 2 + 1)

            def divergence(l, k):
                tick(tt(fa[:, 1:RPP], p1[:, 1:RPP], p1[:, 0:RPP - 1], ALU.subtract))
                dve.wait_ge(s["chain"], p0_done[0])
                tick(tt(fb, p0[:, :, 1:], p0[:, :, 0:IMG], ALU.subtract))
                dve.wait_ge(s["pe_halo"], SLOTS * l + k + 1)
                link(tt(fa[:, 0], p1[:, 0], halo[:, 1], ALU.subtract))
                link(tt(fa, fa, fb, ALU.add))
                tt(fa, o_all[:, bass.ds(l, 1)].rearrange("p a r c -> p (a r) c"), fa, ALU.subtract).then_inc(s["dve_div"], 1)

            def filter_slot(l, k, between=lambda: None):
                if k % 2 == 0:
                    flux(l, k, between)
                else:
                    divergence(l, k)
                    between()

            def head_max(l, i, n):
                dve.wait_ge(s["pe_s"], 16 * l + 4 * i + n + 1)
                dve.tensor_reduce(neg_max[:, n % 2], ps_s[n % 2][:], AX.X, ALU.min).then_inc(s["dve_max"], 1)

            def normalise(l, i, t):
                dve.wait_ge(s["pe_o"], 8 * l + 2 * i + t + 1)
                nums, dens = (sums[t][:, D * k:D * k + D].rearrange("p (c n) -> p c n", c=KC) for k in range(2))
                link(dve.reciprocal(rden[:, t], dens))
                tt(attnT[:, :, P * t:P * t + P], nums, rden[:, t], ALU.mult).then_inc(s["dve_attn"], 1)

            def moments(src, n, done):
                for t in range(n):
                    tick(dve.bn_stats(stats[:, t], src[:, t]))
                dve.wait_ge(s["chain"], chain[0])
                for t in range(n):
                    last = dve.bn_aggr(mv[:, t], stats[:, t])
                    tick(last) if t < n - 1 else last.then_inc(done, 1)

            def text_residual(n, i, ps_in, freed):
                hp = h[:, 2 * i:2 * i + 2]
                tt(hp, ps_in.rearrange("p (t n) -> p t n", t=2), hp, ALU.add).then_inc(freed, 1)
                dve.wait_ge(freed, n + 1)
                return hp

            def norm_start(l, what, i, order):
                n = 4 * l + i + 1
                if what == "A":
                    dve.wait_ge(s["pe_wc"], n)
                    hp = text_residual(n, i, ps_t[:, 1], s["dve_wc"])
                else:
                    dve.wait_ge(s["pe_ff2"], n)
                    dve.wait_ge(s["dve_ln1"], n)
                    hp = text_residual(n, i, ps_t[:, 0], s["dve_ff2"])
                moments(hp, 2, s["dve_stat"])

                def norm_end():
                    dve.wait_ge(s["dve_stat"], 8 * l + order)
                    dve.wait_ge(s["pool_rstd"], 8 * l + order)
                    gain, bias, done = (0, 1, s["dve_ln1"]) if what == "A" else (3, 4, s["h_ready"])
                    dve.wait_ge(s["l_vec"], 16 * l + 16)
                    scaled = [tick(stt(hp[:, t], hp[:, t], mv[:, t, 0:1], vecs[:, gain], ALU.subtract, ALU.mult)) for t in range(2)]
                    for t in range(2):
                        dve.wait_ge(s["chain"], scaled[t])
                        last = stt(hp[:, t], hp[:, t], rstd[:, t:t + 1], vecs[:, bias], ALU.mult, ALU.add)
                        tick(last) if t == 0 else last.then_inc(done, 1)
                return norm_end

            restart()
            with dve.Fori(0, LAYERS) as l:
                link(dve.memset(q_st, 0.0))
                slot = 0
                norm_end = None
                for place, (what, i) in enumerate(ORDER):
                    before, i_before = ORDER[place - 1] if place else (None, None)
                    early = what == "A" and slot % 2 == 0
                    filter_slot(l, slot, (lambda: head_max(l, i, 0)) if early else lambda: None)
                    if before == "A":
                        norm_end = norm_start(l, before, i_before, place)
                    elif before == "F":
                        norm_end()
                    if what == "A":
                        if not early:
                            head_max(l, i, 0)
                        if before == "A":
                            norm_end()
                        head_max(l, i, 1)
                        filter_slot(l, slot + 1, lambda: head_max(l, i, 2))
                        head_max(l, i, 3)
                        filter_slot(l, slot + 2)
                        normalise(l, i, 0)
                        normalise(l, i, 1)
                    else:
                        next_f = place + 1 < len(ORDER) and ORDER[place + 1][0] == "F"
                        if before == "A" and next_f:
                            norm_end()
                        filter_slot(l, slot + 1)
                        if before == "A" and not next_f:
                            norm_end()
                        norm_end = norm_start(l, what, i, place + 1)
                    slot += SLOTS_IN[what]
                norm_end()
                restart()
                dve.wait_ge(s["l_img_rest"], 16 * (PAIRS - 1))

            def order_of(g, j, which):
                return 4 * g + {("x", 0): 1, ("x", 1): 2, ("res", 0): 3, ("res", 1): 4}[which, j]

            def joined_norm(n, src, dst, count, done):
                moments(src, TT, s["f_stat"])
                dve.wait_ge(s["f_stat"], count)
                dve.wait_ge(s["f_rstd"], count)
                for t in range(TT):
                    last = ts(dst[:, t], src[:, t], mv[:, t, 0:1], rstd[:, t:t + 1], ALU.subtract, ALU.mult)
                    tick(last) if t < TT - 1 else last.then_inc(done, 1)

            def tile_max(n, t):
                dve.wait_ge(s["f_s"], TT * n + t + 1)
                link(dve.tensor_reduce(rmax[:, t % 2], ps_s[t % 2][:], AX.X, ALU.max))
                ts(neg_max[:, t], rmax[:, t % 2], sink[:], -1.0, ALU.max, ALU.mult).then_inc(s["f_max"], 1)

            def tile_normalise(n, t):
                dve.wait_ge(s["f_o"], TT * n + t + 1)
                dve.wait_ge(s["f_sink"], TT * n + t + 1)
                o = ps_m[:, 0:33 * FH].rearrange("p (h k) -> p h k", h=FH)
                link(tt(den[:].unsqueeze(2), o[:, :, HD:], sink_e[:, t].unsqueeze(2), ALU.add))
                link(dve.reciprocal(rden_f[:], den[:]))
                tt(attn_f[:, t].rearrange("p (h k) -> p h k", h=FH), o[:, :, 0:HD], rden_f[:].unsqueeze(2).to_broadcast([P, FH, HD]), ALU.mult).then_inc(s["f_attn"], 1)

            def prepare(g, n, j):
                dve.wait_ge(l_x[j], 16 * g + 16)
                ts(x[:, j, 2], h[:, bass.ds(n, 1)].rearrange("p a n -> p (a n)"), 1.0, None, ALU.mult).then_inc(s["f_xt"], 1)
                dve.wait_ge(s["f_xt"], n + 1)
                joined_norm(n, x[:, j], xn, order_of(g, j, "x"), s["f_xn"])

            def fuse_a(g, n, j):
                tile_max(n, 0)
                dve.wait_ge(s["f_v_ps"], n + 1)
                tt(v_f[:, :, :, 0:HD], ps_t[:, 0, 0:64 * 2 * TT].rearrange("p (w j k) -> p w j k", w=2 * TT, j=FKV),
                   bv_f[:].rearrange("p (j k) -> p j k", j=FKV).unsqueeze(1).to_broadcast([P, 2 * TT, FKV, HD]), ALU.add).then_inc(s["f_v"], 1)
                tile_max(n, 1)
                tile_max(n, 2)
                tile_normalise(n, 0)
                if j == 0:
                    dve.wait_ge(s["f_xnT_ps"], n + 1)
                    prepare(g, n + 1, 1)
                tile_normalise(n, 1)
                tile_normalise(n, 2)
                dve.wait_ge(s["f_y_ps"], n + 1)
                dve.wait_ge(s["st_out"], 32 * g + 16)
                rj = res[:, j]
                tt(rj, t_flat[:, 0:TT * D].rearrange("p (t n) -> p t n", t=TT), x[:, j], ALU.add).then_inc(s["f_y"], 1)
                dve.wait_ge(s["f_y"], n + 2)
                link(tt(rj, rj, bo_f[:].unsqueeze(1).to_broadcast([P, TT, D]), ALU.add))
                joined_norm(n, rj, xn2[:, j], order_of(g, j, "res"), s["f_xn2"])

            def squares(n):
                for m in range(MC):
                    dve.wait_ge(s["f_relu"], MC * n + m + 1)
                    tt(hid_f[:, m], hid_f[:, m], hid_f[:, m], ALU.mult).then_inc(s["f_sq"], 1)

            def spike_steps(n, j, cols, done):
                y, m0, m1, spk = y_in[:, j, cols], mem[:, cols], mem_t[:, cols], spikes[:, cols]
                rj = res[:, j].rearrange("p t n -> p (t n)")[:, cols]
                tick(ts(spk, y, 1.0, None, ALU.is_gt))
                for step in range(1, STEPS):
                    was = y if step == 1 else m0
                    link(stt(m1, was, 0.9, y, ALU.mult, ALU.add))
                    link(stt(m0, was, 1.0, m1, ALU.is_gt, ALU.subtract, reverse1=True))
                    link(stt(spk, m0, 1.0, spk, ALU.is_gt, ALU.add))
                last = stt(rj, spk, 1.0 / STEPS, rj, ALU.mult, ALU.add)
                last.then_inc(s["f_out"], 1) if done else tick(last)

            def count_spikes(n, j):
                dve.wait_ge(s["f_out"], n + 2)
                if j == 0:
                    dve.wait_ge(s["f_z"], n + 2)
                    spike_steps(n, j, slice(0, TT * D), True)
                else:
                    dve.wait_ge(s["f_z_2"], n + 1)
                    spike_steps(n, j, slice(0, 2 * D), False)
                    dve.wait_ge(s["f_z"], n + 2)
                    spike_steps(n, j, slice(2 * D, TT * D), True)

            def two_batches(g, last_two):
                for j in range(2):
                    fuse_a(g, 2 * g + j, j)
                squares(2 * g)
                if not last_two:
                    prepare(g + 1, 2 * g + 2, 0)
                for j in range(2):
                    count_spikes(2 * g + j, j)
                restart()

            prepare(0, 0, 0)
            dve.wait_ge(s["l_fus"], 16 * 11)
            for m in range(KC):
                ts(bq_m[:, m], row_mask[:], bq_f[:, m:m + 1], None, ALU.mult).then_inc(s["c_scaled"], 1)
            restart()
            with dve.Fori(0, B // 2 - 1) as g:
                two_batches(g, False)
            two_batches(B // 2 - 1, True)


def kernel(**inputs):
    import numpy as np
    import concourse.bacc as _bacc
    from concourse import mybir as _mybir
    from concourse.bass_utils import run_bass_kernel_spmd as _run

    I = {k: np.asarray(v) for k, v in inputs.items()}

    def chunks(w):
        return np.ascontiguousarray(np.swapaxes(w.reshape(*w.shape[:-2], -1, P, w.shape[-1]), -3, -2))

    t = {n: I["L0_txt_" + n] for n in ("Wq", "Wk", "Wv", "Wc", "W1", "b1", "W2", "b2", "g1", "be1", "g2", "be2")}
    a = {n: I["L0_attn_" + n] for n in ("Wq", "bq", "Wk", "bk", "Wv", "bv", "Wo", "bo")}
    pos = np.arange(SEQ, dtype=np.float32)[:, None]
    div = np.exp(np.arange(0, D, 2, dtype=np.float32) * np.float32(-np.log(np.float32(10000.0)) / np.float32(D)))
    pe = np.zeros((SEQ, D), np.float32)
    pe[:, 0::2], pe[:, 1::2] = np.sin(pos * div), np.cos(pos * div)
    wk4 = np.stack([np.concatenate([a["Wk"][HD * j:HD * j + HD]] * 4, 0) for j in range(FKV)], 0).reshape(FKV * P, D).T
    arrays = {
        "o": I["x"].reshape(B, IMG, IMG),
        "tokens": I["x_txt"].T,
        "vf": np.transpose(I["L0_tok_vector_field"], (2, 0, 1))[::-1],
        "nabla_w": I["L0_tok_nabla_w"].reshape(18),
        "div_w": I["L0_tok_div_w"].reshape(18),
        "pe": pe,
        "emb": I["L0_txt_emb"],
        "w_attn": chunks(np.concatenate([t["Wq"], t["Wk"], t["Wv"], t["Wc"]], -1)),
        "w1": chunks(t["W1"]),
        "w2": chunks(t["W2"]),
        "vecs": np.stack([t["g1"], t["be1"], t["b2"], t["g2"], t["be2"]], 1),
        "b1": np.transpose(t["b1"].reshape(LAYERS, MC, P), (0, 2, 1)),
        "wq_f": chunks(a["Wq"].T),
        "wk_f": chunks(wk4).reshape(P, KC, FKV, P),
        "wv_f": chunks(a["Wv"].T),
        "wo_f": chunks(a["Wo"].T),
        "w_fc": chunks(I["L0_ffn_W_fc"].T),
        "w_pr": chunks(I["L0_ffn_W_proj"].T),
        "bq_f": a["bq"].reshape(KC, P).T,
        "bk_f": np.tile(a["bk"].reshape(FKV, HD), (1, 4)).T,
        "bv_f": a["bv"],
        "bo_f": a["bo"],
        "sink": I["L0_attn_sink_bias"].reshape(1),
    }
    nc = _bacc.Bacc("TRN2", target_bir_lowering=False, num_devices=1)
    feeds, d = {}, {}
    for name, arr in arrays.items():
        arr = np.ascontiguousarray(arr)
        feeds["in_" + name] = arr
        d[name] = nc.dram_tensor("in_" + name, arr.shape, _mybir.dt.from_np(arr.dtype), kind="ExternalInput").ap()
    out = nc.dram_tensor("out", (B, TOK, D), F32, kind="ExternalOutput").ap()
    build(nc, d, out)
    r = _run(nc, [feeds], core_ids=[0])
    return r.results[0]["out"]
```
